# Optimizing a Trainium2 kernel written in Bass

```python
import numpy as np
import jax
import jax.numpy as jnp

def _softmax(x, axis=-1):
    return jax.nn.softmax(x, axis=axis)

def _gelu(x):
    return jax.nn.gelu(x, approximate=True)

def _silu(x):
    return jax.nn.silu(x)

def _sigmoid(x):
    return jax.nn.sigmoid(x)

def _layernorm(x, axis=-1, eps=1e-05):
    m = jnp.mean(x, axis=axis, keepdims=True)
    v = jnp.var(x, axis=axis, keepdims=True)
    return (x - m) / jnp.sqrt(v + eps)

def _scatter_add(tgt, idx, src, axis=0):
    return tgt.at[idx].add(src)

def _segment_sum(src, seg, n):
    return jax.ops.segment_sum(src, seg, n)
kernel_name = 'mk_gnn_resnorm_d1_gnn_r8_40db97'

def setup_inputs(seed: int=0):
    np.random.seed(seed)
    _w = jnp.asarray

    def _rec_inputs():
        import jax
        import jax.numpy as jnp
        _gk = jax.random.key(seed)
        x = -0.000202 + 1 * jax.random.normal(jax.random.fold_in(_gk, 1), (6250, 128), jnp.float32)
        src = jax.random.randint(jax.random.fold_in(_gk, 2), (100000,), 0, 6250, jnp.int32)
        dst = jnp.minimum((6250 * jax.random.uniform(jax.random.fold_in(_gk, 3), (100000,)) ** 2.0).astype(jnp.int32), 49999)
        _o = jnp.argsort(dst, stable=True)
        src = src[_o]
        dst = dst[_o]
        edge_type_8 = jax.random.randint(jax.random.fold_in(_gk, 12), (100000,), 0, 8, jnp.int32)
        node_type_8 = jax.random.randint(jax.random.fold_in(_gk, 13), (6250,), 0, 8, jnp.int32)
        return (x, src, dst, edge_type_8, node_type_8)
    x, src, dst, edge_type_8, node_type_8 = _rec_inputs()

    def _L0_gnn_setup():
        import jax, jax.numpy as jnp
        import numpy as np
        N = 6250
        E = 100000
        DIN = 128
        DH = 128
        H = 8
        DK = DH // H
        TN = 8
        TE = 8
        NB = 4

        def _decomp(x, nt, w_comp, w_basis):
            T = w_comp.shape[0]
            W = (w_comp @ w_basis).reshape(T, x.shape[-1], -1)
            h_all = jnp.einsum('ni,tio->tno', x, W)
            return h_all[nt, jnp.arange(x.shape[0])]
        key = jax.random.key(seed)
        ks = jax.random.split(key, 20)
        inp = {}
        inp['node_feat'] = jax.random.normal(ks[0], (N, DIN), jnp.float32)
        inp['node_type'] = jax.random.randint(ks[1], (N,), 0, TN)
        inp['src'] = jax.random.randint(ks[2], (E,), 0, N)
        inp['dst'] = jax.random.randint(ks[3], (E,), 0, N)
        inp['edge_type'] = jax.random.randint(ks[4], (E,), 0, TE)
        s = 0.05
        for i, nm in enumerate(['k', 'q', 'v', 'a']):
            inp['w_comp_' + nm] = jax.random.normal(ks[5 + 2 * i], (TN, NB), jnp.float32) * s
            inp['w_basis_' + nm] = jax.random.normal(ks[6 + 2 * i], (NB, DIN * DH), jnp.float32) * s
        inp['relation_pri'] = jnp.ones((TE, H), jnp.float32)
        inp['relation_att'] = jax.random.uniform(ks[13], (TE, H, DK, DK), jnp.float32, -0.25, 0.25)
        inp['relation_msg'] = jax.random.uniform(ks[14], (TE, H, DK, DK), jnp.float32, -0.25, 0.25)
        inp['loop_weight'] = jax.random.uniform(ks[15], (DIN, DH), jnp.float32, -0.08, 0.08)
        inp['bias'] = jnp.zeros((DH,), jnp.float32)
        return inp
    _L0_gnn_all = _L0_gnn_setup()
    _L0_gnn_in = {k: v for k, v in _L0_gnn_all.items() if k in ('w_comp_k', 'w_basis_k', 'w_comp_q', 'w_basis_q', 'w_comp_v', 'w_basis_v', 'w_comp_a', 'w_basis_a', 'relation_pri', 'relation_att', 'relation_msg', 'loop_weight', 'bias')}
    del _L0_gnn_all
    return {'x': x, 'src': src, 'dst': dst, 'edge_type_8': edge_type_8, 'node_type_8': node_type_8, 'L0_gnn_w_comp_k': _L0_gnn_in['w_comp_k'], 'L0_gnn_w_basis_k': _L0_gnn_in['w_basis_k'], 'L0_gnn_w_comp_q': _L0_gnn_in['w_comp_q'], 'L0_gnn_w_basis_q': _L0_gnn_in['w_basis_q'], 'L0_gnn_w_comp_v': _L0_gnn_in['w_comp_v'], 'L0_gnn_w_basis_v': _L0_gnn_in['w_basis_v'], 'L0_gnn_w_comp_a': _L0_gnn_in['w_comp_a'], 'L0_gnn_w_basis_a': _L0_gnn_in['w_basis_a'], 'L0_gnn_relation_pri': _L0_gnn_in['relation_pri'], 'L0_gnn_relation_att': _L0_gnn_in['relation_att'], 'L0_gnn_relation_msg': _L0_gnn_in['relation_msg'], 'L0_gnn_loop_weight': _L0_gnn_in['loop_weight'], 'L0_gnn_bias': _L0_gnn_in['bias']}

def reference(x, src, dst, edge_type_8, node_type_8, L0_gnn_w_comp_k, L0_gnn_w_basis_k, L0_gnn_w_comp_q, L0_gnn_w_basis_q, L0_gnn_w_comp_v, L0_gnn_w_basis_v, L0_gnn_w_comp_a, L0_gnn_w_basis_a, L0_gnn_relation_pri, L0_gnn_relation_att, L0_gnn_relation_msg, L0_gnn_loop_weight, L0_gnn_bias):
    import jax
    import jax.numpy as jnp

    def _L0_gnn_ref(node_feat, node_type, src, dst, edge_type, w_comp_k, w_basis_k, w_comp_q, w_basis_q, w_comp_v, w_basis_v, w_comp_a, w_basis_a, relation_pri, relation_att, relation_msg, loop_weight, bias):
        import jax, jax.numpy as jnp
        import numpy as np
        N = 6250
        E = 100000
        DIN = 128
        DH = 128
        H = 8
        DK = DH // H
        TN = 8
        TE = 8
        NB = 4

        def _decomp(x, nt, w_comp, w_basis):
            T = w_comp.shape[0]
            W = (w_comp @ w_basis).reshape(T, x.shape[-1], -1)
            h_all = jnp.einsum('ni,tio->tno', x, W)
            return h_all[nt, jnp.arange(x.shape[0])]
        n = node_feat.shape[0]
        scale = (DH / H) ** (-0.5)
        k = _decomp(node_feat, node_type, w_comp_k, w_basis_k).reshape(n, H, DK)
        q = _decomp(node_feat, node_type, w_comp_q, w_basis_q).reshape(n, H, DK)
        v = _decomp(node_feat, node_type, w_comp_v, w_basis_v).reshape(n, H, DK)
        kt = jnp.einsum('nhi,thij->tnhj', k, relation_att)[edge_type, src]
        e = (q[dst] * kt).sum(-1) * relation_pri[edge_type] * scale
        m = jax.ops.segment_max(e, dst, num_segments=n)
        ex = jnp.exp(e - m[dst])
        denom = jax.ops.segment_sum(ex, dst, num_segments=n)
        a = ex / denom[dst]
        vt = jnp.einsum('nhi,thij->tnhj', v, relation_msg)[edge_type, src]
        agg = jax.ops.segment_sum(a[..., None] * vt, dst, num_segments=n)
        agg = agg.reshape(n, DH)
        out = _decomp(agg, node_type, w_comp_a, w_basis_a)
        out = out + node_feat @ loop_weight + bias
        return jax.nn.relu(out)
    x = _layernorm(x + _L0_gnn_ref(x, node_type_8, src, dst, edge_type_8, L0_gnn_w_comp_k, L0_gnn_w_basis_k, L0_gnn_w_comp_q, L0_gnn_w_basis_q, L0_gnn_w_comp_v, L0_gnn_w_basis_v, L0_gnn_w_comp_a, L0_gnn_w_basis_a, L0_gnn_relation_pri, L0_gnn_relation_att, L0_gnn_relation_msg, L0_gnn_loop_weight, L0_gnn_bias), axis=-1)
    return x

_drawn_inputs = setup_inputs


def setup_inputs(seed=0):
    import zlib

    import numpy as np

    out = dict(_drawn_inputs(seed))
    spreads = {'L0_gnn_relation_pri': (1.0, 0.6), 'L0_gnn_bias': (0.0, 2.0)}
    factors = {'L0_gnn_w_comp_k': 8.0,
     'L0_gnn_w_basis_k': 8.0,
     'L0_gnn_w_comp_q': 8.0,
     'L0_gnn_w_basis_q': 8.0,
     'L0_gnn_w_comp_v': 8.0,
     'L0_gnn_w_basis_v': 8.0,
     'L0_gnn_w_comp_a': 8.0,
     'L0_gnn_w_basis_a': 8.0,
     'L0_gnn_relation_att': 8.0,
     'L0_gnn_relation_msg': 8.0,
     'L0_gnn_loop_weight': 3.209}
    for name, (base, spread) in spreads.items():
        noise = np.random.default_rng([zlib.crc32(name.encode()), seed]).standard_normal(out[name].shape)
        drawn = base * np.exp(spread * noise) if base else spread * noise
        out[name] = jnp.asarray(drawn.astype(out[name].dtype))
    for name, factor in factors.items():
        out[name] = (out[name] * factor).astype(out[name].dtype)
    return out
```

```python
import concourse.bass as bass
from concourse import mybir
from contextlib import ExitStack


def graph_transformer_layer(
    nc: bass.Bass,
    x: bass.AP,
    src: bass.AP,
    dst: bass.AP,
    edge_type: bass.AP,
    node_type: bass.AP,
    comp_k: bass.AP,
    basis_k: bass.AP,
    comp_q: bass.AP,
    basis_q: bass.AP,
    comp_v: bass.AP,
    basis_v: bass.AP,
    comp_a: bass.AP,
    basis_a: bass.AP,
    rel_pri: bass.AP,
    rel_att: bass.AP,
    rel_msg: bass.AP,
    loop_w: bass.AP,
    bias: bass.AP,
    out: bass.AP,
):
    f32, i32, bf16 = mybir.dt.float32, mybir.dt.int32, mybir.dt.bfloat16
    ALU, ACT, AX = mybir.AluOpType, mybir.ActivationFunctionType, mybir.AxisListType

    P = 128
    N, D = x.shape
    E = src.shape[0]
    T, H, DK, _ = rel_att.shape
    NB = comp_k.shape[1]
    SCALE = float(D / H) ** -0.5
    BIG = 1e30
    EPS = 1e-5

    BLOCKS = -(-N // P)
    NP = BLOCKS * P
    CB = 7
    CHUNKS = BLOCKS // CB
    CN = CB * P
    HALF = CN // 2
    assert CHUNKS * CB == BLOCKS and CN % 2 == 0 and HALF <= 512

    G = 32
    NBATCH = G // 4
    IL = 16
    IH = G // IL
    TROWS = 112
    TPR = 7
    TILES = TROWS * TPR
    FULL = E // P
    REST = E - FULL * P
    PADT = TILES - FULL
    assert -(-E // P) <= TILES and TILES + BLOCKS - 1 <= P * TPR
    GROUPS = -(-(TILES + BLOCKS - 1) // G)
    IPR = 7
    ITEMS = P * IPR
    assert GROUPS * G <= ITEMS and GROUPS % 2 == 0
    W = D + H

    table = nc.dram_tensor("table", [NP * T, 2 * D], f32, kind="Internal").ap()
    tile_rows = nc.dram_tensor("tile_rows", [TILES, 3 * P], i32, kind="Internal").ap()
    tile_blocks = nc.dram_tensor("tile_blocks", [2, TILES], f32, kind="Internal").ap()
    item_bias = nc.dram_tensor("item_bias", [ITEMS, P], f32, kind="Internal").ap()
    item_keys = nc.dram_tensor("item_keys", [3, ITEMS], f32, kind="Internal").ap()
    item_block = nc.dram_tensor("item_block", [1, ITEMS], i32, kind="Internal").ap()

    ctx = ExitStack()
    with ctx:
        def sb(name, shape, dt=f32):
            return ctx.enter_context(nc.sbuf_tensor(name, shape, dt))

        def pb(name):
            return ctx.enter_context(nc.psum_tensor(name, [P, 512], f32))

        def sem(name):
            return ctx.enter_context(nc.semaphore(name))

        ident = sb("ident", [P, P])
        ones = sb("ones", [1, P])
        lane = sb("lane", [P, P])
        item_no = sb("item_no", [P, IPR])
        type_no = sb("type_no", [96, 1])
        Ba = sb("Ba", [P, NB, D])
        Wl = sb("Wl", [P, D])
        brow = sb("brow", [1, D])
        q_all = sb("q_all", [P, BLOCKS * D])
        agg = sb("agg", [P, BLOCKS * W])
        ca = sb("ca", [P, BLOCKS * NB])
        neg_lane = sb("neg_lane", [P, ITEMS])
        rows_idx = sb("rows_idx", [P, ITEMS], i32)
        iblk = sb("iblk", [1, ITEMS], i32)
        carries = sb("carries", [1, ITEMS])
        carry = sb("carry", [1, 3 * ITEMS], bf16)
        car = carry[:, :].rearrange("p (k i) -> p k i", k=3)
        kv = sb("kv", [P, 2 * G * 2 * D])
        onehot = sb("onehot", [P, 2 * G * P])
        work = sb("work", [P, 5632 + 128])
        seg = sb("seg", [P, 2 * (IH * P + 1)])
        rows8 = sb("rows8", [1, 3 * H * G])
        end_run = sb("end_run", [1, 2 * H * G + 2])
        end_out = sb("end_out", [1, 2 * H * G])
        run_top = sb("run_top", [1, 4 * H])
        cols = sb("cols", [P, 4])
        rise = sb("rise", [P, H])
        idx_now = [sb(f"idx_now{r}", [P, G], i32) for r in range(2)]

        class Space:
            def __init__(self, tensor, size, at=0):
                self.tensor, self.size, self.at = tensor, size, at

            def take(self, n, rows=P):
                self.at += n
                assert self.at <= self.size
                return self.tensor[0:rows, self.at - n:self.at]

        s2 = Space(work, 5760)
        sq = s2.take(2 * 4 * P).rearrange("p (r u e) -> p r u e", r=2, u=4)
        spread = s2.take(2 * 4 * P).rearrange("p (r u e) -> p r u e", r=2, u=4)
        prod = s2.take(2 * 4 * D).rearrange("p (r u d) -> p r u d", r=2, u=4)
        wv = s2.take(2 * 4 * D).rearrange("p (r u d) -> p r u d", r=2, u=4)
        score = s2.take(2 * IH * H * IL).rearrange("p (r c) -> p r c", r=2)
        fwd = s2.take(IH * P)
        bwd = s2.take(IH * P)
        diff = s2.take(IH * P)
        ex = s2.take(IH * P)
        s1 = Space(kv, 2 * G * 2 * D)
        x_in = s1.take(CN)
        xT = s1.take(CN)
        scaled = s1.take(2 * NB * CN).rearrange("p (r b n) -> p r b n", r=2, b=NB)
        kvT = s1.take(2 * CN).rearrange("p (r n) -> p r n", r=2)
        stage = s1.take(2 * T * 2 * D).rearrange("p (r t f) -> p r t f", r=2, t=T)
        w1 = Space(work, 5760)
        ntype = w1.take(CN, 96).bitcast(i32)
        is_type = w1.take(CN // 2, 96).bitcast(bf16)
        comp_w = w1.take(3 * NB * P // 2, 96).bitcast(bf16).rearrange("p (j m) -> p j m", m=P)
        Bq, Bk, Bv = [w1.take(NB * D).rearrange("p (b d) -> p b d", b=NB) for _ in range(3)]
        pri = w1.take(T)
        comp = w1.take(4 * NB, 96)
        comp_r = w1.take(4 * NB, 96)
        comp_p = w1.take(3 * 2 * NB, 96).bitcast(bf16).rearrange("p (k j) -> p k j", k=3)
        comp_s = w1.take(2 * NB, 96).bitcast(bf16)
        h1 = Space(onehot, 2 * G * P)
        att = h1.take(T * D)
        msg = h1.take(T * D)
        tfl = h1.take(2 * TILES)
        tstart = h1.take(TILES)
        tgap = h1.take(TILES)
        tcmp = h1.take(TILES)
        tprod = h1.take(TILES)
        fc = h1.take(IPR * 6).rearrange("p (k c) -> p k c", k=6)
        ic = h1.take(IPR * 3).bitcast(i32).rearrange("p (k c) -> p k c", k=3)
        pad_rows = h1.take(3 * P, PADT).bitcast(i32)
        a0 = Space(agg, BLOCKS * W)
        s0i = a0.take(TPR * 3 * P).bitcast(i32)
        tdst = s0i[0:TROWS, 0:TPR * P].rearrange("p (c e) -> p c e", c=TPR)
        irows = s0i.rearrange("p (c k e) -> p c k e", c=IPR, k=3)
        irow = s0i.rearrange("p (c f) -> p c f", c=IPR)
        lanes = a0.take(IPR * P).rearrange("p (c e) -> p c e", c=IPR)
        krow = a0.take(3 * ITEMS, 1).rearrange("p (k i) -> p k i", k=3)
        etf = tfl[:, 0:IPR * P].rearrange("p (c e) -> p c e", c=IPR)
        srcf = h1.take(IPR * P).rearrange("p (c e) -> p c e", c=IPR)
        biasr = neg_lane[:, :].rearrange("p (c e) -> p c e", c=IPR)
        s3 = Space(kv, 2 * G * 2 * D)
        x3 = s3.take(CN)
        an = s3.take(CN)
        anb = s3.take(NB * CN).rearrange("p (b n) -> p b n", b=NB)
        anT = s3.take(2 * NB * P).rearrange("p (r b n) -> p r b n", r=2, b=NB)
        xT3 = s3.take(CN)
        y = s3.take(CN)
        yo = s3.take(CN)
        rden = s3.take(CB * H)
        stats = s3.take(CB * 6).rearrange("p (c k) -> p c k", c=CB)
        mv = s3.take(CB * 2).rearrange("p (c k) -> p c k", c=CB)
        rstd = s3.take(CB)
        eps = s3.take(1)

        PB = [pb(f"pb{i}") for i in range(8)]

        s_const = sem("s_const")
        s_wload = sem("s_wload")
        s_comp = sem("s_comp")
        s_rel = sem("s_rel")
        s_setup = sem("s_setup")
        s_trow = sem("s_trow")
        s_tdst = sem("s_tdst")
        s_tb = sem("s_tb")
        s_tbr = sem("s_tbr")
        s_irow = sem("s_irow")
        s_iblk = sem("s_iblk")
        s_ikey = sem("s_ikey")
        s_ibias = sem("s_ibias")
        s_rows = sem("s_rows")
        s_turned = sem("s_turned")
        s_untld = sem("s_untld")
        s_xin = sem("s_xin")
        s_nt = sem("s_nt")
        s_xt = sem("s_xt")
        s_xtc = sem("s_xtc")
        s_ot = sem("s_ot")
        s_cb = sem("s_cb")
        s_sc = sem("s_sc")
        s_pj = sem("s_pj")
        s_pjc = sem("s_pjc")
        s_hold = sem("s_hold")
        s_tk = sem("s_tk")
        s_ta = sem("s_ta")
        s_tv = sem("s_tv")
        s_tab = [sem(f"s_tab{r}") for r in range(2)]
        s_idx = [sem(f"s_idx{r}") for r in range(2)]
        s_seg = [sem(f"s_seg{r}") for r in range(2)]
        s_kv = [[sem(f"s_kv{r}_{b}") for b in range(NBATCH)] for r in range(2)]
        s_sq = sem("s_sq")
        s_hot = sem("s_hot")
        s_turn = sem("s_turn")
        s_spr = sem("s_spr")
        s_qe = sem("s_qe")
        s_prod = sem("s_prod")
        s_score = sem("s_score")
        s_t1 = sem("s_t1")
        s_t3 = sem("s_t3")
        s_t5 = sem("s_t5")
        s_t7 = sem("s_t7")
        s_t9 = sem("s_t9")
        s_r8 = sem("s_r8")
        s_mx = sem("s_mx")
        s_ex = sem("s_ex")
        s_rise = sem("s_rise")
        s_resc = sem("s_resc")
        s_wv = sem("s_wv")
        s_part = sem("s_part")
        s_add = sem("s_add")
        s_end = sem("s_end")
        s_x3 = sem("s_x3")
        s_nrm = sem("s_nrm")
        s_v3 = sem("s_v3")
        s_anb = sem("s_anb")
        s_xt3 = sem("s_xt3")
        s_xc3 = sem("s_xc3")
        s_tr3 = sem("s_tr3")
        s_cp3 = sem("s_cp3")
        s_mm3 = sem("s_mm3")
        s_o3 = sem("s_o3")
        s_res = sem("s_res")
        s_stat = sem("s_stat")
        s_aggr = sem("s_aggr")
        s_std = sem("s_std")
        s_fin = sem("s_fin")
        s_out = sem("s_out")

        block = ctx.enter_context(nc.Block())

        RING = [(CB + 1 - r) // 2 for r in range(2)]
        MX_SCAN, MX_CARRY, MX_TOP, MX_DIFF, MX = 2, 12, 17, 20, 20
        PJ = CB + 4
        V3 = V3_RSTD = 3
        POOL_FROM = 4
        mark = {}

        def known(g):
            return isinstance(g, int)

        def after(engine, s, base, per, k):
            if known(base) and base * per + k <= 0:
                return
            engine.wait_ge(s, base * per + k)

        def hold(engine):
            engine.sem_inc(s_hold, 1)

        @block.vector
        def _(dve):
            n = [0]

            def did(ins, name=None):
                n[0] += 1
                ins.then_inc(s_setup, 1)
                if name:
                    mark[name] = n[0]
                dve.wait_ge(s_setup, n[0])

            v = nc.vector
            did(v.memset(pad_rows[:, 0:P], NP - 1))
            did(v.memset(pad_rows[:, P:3 * P], 0), "pad")
            did(v.memset(att, 0.0))
            did(v.memset(msg, 0.0), "rel_zero")
            did(v.memset(ones[:, :], 1.0))
            did(v.memset(ntype, -1))
            did(v.memset(comp, 0.0), "comp_zero")

            dve.wait_ge(s_comp, 16 * 12)
            did(v.tensor_copy(comp_p[:, 0, :], comp))
            did(v.tensor_tensor(comp_r, comp, comp_p[:, 0, :], ALU.subtract))
            did(v.tensor_copy(comp_p[:, 1, :], comp_r))
            did(v.tensor_tensor(comp_r, comp_r, comp_p[:, 1, :], ALU.subtract))
            did(v.tensor_copy(comp_p[:, 2, :], comp_r))
            for k in range(3):
                did(v.tensor_copy(comp_s[32 * k:32 * k + 32, :], comp_p[32 * k:32 * k + 32, k, :]))
            did(v.tensor_copy(comp_w, comp_s[:, 0:3 * NB].unsqueeze(2).broadcast_to([96, 3 * NB, P])),
                "comp")
            dve.wait_ge(s_rel, 16 * 3 * H)
            a3 = att.rearrange("p (t d) -> p t d", t=T)
            did(v.scalar_tensor_tensor(a3, a3, SCALE, pri.unsqueeze(2).broadcast_to([P, T, D]),
                                       ALU.mult, ALU.mult), "att")

            def stage1(ch):
                dve.wait_ge(s_nt, ch * 48 + 48)
                after(dve, s_pj, ch, PJ, 0)
                v.tensor_scalar(is_type, ntype, type_no[:, :], None, ALU.is_equal).then_inc(s_ot, 1)
                for kind in range(3):
                    for h in range(2):
                        for b in range(NB):
                            j = (kind * 2 + h) * NB + b
                            if j == 0:
                                dve.wait_ge(s_xtc, ch * 2 + 2)
                            if j == 2 * 2 * NB:
                                dve.wait_ge(s_pj, ch * PJ + CB)
                            dve.wait_ge(s_cb, ch * 24 + j + 1)
                            v.tensor_tensor(scaled[:, kind % 2, b, h * HALF:(h + 1) * HALF],
                                            xT[:, h * HALF:(h + 1) * HALF],
                                            PB[j % 2][:, 0:HALF], ALU.mult).then_inc(s_sc, 1)
                for blk in range(CB):
                    for u in range(2):
                        dve.wait_ge(s_tk, (ch * CB + blk) * 4 + 2 + u + 1)
                        if u == 0:
                            after(dve, s_tab[blk % 2], ch, 16 * RING[blk % 2], 16 * (blk // 2))
                        v.tensor_copy(stage[:, blk % 2, 4 * u:4 * u + 4, D:2 * D],
                                      PB[4 + 2 + u][:, :].rearrange("p (t d) -> p t d", t=4))\
                            .then_inc(s_tv, 1)

            dve.wait_ge(s_tdst, 16)
            did(v.tensor_copy(ic[0:TROWS, 0, :], tdst[:, :, 0]))
            did(v.tensor_copy(ic[0:TROWS, 1, :], tdst[:, :, P - 1]))
            did(v.tensor_scalar(ic[0:TROWS, 2, :], ic[0:TROWS, 0, :], P.bit_length() - 1, None,
                                ALU.logical_shift_right))
            did(v.tensor_copy(fc[0:TROWS, 0, :], ic[0:TROWS, 2, :]))
            did(v.tensor_scalar(ic[0:TROWS, 2, :], ic[0:TROWS, 1, :], P.bit_length() - 1, None,
                                ALU.logical_shift_right))
            did(v.tensor_copy(fc[0:TROWS, 1, :], ic[0:TROWS, 2, :]))
            did(v.scalar_tensor_tensor(fc[0:TROWS, 1, :], fc[0:TROWS, 1, :], 1.0, fc[0:TROWS, 0, :],
                                       ALU.add, ALU.subtract), "tiles")
            dve.wait_ge(s_const, 7)
            stage1(0)

            dve.wait_ge(s_tbr, 16)
            tb, tn = tfl[:, 0:TILES], tfl[:, TILES:2 * TILES]
            did(v.tensor_tensor_scan(tstart, tn, tn, 0.0, ALU.add, ALU.max))
            did(v.tensor_tensor(tstart, tstart, tn, ALU.subtract))
            did(v.tensor_tensor(tcmp, tb, tstart, ALU.subtract))
            did(v.tensor_copy(tgap[:, 0:1], tcmp[:, 0:1]))
            did(v.tensor_tensor(tgap[:, 1:TILES], tcmp[:, 1:TILES], tcmp[:, 0:TILES - 1], ALU.subtract))
            for k in range(IPR):
                did(v.tensor_scalar(tcmp, tstart, item_no[:, k:k + 1], None, ALU.is_le))
                did(v.tensor_reduce(fc[:, 0, k:k + 1], tcmp, AX.X, ALU.add))
                did(v.tensor_tensor(tprod, tcmp, tgap, ALU.mult))
                did(v.tensor_reduce(fc[:, 1, k:k + 1], tprod, AX.X, ALU.add))
            did(v.tensor_scalar(fc[:, 0, :], fc[:, 0, :], -1.0, None, ALU.add))
            did(v.tensor_copy(ic[:, 0, :], fc[:, 0, :]), "item_tile")
            did(v.tensor_tensor(fc[:, 1, :], fc[:, 1, :], item_no[:, :], ALU.add))
            did(v.tensor_scalar(fc[:, 2, :], fc[:, 1, :], float(BLOCKS - 1), None, ALU.min))
            did(v.tensor_copy(ic[:, 1, :], fc[:, 2, :]), "item_block")
            did(v.tensor_scalar(fc[:, 5, :], fc[:, 1, :], float(P), None, ALU.mult))
            stage1(1)

            dve.wait_ge(s_irow, 16 * IPR)
            did(v.tensor_copy(lanes, irows[:, :, 0, :]))
            did(v.tensor_copy(fc[:, 3, :], lanes[:, :, 0]))
            did(v.tensor_copy(fc[:, 4, :], lanes[:, :, P - 1]), "item_ends")
            did(v.tensor_tensor(biasr[:, :, 1:P], lanes[:, :, 1:P], lanes[:, :, 0:P - 1], ALU.not_equal))
            did(v.memset(biasr[:, :, 0:1], 1.0))
            did(v.tensor_scalar(biasr, biasr, -BIG, None, ALU.mult), "bias")
            for k in range(IPR):
                did(v.tensor_scalar(lanes[:, k, :], lanes[:, k, :], -1.0, fc[:, 5, k:k + 1],
                                    ALU.mult, ALU.add))
            did(v.tensor_copy(srcf, irows[:, :, 1, :]))
            did(v.tensor_copy(etf, irows[:, :, 2, :]))
            did(v.scalar_tensor_tensor(srcf, srcf, float(T), etf, ALU.mult, ALU.add), "rows")
            stage1(2)

            dve.wait_ge(s_ibias, 16)
            for a, (o, first_bank) in enumerate(((neg_lane, 4), (rows_idx, 6))):
                turned = o[:, :].rearrange("e (p c) -> e c p", c=IPR)
                for k in range(IPR):
                    if k % 4 == 0:
                        dve.wait_ge(s_turned, a * IPR + min(k + 4, IPR))
                    v.tensor_copy(turned[:, k, :],
                                  PB[first_bank + k // 4][:, (k % 4) * P:(k % 4 + 1) * P]).then_inc(s_untld, 1)
            dve.wait_ge(s_ikey, 48)
            last = ITEMS - 1
            it_, if_, il_ = krow[:, 0, :], krow[:, 1, :], krow[:, 2, :]
            did(v.memset(carries[:, 0:1], 0.0))
            did(v.tensor_tensor(carries[:, 1:], it_[:, 1:], it_[:, 0:last], ALU.subtract))
            did(v.tensor_scalar(carries[:, 1:], carries[:, 1:], 1.0, None, ALU.is_equal))
            did(v.tensor_tensor(it_[:, 1:], if_[:, 1:], il_[:, 0:last], ALU.is_equal))
            did(v.tensor_tensor(carries[:, 1:], carries[:, 1:], it_[:, 1:], ALU.mult))
            did(v.tensor_tensor(it_, if_, il_, ALU.is_equal))
            did(v.tensor_tensor(if_, it_, carries[:, :], ALU.mult))
            did(v.memset(il_[:, last:], 0.0))
            did(v.tensor_tensor(il_[:, 0:last], it_[:, 0:last], carries[:, 1:], ALU.mult))
            for k, a in enumerate((if_, carries[:, :], il_)):
                did(v.tensor_scalar(car[:, k, :], a, -1.0, BIG, ALU.add, ALU.mult))
            did(v.memset(end_run[:, :], 0.0))
            did(v.memset(run_top[:, :], 0.0))
            for r in range(2):
                did(v.memset(seg[:, (r + 1) * (IH * P + 1) - 1:(r + 1) * (IH * P + 1)], -BIG))
            dve.wait_ge(s_turned, 2 * IPR)
            did(v.memset(agg[:, :], 0.0), "stage0")
            with dve.Fori(3, CHUNKS) as ch:
                stage1(ch)

            def scores(g, par, use, b):
                r = b % 2
                dve.wait_ge(s_kv[par][b], use * 64 + 64)
                dve.wait_ge(s_qe, g * NBATCH + b + 1)
                rows = kv[:, (par * G + b * 4) * 2 * D:(par * G + b * 4 + 4) * 2 * D]\
                    .rearrange("p (u f) -> p u f", u=4)
                v.tensor_tensor(prod[:, r, :, :], rows[:, :, 0:D],
                                PB[2 + r][:, :].rearrange("p (u d) -> p u d", u=4), ALU.mult)\
                    .then_inc(s_prod, 1)
                dve.wait_ge(s_prod, g * NBATCH + b + 1)
                o = b // (IL // 4) * H * IL
                sc = score[:, par, o:o + H * IL].rearrange("p (h l) -> p h l", h=H)
                l0 = b % (IL // 4) * 4
                v.tensor_reduce(sc[:, :, l0:l0 + 4].rearrange("p h l -> p l h"),
                                prod[:, r, :, :].rearrange("p u (h k) -> p u h k", h=H),
                                AX.X, ALU.add).then_inc(s_score, 1)

            eT, topT = PB[6][:, 0:IH * P], PB[6][:, IH * P:2 * IH * P]
            L = IH * P
            HG = H * G
            r8 = rows8[:, :].rearrange("p (k h i) -> p k h i", k=3, h=H)
            ahead = end_run[:, 1:HG + 1]
            behind = end_run[:, HG + 1:2 * HG + 1]
            by_row = lambda a: a.rearrange("p (h i l) -> p i h l", h=H, i=IH)
            eout = end_out[:, :].rearrange("p (k i h l) -> p k i h l", k=2, i=IH, h=H)

            def maxima(g, par, use):
                k = [0]

                def step(ins):
                    k[0] += 1
                    ins.then_inc(s_mx, 1)
                    dve.wait_ge(s_mx, g * MX + k[0])

                sg = seg[:, par * (L + 1):(par + 1) * (L + 1)]
                run_in = run_top[:, (1 - par) * H:(2 - par) * H]
                run_out = run_top[:, par * H:(par + 1) * H]
                delta = run_top[:, 2 * H:3 * H]

                def scans():
                    dve.wait_ge(s_seg[par], (use + 1) * 16 * H)
                    dve.wait_ge(s_t1, g + 1)
                    step(v.tensor_tensor_scan(fwd, sg[:, 0:L], eT, 0.0, ALU.add, ALU.max))
                    step(v.tensor_tensor_scan(bwd[:, ::-1], sg[:, L:0:-1], eT[:, ::-1], 0.0,
                                              ALU.add, ALU.max))
                    assert k[0] == MX_SCAN

                def carried():
                    dve.wait_ge(s_t3, g + 1)
                    dve.wait_ge(s_r8, g * 3 + 3)
                    rl = PB[7][0:1, 0:HG].rearrange("p (h i) -> p h i", h=H)
                    step(v.tensor_tensor(delta, run_in, r8[:, 0, :, 0], ALU.add))
                    step(v.tensor_tensor(rl[:, :, 0], rl[:, :, 0], delta, ALU.max))
                    step(v.memset(r8[:, 0, :, 0:1], -BIG))
                    step(v.memset(r8[:, 2, :, G - 1:G], -BIG))
                    step(v.tensor_tensor_scan(ahead, rows8[:, 0:HG], PB[7][0:1, 0:HG], 0.0,
                                              ALU.add, ALU.max))
                    step(v.tensor_tensor_scan(behind[:, ::-1], rows8[:, 3 * HG - 1:2 * HG - 1:-1],
                                              PB[7][0:1, 2 * HG - 1:HG - 1:-1], 0.0, ALU.add, ALU.max))
                    into = rows8[:, HG:2 * HG]
                    step(v.tensor_tensor(eout[:, 0, :, :, :], by_row(end_run[:, 0:HG]), by_row(into), ALU.add))
                    step(v.tensor_tensor(eout[:, 0, 0, :, 0], run_in, r8[:, 1, :, 0], ALU.add))
                    step(v.tensor_tensor(eout[:, 1, :, :, :], by_row(end_run[:, HG + 2:2 * HG + 2]),
                                         by_row(rows8[:, HG + 1:2 * HG + 1]), ALU.add))
                    step(v.memset(eout[:, 1, IH - 1, :, IL - 1:IL], -BIG))
                    assert k[0] == MX_CARRY

                def tops():
                    dve.wait_ge(s_t5, g + 1)
                    step(v.tensor_copy(cols[:, :], PB[7][:, 0:4]))
                    e3 = eT.rearrange("p (i e) -> p i e", i=IH)
                    step(v.tensor_tensor(e3[:, :, 0], e3[:, :, 0], cols[:, 0:IH], ALU.max))
                    step(v.tensor_tensor(e3[:, :, P - 1], e3[:, :, P - 1], cols[:, IH:2 * IH], ALU.max))
                    step(v.tensor_tensor_scan(fwd, sg[:, 0:L], eT, 0.0, ALU.add, ALU.max))
                    step(v.tensor_tensor_scan(bwd[:, ::-1], sg[:, L:0:-1], fwd[:, ::-1], 0.0,
                                              ALU.add, ALU.max))
                    assert k[0] == MX_TOP

                def differences():
                    dve.wait_ge(s_t7, g + 1)
                    step(v.tensor_tensor(delta, run_in, topT[0:1, 0:H * IL:IL], ALU.subtract))
                    step(v.tensor_scalar(delta, delta, carries[0:1, bass.ds(g * G, 1)], None, ALU.mult))
                    v.tensor_copy(run_out, ahead[:, G - 1::G])
                    step(v.tensor_tensor(diff, score[:, par, :], topT, ALU.subtract))
                    assert k[0] == MX_DIFF == MX

                return scans, carried, tops, differences

            def weigh(g, par, b):
                if b == 0:
                    dve.wait_ge(s_ex, g + 1)
                after(dve, s_part, g, 2 * NBATCH, 2 * (b - 2) + 2)
                rows = kv[:, (par * G + b * 4) * 2 * D:(par * G + b * 4 + 4) * 2 * D]\
                    .rearrange("p (u f) -> p u f", u=4)[:, :, D:2 * D]
                o = b // (IL // 4) * H * IL
                l0 = b % (IL // 4) * 4
                e = ex[:, o:o + H * IL].rearrange("p (h l) -> p l h", h=H)[:, l0:l0 + 4, :]
                v.tensor_tensor(wv[:, b % 2, :, :].rearrange("p u (h k) -> p u h k", h=H),
                                rows.rearrange("p u (h k) -> p u h k", h=H),
                                e.unsqueeze(3).broadcast_to([P, 4, H, DK]), ALU.mult).then_inc(s_wv, 1)

            def blocks_of(g, i, count):
                return nc.values_load_multi_w_load_instructions(
                    iblk[0:1, bass.ds(g * G + i, count)], engines=(dve.engine,), min_val=0,
                    max_val=BLOCKS - 1)[1]

            def rescale(g):
                (blk,) = blocks_of(g, 0, 1)
                a = agg[:, bass.ds(blk * W, W)]
                dve.wait_ge(s_rise, g + 1)
                after(dve, s_add, g, G, 0)
                v.tensor_tensor(a[:, 0:D].rearrange("p (h k) -> p h k", h=H),
                                a[:, 0:D].rearrange("p (h k) -> p h k", h=H),
                                rise[:, :].unsqueeze(2).broadcast_to([P, H, DK]), ALU.mult)\
                    .then_inc(s_resc, 1)
                v.tensor_tensor(a[:, D:W], a[:, D:W], rise[:, :], ALU.mult).then_inc(s_resc, 1)
                dve.wait_ge(s_resc, g * 2 + 2)

            def add(g, b):
                blks = blocks_of(g, b * 4, 4)
                for u in range(4):
                    i = b * 4 + u
                    if u % 2 == 0:
                        dve.wait_ge(s_part, g * 2 * NBATCH + i // 2 + 1)
                    after(dve, s_add, g, G, i)
                    a = agg[:, bass.ds(blks[u] * W, W)]
                    v.tensor_tensor(a, a, PB[4 + i // 2 % 2][:, (u % 2) * 256:(u % 2) * 256 + W],
                                    ALU.add).then_inc(s_add, 1)

            def half_group(g, par, use, prev):
                parts = maxima(g - 1, 1 - par, use if par else use - 1) if prev else ()
                for s in range(NBATCH):
                    if prev and s < 4:
                        parts[s]()
                    if prev and s >= 4:
                        b = 2 * (s - 4)
                        weigh(g - 1, 1 - par, b)
                        if s == 4:
                            rescale(g - 1)
                        else:
                            add(g - 1, b - 1)
                        weigh(g - 1, 1 - par, b + 1)
                        add(g - 1, b)
                    scores(g, par, use, s)
                if prev:
                    add(g - 1, NBATCH - 1)

            half_group(0, 0, 0, False)
            half_group(1, 1, 0, True)
            with dve.Fori(1, GROUPS // 2) as it:
                half_group(it * 2, 0, it, True)
                half_group(it * 2 + 1, 1, it, True)
            for part_ in maxima(GROUPS - 1, 1, GROUPS // 2 - 1):
                part_()
            weigh(GROUPS - 1, 1, 0)
            rescale(GROUPS - 1)
            for b in range(1, NBATCH):
                weigh(GROUPS - 1, 1, b)
                add(GROUPS - 1, b - 1)
            add(GROUPS - 1, NBATCH - 1)

            dve.wait_ge(s_add, GROUPS * G)
            v.memset(eps, EPS).then_inc(s_end, 1)
            def stage3(ch):
                k3 = [0]

                def step3(ins):
                    k3[0] += 1
                    ins.then_inc(s_v3, 1)
                    dve.wait_ge(s_v3, ch * V3 + k3[0])

                ag = agg[:, bass.ds(ch * (CB * W), CB * W)].rearrange("p (c w) -> p c w", c=CB)
                rd = rden.rearrange("p (c h) -> p c h", c=CB)
                step3(v.tensor_scalar(rd, ag[:, :, D:W], 1e-30, None, ALU.max))
                step3(v.reciprocal(rden, rden))
                after(dve, s_anb, ch, NB, 0)
                after(dve, s_tr3, ch, CB, 0)
                v.tensor_tensor(an.rearrange("p (c h k) -> p c h k", c=CB, h=H),
                                ag[:, :, 0:D].rearrange("p c (h k) -> p c h k", h=H),
                                rd.unsqueeze(3).broadcast_to([P, CB, H, DK]), ALU.mult).then_inc(s_nrm, 1)
                dve.wait_ge(s_nrm, ch + 1)
                for b in range(2):
                    cab = ca[:, bass.ds(ch * (CB * NB), CB * NB)]\
                        .rearrange("p (c b) -> p c b", b=NB)[:, :, b:b + 1]
                    v.tensor_tensor(anb[:, b, :].rearrange("p (c d) -> p c d", c=CB),
                                    an.rearrange("p (c d) -> p c d", c=CB),
                                    cab.broadcast_to([P, CB, D]), ALU.mult).then_inc(s_anb, 1)
                after(dve, s_fin, ch, CB, 0)
                for h, (c0, c1) in enumerate(((0, 4), (4, CB))):
                    dve.wait_ge(s_o3, ch * 2 + h + 1)
                    v.scalar_tensor_tensor(y[:, c0 * D:c1 * D], PB[4 + h][:, 0:(c1 - c0) * D], 0.0,
                                           x3[:, c0 * D:c1 * D], ALU.max, ALU.add).then_inc(s_res, 1)
                dve.wait_ge(s_res, ch * 2 + 2)
                for c in range(CB):
                    v.bn_stats(stats[:, c, :], y[:, c * D:(c + 1) * D]).then_inc(s_stat, 1)
                dve.wait_ge(s_stat, ch * CB + CB)
                hold(dve)
                for c in range(CB):
                    v.bn_aggr(mv[:, c, :], stats[:, c, :]).then_inc(s_aggr, 1)
                dve.wait_ge(s_std, ch + 1)
                step3(v.reciprocal(rstd, rstd))
                assert k3[0] == V3_RSTD == V3
                after(dve, s_out, ch, 16, 0)
                for c in range(POOL_FROM):
                    v.tensor_scalar(yo[:, c * D:(c + 1) * D], y[:, c * D:(c + 1) * D], mv[:, c, 0:1],
                                    rstd[:, c:c + 1], ALU.subtract, ALU.mult).then_inc(s_fin, 1)

            stage3(0)
            with dve.Fori(1, CHUNKS) as ch:
                stage3(ch)

        @block.sync
        def _(sp):
            for b, w in ((Bq, basis_q), (Bk, basis_k), (Bv, basis_v), (Ba, basis_a)):
                sp.dma_start(b[:, :, :], w.rearrange("b (i o) -> i b o", o=D)).then_inc(s_wload, 16)
            sp.dma_start(Wl[:, :], loop_w).then_inc(s_wload, 16)
            sp.dma_start(brow[:, :], bias.rearrange("(a d) -> a d", a=1)).then_inc(s_wload, 16)

            def tile_load(k, a):
                sp.dma_start(tile_rows[0:FULL, k * P:(k + 1) * P],
                             a[0:FULL * P].rearrange("(t e) -> t e", e=P)).then_inc(s_trow, 16)
                sp.dma_start(tile_rows[FULL:FULL + 1, k * P:k * P + REST],
                             a[FULL * P:].rearrange("(t e) -> t e", t=1)).then_inc(s_trow, 16)

            tile_load(0, dst)
            tile_load(1, src)
            tile_load(2, edge_type)
            sp.wait_ge(s_setup, mark["pad"])
            p3 = pad_rows.rearrange("p (k e) -> p k e", k=3)
            r3 = tile_rows.rearrange("t (k e) -> t k e", k=3)
            sp.dma_start(r3[FULL:FULL + 1, :, REST:P], p3[0:1, :, REST:P]).then_inc(s_trow, 16)
            sp.dma_start(r3[FULL + 1:TILES, :, :], p3[1:PADT, :, :]).then_inc(s_trow, 16)

            def chunk_in(ch):
                after(sp, s_xt, ch, CB, 0)
                hold(sp)
                full = CB if not (known(ch) and ch == CHUNKS - 1) else CB - 1
                xi = x_in.rearrange("p (c d) -> p c d", c=CB)
                sp.dma_start(xi[:, 0:full, :],
                             x[bass.ds(ch * CN, full * P), :].rearrange("(c p) d -> p c d", p=P))\
                    .then_inc(s_xin, 16)
                rest = N - (CHUNKS - 1) * CN - (CB - 1) * P
                if full < CB:
                    sp.dma_start(xi[0:rest, full, :], x[N - rest:N, :]).then_inc(s_xin, 16)
                after(sp, s_ot, ch, 1, 0)
                hold(sp)
                many = CN if full == CB else N - (CHUNKS - 1) * CN
                for k in range(3):
                    sp.dma_start(ntype[32 * k:32 * k + T, 0:many],
                                 node_type[bass.ds(ch * CN, many)].rearrange("(a n) -> a n", a=1)
                                 .broadcast_to([T, many])).then_inc(s_nt, 16)

            def chunk_out(ch):
                for blk in range(CB):
                    sp.wait_ge(s_ta, (ch * CB + blk) * 2 + 2)
                    sp.wait_ge(s_tv, (ch * CB + blk) * 2 + 2)
                    hold(sp)
                    sp.dma_start(table[bass.ds((ch * CB + blk) * P * T, P * T), :]
                                 .rearrange("(p t) f -> p t f", t=T),
                                 stage[:, blk % 2, :, :]).then_inc(s_tab[blk % 2], 16)

            sp.wait_ge(s_setup, mark["comp_zero"])
            chunk_in(0)
            sp.wait_ge(s_trow, 16 * 8)
            sp.dma_start(tdst, tile_rows.rearrange("(p c) f -> p c f", c=TPR)[:, :, 0:P])\
                .then_inc(s_tdst, 16)
            sp.wait_ge(s_setup, mark["tiles"])
            sp.dma_start(tile_blocks.rearrange("k (p c) -> p k c", c=TPR), fc[0:TROWS, 0:2, :])\
                .then_inc(s_tb, 16)
            sp.wait_ge(s_tb, 16)
            sp.dma_start(tfl, tile_blocks.rearrange("(a k) t -> a (k t)", a=1).broadcast_to([P, 2 * TILES]))\
                .then_inc(s_tbr, 16)
            chunk_in(1)
            chunk_out(0)
            sp.wait_ge(s_setup, mark["item_block"])
            sp.dma_start(item_block.rearrange("a (p c) -> (a p) c", c=IPR), ic[:, 1, :]).then_inc(s_iblk, 16)
            sp.wait_ge(s_iblk, 16)
            sp.dma_start(iblk[:, :], item_block).then_inc(s_iblk, 16)
            chunk_in(2)
            chunk_out(1)
            sp.wait_ge(s_setup, mark["item_ends"])
            kd = item_keys.rearrange("k (p c) -> p k c", c=IPR)
            sp.dma_start(kd[:, 0:1, :], fc[:, 0:1, :]).then_inc(s_ikey, 16)
            sp.dma_start(kd[:, 1:3, :], fc[:, 3:5, :]).then_inc(s_ikey, 16)
            sp.wait_ge(s_ikey, 32)
            sp.dma_start(krow, item_keys.rearrange("(a k) i -> a k i", a=1)).then_inc(s_ikey, 16)
            sp.wait_ge(s_setup, mark["bias"])
            sp.dma_start(item_bias.rearrange("(p c) e -> p c e", c=IPR), biasr).then_inc(s_ibias, 16)
            chunk_in(3)
            chunk_out(2)
            with sp.Fori(3, CHUNKS - 2) as ch:
                chunk_in(ch + 1)
                chunk_out(ch)
            chunk_in(CHUNKS - 1)
            chunk_out(CHUNKS - 2)
            chunk_out(CHUNKS - 1)

            sp.wait_ge(s_setup, mark["stage0"])

            def group(g, par):
                after(sp, s_score, g - 2, NBATCH, NBATCH)
                hold(sp)
                sp.dma_start(idx_now[par][:, :], rows_idx[:, bass.ds(g * G, G)]).then_inc(s_idx[par], 16)
                after(sp, s_mx, g - 2, MX, MX_TOP)
                hold(sp)
                seg3 = seg[:, par * (IH * P + 1):par * (IH * P + 1) + IH * P]\
                    .rearrange("p (i e) -> p i e", i=IH)
                rows = item_bias[bass.ds(g * G, G), :].rearrange("(i l) e -> l i e", l=IL)
                for h in range(H):
                    sp.dma_start(seg3[h * IL:(h + 1) * IL, :, :], rows).then_inc(s_seg[par], 16)

            group(0, 0)
            group(1, 1)
            with sp.Fori(1, GROUPS // 2) as it:
                group(it * 2, 0)
                group(it * 2 + 1, 1)

            sp.wait_ge(s_end, 1)
            whole = BLOCKS - 1
            rest = N - whole * P

            def load(ch):
                after(sp, s_res, ch, 2, 0)
                hold(sp)
                last = known(ch) and ch == CHUNKS - 1
                n = CB - 1 if last else CB
                xc = x3.rearrange("p (c d) -> p c d", c=CB)
                sp.dma_start(xc[:, 0:n, :],
                             x[bass.ds(ch * CN, n * P), :].rearrange("(c p) d -> p c d", p=P)).then_inc(s_x3, 16)
                if last:
                    sp.dma_start(xc[0:rest, n, :], x[whole * P:N, :]).then_inc(s_x3, 16)

            def store(ch):
                sp.wait_ge(s_fin, ch * CB + CB)
                hold(sp)
                last = known(ch) and ch == CHUNKS - 1
                n = CB - 1 if last else CB
                oc = yo.rearrange("p (c d) -> p c d", c=CB)
                sp.dma_start(out[bass.ds(ch * CN, n * P), :].rearrange("(c p) d -> p c d", p=P),
                             oc[:, 0:n, :]).then_inc(s_out, 16)
                if last:
                    sp.dma_start(out[whole * P:N, :], oc[0:rest, n, :]).then_inc(s_out, 16)

            load(0)
            load(1)
            store(0)
            with sp.Fori(1, CHUNKS - 2) as ch:
                load(ch + 1)
                store(ch)
            load(CHUNKS - 1)
            store(CHUNKS - 2)
            store(CHUNKS - 1)
            sp.wait_ge(s_out, 16 * (CHUNKS + 1))

        @block.gpsimd
        def _(pool):
            g_ = nc.gpsimd
            g_.memset(ident[:, :], 0.0).then_inc(s_const, 1)
            g_.iota(lane[:, :], [[1, P]], base=0, channel_multiplier=0,
                    allow_small_or_imprecise_dtypes=True).then_inc(s_const, 1)
            g_.iota(item_no[:, :], [[1, IPR]], base=0, channel_multiplier=IPR,
                    allow_small_or_imprecise_dtypes=True).then_inc(s_const, 1)
            for k in range(3):
                pool.wait_ge(s_const, 3 + k)
                g_.iota(type_no[32 * k:32 * k + 32, :], [[0, 1]], base=0, channel_multiplier=1,
                        allow_small_or_imprecise_dtypes=True).then_inc(s_const, 1)
            pool.wait_ge(s_const, 6)
            g_.affine_select(out=ident[:, :], in_=ident[:, :], compare_op=ALU.not_equal, fill=1.0,
                             base=0, pattern=[[-1, P]], channel_multiplier=1).then_inc(s_const, 1)

            pool.wait_ge(s_setup, mark["item_tile"])
            for k in range(IPR):
                pool.indirect_dma_start(
                    out=irow[:, k, :], out_offset=None, in_=tile_rows,
                    in_offset=bass.IndirectOffsetOnAxis(ap=ic[:, 0, k:k + 1], axis=0)).then_inc(s_irow, 16)

            for r in range(2):
                pool.wait_ge(s_tab[r], 16 * RING[r] * CHUNKS)

            def gather(g, par, use):
                after(pool, s_idx[par], use, 16, 16)
                for b in range(NBATCH):
                    after(pool, s_wv, g - 2, NBATCH, b + 1)
                    hold(pool)
                    for u in range(4):
                        i = b * 4 + u
                        o = (par * G + i) * 2 * D
                        pool.indirect_dma_start(
                            out=kv[:, o:o + 2 * D], out_offset=None, in_=table,
                            in_offset=bass.IndirectOffsetOnAxis(ap=idx_now[par][:, i:i + 1], axis=0))\
                            .then_inc(s_kv[par][b], 16)

            gather(0, 0, 0)
            gather(1, 1, 0)
            with pool.Fori(1, GROUPS // 2) as it:
                gather(it * 2, 0, it)
                gather(it * 2 + 1, 1, it)

            def coefficients(ch):
                pool.wait_ge(s_nrm, ch + 1)
                after(pool, s_tr3, ch, CB, 0)
                hold(pool)
                for b in range(2, NB):
                    cab = ca[:, bass.ds(ch * (CB * NB), CB * NB)].rearrange("p (c b) -> p c b", b=NB)[:, :, b:b + 1]
                    g_.tensor_tensor(anb[:, b, :].rearrange("p (c d) -> p c d", c=CB),
                                     an.rearrange("p (c d) -> p c d", c=CB),
                                     cab.broadcast_to([P, CB, D]), ALU.mult).then_inc(s_anb, 1)

            def normalise(ch):
                pool.wait_ge(s_v3, ch * V3 + V3_RSTD)
                after(pool, s_out, ch, 16, 0)
                hold(pool)
                for c in range(POOL_FROM, CB):
                    g_.tensor_scalar(yo[:, c * D:(c + 1) * D], y[:, c * D:(c + 1) * D], mv[:, c, 0:1],
                                     rstd[:, c:c + 1], ALU.subtract, ALU.mult).then_inc(s_fin, 1)

            coefficients(0)
            normalise(0)
            with pool.Fori(1, CHUNKS) as ch:
                coefficients(ch)
                normalise(ch)

        @block.scalar
        def _(act):
            a_ = nc.scalar
            act.wait_ge(s_setup, mark["comp_zero"])
            for k in range(3):
                for j, w in enumerate((comp_q, comp_k, comp_v, comp_a)):
                    act.dma_start(comp[32 * k:32 * k + T, j * NB:(j + 1) * NB], w).then_inc(s_comp, 16)
            for h in range(H):
                r = slice(h * DK, (h + 1) * DK)
                for m, w in ((att, rel_att), (msg, rel_msg)):
                    act.dma_start(m.rearrange("p (t d) -> p t d", t=T)[r, :, r],
                                  w[:, h, :, :].rearrange("t i j -> i t j")).then_inc(s_rel, 16)
                with nc.allow_non_contiguous_dma(reason="64 priorities"):
                    act.dma_start(pri[r, :], rel_pri[:, h:h + 1].rearrange("t a -> a t").broadcast_to([DK, T]))\
                        .then_inc(s_rel, 16)

            def stage1(ch):
                for u, (c0, c1) in enumerate(((0, 4), (4, CB))):
                    act.wait_ge(s_xt, ch * CB + c1)
                    if u == 0:
                        after(act, s_sc, ch, 24, 0)
                    a_.activation(xT[:, c0 * P:c1 * P], PB[2 + u][:, 0:(c1 - c0) * P], ACT.Copy)\
                        .then_inc(s_xtc, 1)
                for o in range(PJ):
                    act.wait_ge(s_pj, ch * PJ + o + 1)
                    bank = PB[2 + o % 2]
                    if o < CB:
                        hold(act)
                        a_.activation(q_all[:, bass.ds((ch * CB + o) * D, D)], bank[:, 0:D], ACT.Copy)
                        a_.activation(ca[:, bass.ds((ch * CB + o) * NB, NB)], bank[:, D:D + NB], ACT.Copy)\
                            .then_inc(s_pjc, 1)
                    else:
                        kind, h = (o - CB) // 2, (o - CB) % 2
                        if o == CB:
                            after(act, s_tk, ch, CB * 4, 0)
                        a_.activation(kvT[:, kind, h * HALF:(h + 1) * HALF], bank[:, 0:HALF], ACT.Copy)\
                            .then_inc(s_pjc, 1)
                for blk in range(CB):
                    for u in range(2):
                        act.wait_ge(s_tk, (ch * CB + blk) * 4 + u + 1)
                        if u == 0:
                            after(act, s_tab[blk % 2], ch, 16 * RING[blk % 2], 16 * (blk // 2))
                        a_.activation(stage[:, blk % 2, 4 * u:4 * u + 4, 0:D],
                                      PB[4 + u][:, :].rearrange("p (t d) -> p t d", t=4), ACT.Copy)\
                            .then_inc(s_ta, 1)

            for ch in range(3):
                stage1(ch)
            with act.Fori(3, CHUNKS) as ch:
                stage1(ch)

            act.wait_ge(s_tk, CHUNKS * CB * 4)
            act.wait_ge(s_setup, mark["stage0"])

            def one_hot(g, par, b):
                r = b % 2
                after(act, s_hot, g, NBATCH, b - 1)
                hold(act)
                for u in range(4):
                    a_.activation(sq[:, r, u, :], lane[:, :], ACT.Square,
                                  bias=neg_lane[:, bass.ds(g * G + b * 4 + u, 1)]).then_inc(s_sq, 1)
                act.wait_ge(s_sq, g * G + b * 4 + 4)
                after(act, s_part, g - 2, 2 * NBATCH, 2 * b + 2)
                o = (par * G + b * 4) * P
                a_.activation(onehot[:, o:o + 4 * P], sq[:, r, :, :].rearrange("p u e -> p (u e)"), ACT.Relu,
                              bias=1.0, scale=-1.0).then_inc(s_hot, 1)

            def evacuate(g, b):
                act.wait_ge(s_turn, g * NBATCH + b + 1)
                after(act, s_qe, g, NBATCH, b - 1)
                a_.activation(spread[:, b % 2, :, :].rearrange("p u e -> p (u e)"), PB[b % 2][:, :], ACT.Copy)\
                    .then_inc(s_spr, 1)

            def carry_terms(g):
                after(act, s_mx, g - 1, MX, MX_CARRY)
                hold(act)
                for k in range(3):
                    a_.activation(rows8[:, k * H * G:(k + 1) * H * G].rearrange("p (h i) -> p h i", h=H),
                                  car[:, k, bass.ds(g * G, G)].unsqueeze(1).broadcast_to([1, H, G]),
                                  ACT.Copy).then_inc(s_r8, 1)

            def exponentials(g):
                act.wait_ge(s_mx, g * MX + MX)
                after(act, s_part, g, 2 * NBATCH, 0)
                a_.activation(ex, diff, ACT.Exp).then_inc(s_ex, 1)
                act.wait_ge(s_t9, g + 1)
                after(act, s_resc, g, 2, 0)
                a_.activation(rise[:, :], PB[7][:, 8:8 + H], ACT.Exp).then_inc(s_rise, 1)

            def half_group(g, par, prev):
                one_hot(g, par, 0)
                if prev:
                    carry_terms(g - 1)
                for s in range(NBATCH):
                    if s + 1 < NBATCH:
                        one_hot(g, par, s + 1)
                    if prev and s == 4:
                        exponentials(g - 1)
                    evacuate(g, s)

            half_group(0, 0, False)
            half_group(1, 1, True)
            with act.Fori(1, GROUPS // 2) as it:
                half_group(it * 2, 0, True)
                half_group(it * 2 + 1, 1, True)
            carry_terms(GROUPS - 1)
            exponentials(GROUPS - 1)

            def stage3(ch):
                for u, (c0, c1) in enumerate(((0, 4), (4, CB))):
                    act.wait_ge(s_xt3, ch * CB + c1)
                    after(act, s_mm3, ch, CB, 0)
                    a_.activation(xT3[:, c0 * P:c1 * P], PB[2 + u][:, 0:(c1 - c0) * P], ACT.Copy)\
                        .then_inc(s_xc3, 1)
                for c in range(CB):
                    act.wait_ge(s_tr3, ch * CB + c + 1)
                    after(act, s_mm3, ch, CB, max(c - 1, 0))
                    a_.activation(anT[:, c % 2, :, :].rearrange("p b n -> p (b n)"), PB[c % 2][:, :], ACT.Copy)\
                        .then_inc(s_cp3, 1)
                act.wait_ge(s_aggr, ch * CB + CB)
                a_.activation(rstd, mv[:, :, 1], ACT.Sqrt, bias=eps[:, 0:1]).then_inc(s_std, 1)

            stage3(0)
            with act.Fori(1, CHUNKS) as ch:
                stage3(ch)

        @block.tensor
        def _(pe):
            t_ = nc.tensor

            def stage1(ch):
                last = known(ch) and ch == CHUNKS - 1
                pe.wait_ge(s_xin, (ch + (2 if last else 1)) * 16)
                after(pe, s_pjc, ch, PJ, 0)
                for c in range(CB):
                    t_.transpose(PB[2 + c // 4][:, c % 4 * P:(c % 4 + 1) * P], x_in[:, c * D:(c + 1) * D],
                                 ident[:, :]).then_inc(s_xt, 1)
                pe.wait_ge(s_ot, ch + 1)

                def coefficients(kind):
                    for h in range(2):
                        for b in range(NB):
                            j = (kind * 2 + h) * NB + b
                            after(pe, s_sc, ch, 24, j - 1)
                            t_.matmul(PB[j % 2][:, 0:HALF], comp_w[:, kind * NB + b, :],
                                      is_type[:, h * HALF:(h + 1) * HALF], start=True, stop=True)\
                                .then_inc(s_cb, 1)

                def place(o):
                    if o < 2:
                        pe.wait_ge(s_xtc, ch * 2 + 2)
                    else:
                        pe.wait_ge(s_pjc, ch * PJ + o - 1)
                    return PB[2 + o % 2]

                def project(kind, B):
                    for h in range(2):
                        pe.wait_ge(s_sc, ch * 24 + (kind * 2 + h + 1) * NB)
                        o = CB + (kind - 1) * 2 + h
                        bank = place(o)
                        for b in range(NB):
                            mm = t_.matmul(bank[:, 0:HALF], B[:, b, :],
                                           scaled[:, kind % 2, b, h * HALF:(h + 1) * HALF],
                                           start=(b == 0), stop=(b == NB - 1))
                        mm.then_inc(s_pj, 1)

                coefficients(0)
                coefficients(1)
                for o in range(CB):
                    pe.wait_ge(s_sc, ch * 24 + (2 if (o + 1) * P > HALF else 1) * NB)
                    bank = place(o)
                    for b in range(NB):
                        t_.matmul(bank[:, 0:D], scaled[:, 0, b, o * P:(o + 1) * P], Bq[:, b, :],
                                  start=(b == 0), stop=(b == NB - 1))
                    t_.matmul(bank[:, D:D + NB], is_type[:, o * P:(o + 1) * P], comp_s[:, 3 * NB:4 * NB],
                              start=True, stop=True).then_inc(s_pj, 1)
                coefficients(2)
                project(1, Bk)
                project(2, Bv)
                for blk in range(CB):
                    for j in range(4):
                        kind, h = j // 2, j % 2
                        if blk == 0 and h == 0:
                            pe.wait_ge(s_pjc, ch * PJ + CB + 2 * kind + 2)
                        after(pe, (s_ta, s_tv)[kind], ch, 2 * CB, 2 * blk + h - 1)
                        t_.matmul(PB[4 + j][:, :], kvT[:, kind, blk * P:(blk + 1) * P],
                                  (att, msg)[kind][:, h * 512:(h + 1) * 512], start=True, stop=True)\
                            .then_inc(s_tk, 1)

            pe.wait_ge(s_const, 7)
            pe.wait_ge(s_wload, 16 * 6)
            pe.wait_ge(s_setup, mark["att"])
            for ch in range(3):
                stage1(ch)
            pe.wait_ge(s_setup, mark["rows"])
            pe.wait_ge(s_ta, 3 * 2 * CB)
            pe.wait_ge(s_tv, 3 * 2 * CB)
            for a, (rows, bank) in enumerate(((lanes, 4), (srcf, 6))):
                for k in range(IPR):
                    t_.transpose(PB[bank + k // 4][:, k % 4 * P:(k % 4 + 1) * P], rows[:, k, :],
                                 ident[:, :]).then_inc(s_turned, 1)
            pe.wait_ge(s_untld, 2 * IPR)
            with pe.Fori(3, CHUNKS - 1) as ch:
                stage1(ch)
            stage1(CHUNKS - 1)

            pe.wait_ge(s_pjc, CHUNKS * PJ)
            pe.wait_ge(s_ta, CHUNKS * 2 * CB)
            pe.wait_ge(s_tv, CHUNKS * 2 * CB)
            pe.wait_ge(s_iblk, 32)
            L = IH * P
            HG = H * G

            def turn(g, par, b):
                pe.wait_ge(s_hot, g * NBATCH + b + 1)
                after(pe, s_spr, g, NBATCH, b - 1)
                for u in range(4):
                    o = (par * G + b * 4 + u) * P
                    mm = t_.transpose(PB[b % 2][:, u * P:(u + 1) * P], onehot[:, o:o + P], ident[:, :])
                mm.then_inc(s_turn, 1)

            def queries(g, b):
                blks = nc.values_load_multi_w_load_instructions(
                    iblk[0:1, bass.ds(g * G + b * 4, 4)], engines=(pe.engine,), min_val=0,
                    max_val=BLOCKS - 1)[1]
                pe.wait_ge(s_spr, g * NBATCH + b + 1)
                after(pe, s_prod, g, NBATCH, b - 1)
                for u in range(4):
                    mm = t_.matmul(PB[2 + b % 2][:, u * D:(u + 1) * D], spread[:, b % 2, u, :],
                                   q_all[:, bass.ds(blks[u] * D, D)], start=True, stop=True)
                mm.then_inc(s_qe, 1)

            def turn_scores(g, par):
                pe.wait_ge(s_score, g * NBATCH + NBATCH)
                for i in range(IH):
                    mm = t_.transpose(PB[6][:, i * P:(i + 1) * P], score[:, par, i * P:(i + 1) * P], ident[:, :])
                mm.then_inc(s_t1, 1)

            def turn_ends(g):
                pe.wait_ge(s_mx, g * MX + MX_SCAN)
                after(pe, s_rise, g, 1, 0)
                for k, (scan, e) in enumerate(((fwd, P - 1), (bwd, 0))):
                    for i in range(IH):
                        dest = PB[7][0:1, k * HG:(k + 1) * HG].rearrange("p (h j) -> p h j", h=H)
                        mm = t_.transpose(dest[:, :, i * IL:(i + 1) * IL], scan[:, i * P + e:i * P + e + 1],
                                          ident[:, :])
                mm.then_inc(s_t3, 1)

            def turn_carried(g):
                pe.wait_ge(s_mx, g * MX + MX_CARRY)
                for k in range(2):
                    for i in range(IH):
                        o = (k * IH + i) * P
                        mm = t_.matmul(PB[7][:, k * IH + i:k * IH + i + 1], end_out[:, o:o + P],
                                       ones[0:1, 0:1], start=True, stop=True)
                mm.then_inc(s_t5, 1)

            def turn_tops(g):
                pe.wait_ge(s_mx, g * MX + MX_TOP)
                for i in range(IH):
                    mm = t_.transpose(PB[6][:, L + i * P:L + (i + 1) * P], bwd[:, i * P:(i + 1) * P],
                                      ident[:, :])
                mm.then_inc(s_t7, 1)

            def place_rise(g, par):
                pe.wait_ge(s_mx, g * MX + MX_DIFF)
                t_.matmul(PB[7][:, 8:8 + H], onehot[0:1, par * G * P:par * G * P + P],
                          run_top[:, 2 * H:3 * H], start=True, stop=True).then_inc(s_t9, 1)

            def sums(g, par, b):
                for h in range(2):
                    pe.wait_ge(s_wv, g * NBATCH + b + 1)
                    after(pe, s_add, g, G, 4 * b + 2 * h - 2)
                    for u in range(2):
                        i = b * 4 + h * 2 + u
                        bank = PB[4 + h]
                        o = (par * G + i) * P
                        t_.matmul(bank[:, u * 256:u * 256 + D], onehot[:, o:o + P],
                                  wv[:, b % 2, h * 2 + u, :], start=True, stop=True)
                        e = i // IL * H * IL + i % IL
                        mm = t_.matmul(bank[:, u * 256 + D:u * 256 + W], onehot[:, o:o + P],
                                       ex[:, e:e + (H - 1) * IL + 1:IL], start=True, stop=True)
                    mm.then_inc(s_part, 1)

            def half_group(g, par, prev):
                if prev:
                    turn_scores(g - 1, 1 - par)
                turn(g, par, 0)
                for s in range(NBATCH):
                    if prev and s == 1:
                        turn_ends(g - 1)
                    if prev and s == 2:
                        turn_carried(g - 1)
                    if prev and s == 3:
                        turn_tops(g - 1)
                    if prev and s >= 4:
                        if s == 4:
                            place_rise(g - 1, 1 - par)
                        sums(g - 1, 1 - par, 2 * (s - 4))
                        sums(g - 1, 1 - par, 2 * (s - 4) + 1)
                    if s + 1 < NBATCH:
                        turn(g, par, s + 1)
                    queries(g, s)

            half_group(0, 0, False)
            half_group(1, 1, True)
            with pe.Fori(1, GROUPS // 2) as it:
                half_group(it * 2, 0, True)
                half_group(it * 2 + 1, 1, True)
            g = GROUPS - 1
            turn_scores(g, 1)
            turn_ends(g)
            turn_carried(g)
            turn_tops(g)
            place_rise(g, 1)
            for b in range(NBATCH):
                sums(g, 1, b)

            def stage3(ch):
                last = known(ch) and ch == CHUNKS - 1
                pe.wait_ge(s_x3, (ch + (2 if last else 1)) * 16)
                after(pe, s_xc3, ch, 2, 0)
                for c in range(CB):
                    t_.transpose(PB[2 + c // 4][:, c % 4 * P:(c % 4 + 1) * P], x3[:, c * D:(c + 1) * D],
                                 ident[:, :]).then_inc(s_xt3, 1)

                def turn3(c):
                    if c == 0:
                        pe.wait_ge(s_anb, ch * NB + NB)
                    after(pe, s_cp3, ch, CB, max(c - 1, 0))
                    for b in range(NB):
                        mm = t_.transpose(PB[c % 2][:, b * P:(b + 1) * P], anb[:, b, c * D:(c + 1) * D],
                                          ident[:, :])
                    mm.then_inc(s_tr3, 1)

                turn3(0)
                for c in range(CB):
                    if c + 1 < CB:
                        turn3(c + 1)
                    if c % 4 == 0:
                        pe.wait_ge(s_xc3, ch * 2 + c // 4 + 1)
                        after(pe, s_res, ch, 2, 0)
                    pe.wait_ge(s_cp3, ch * CB + c + 1)
                    o = PB[4 + c // 4][:, c % 4 * D:(c % 4 + 1) * D]
                    for b in range(NB):
                        mm = t_.matmul(o, anT[:, c % 2, b, :], Ba[:, b, :], start=(b == 0), stop=False)
                    mm.then_inc(s_mm3, 1)
                    t_.matmul(o, xT3[:, c * P:(c + 1) * P], Wl[:, :], start=False, stop=False)
                    mm = t_.matmul(o, ones[0:1, :], brow[:, :], start=False, stop=True)
                    if c in (3, CB - 1):
                        mm.then_inc(s_o3, 1)

            stage3(0)
            with pe.Fori(1, CHUNKS - 1) as ch:
                stage3(ch)
            stage3(CHUNKS - 1)



_INS = ["x", "src", "dst", "edge_type_8", "node_type_8",
        "L0_gnn_w_comp_k", "L0_gnn_w_basis_k", "L0_gnn_w_comp_q", "L0_gnn_w_basis_q",
        "L0_gnn_w_comp_v", "L0_gnn_w_basis_v", "L0_gnn_w_comp_a", "L0_gnn_w_basis_a",
        "L0_gnn_relation_pri", "L0_gnn_relation_att", "L0_gnn_relation_msg",
        "L0_gnn_loop_weight", "L0_gnn_bias"]


def kernel(**inputs):
    import numpy as _np
    import concourse.bacc as _bacc
    from concourse import mybir as _mybir
    from concourse.bass_utils import run_bass_kernel_spmd as _run

    nc = _bacc.Bacc("TRN2", target_bir_lowering=False, num_devices=1)
    arrays, args = {}, []
    for name in _INS:
        a = _np.ascontiguousarray(inputs[name])
        arrays[f"in_{name}_dram"] = a
        args.append(nc.dram_tensor(f"in_{name}_dram", a.shape, _mybir.dt.from_np(a.dtype), kind="ExternalInput").ap())
    n, d = arrays["in_x_dram"].shape
    args.append(nc.dram_tensor("out_0_dram", (n, d), _mybir.dt.float32, kind="ExternalOutput").ap())
    graph_transformer_layer(nc, *args)
    r = _run(nc, [arrays], core_ids=[0])
    return r.results[0]["out_0_dram"]
```

```python
import concourse.bass as bass
from concourse import mybir
from contextlib import ExitStack


def graph_transformer_layer(
    nc: bass.Bass,
    x: bass.AP,
    src: bass.AP,
    dst: bass.AP,
    edge_type: bass.AP,
    node_type: bass.AP,
    comp_k: bass.AP,
    basis_k: bass.AP,
    comp_q: bass.AP,
    basis_q: bass.AP,
    comp_v: bass.AP,
    basis_v: bass.AP,
    comp_a: bass.AP,
    basis_a: bass.AP,
    rel_pri: bass.AP,
    rel_att: bass.AP,
    rel_msg: bass.AP,
    loop_w: bass.AP,
    bias: bass.AP,
    out: bass.AP,
):
    f32, i32, bf16 = mybir.dt.float32, mybir.dt.int32, mybir.dt.bfloat16
    ALU, ACT, AX = mybir.AluOpType, mybir.ActivationFunctionType, mybir.AxisListType

    P = 128
    N, D = x.shape
    E = src.shape[0]
    T, H, DK, _ = rel_att.shape
    NB = comp_k.shape[1]
    SCALE = float(D / H) ** -0.5
    BIG = 1e30
    EPS = 1e-5

    BLOCKS = -(-N // P)
    NP = BLOCKS * P
    CB = 7
    CHUNKS = BLOCKS // CB
    CN = CB * P
    HALF = CN // 2
    assert CHUNKS * CB == BLOCKS and CN % 2 == 0 and HALF <= 512

    G = 32
    NBATCH = G // 4
    IL = 16
    IH = G // IL
    TROWS = 112
    TPR = 7
    TILES = TROWS * TPR
    FULL = E // P
    REST = E - FULL * P
    PADT = TILES - FULL
    assert -(-E // P) <= TILES and TILES + BLOCKS - 1 <= P * TPR
    GROUPS = -(-(TILES + BLOCKS - 1) // G)
    IPR = 7
    ITEMS = P * IPR
    assert GROUPS * G <= ITEMS and GROUPS % 2 == 0
    W = D + H
    WR = 4
    WORK = 4 * P + 2 * 4 * P + 2 * 4 * D + WR * 4 * W + 2 * IH * P + 3 * IH * P

    table = nc.dram_tensor("table", [NP * T, 2 * D], f32, kind="Internal").ap()
    tile_rows = nc.dram_tensor("tile_rows", [TILES, 3 * P], i32, kind="Internal").ap()
    tile_blocks = nc.dram_tensor("tile_blocks", [2, TILES], f32, kind="Internal").ap()
    item_bias = nc.dram_tensor("item_bias", [ITEMS, P], f32, kind="Internal").ap()
    item_keys = nc.dram_tensor("item_keys", [3, ITEMS], f32, kind="Internal").ap()
    item_block = nc.dram_tensor("item_block", [1, ITEMS], i32, kind="Internal").ap()

    ctx = ExitStack()
    with ctx:
        def sb(name, shape, dt=f32):
            return ctx.enter_context(nc.sbuf_tensor(name, shape, dt))

        def pb(name):
            return ctx.enter_context(nc.psum_tensor(name, [P, 512], f32))

        def sem(name):
            return ctx.enter_context(nc.semaphore(name))

        ident = sb("ident", [P, P])
        ones = sb("ones", [1, P])
        lane = sb("lane", [P, P])
        item_no = sb("item_no", [P, IPR])
        type_no = sb("type_no", [96, 1])
        Ba = sb("Ba", [P, NB, D])
        Wl = sb("Wl", [P, D])
        brow = sb("brow", [1, D])
        q_all = sb("q_all", [P, BLOCKS * D])
        agg = sb("agg", [P, BLOCKS * W])
        ca = sb("ca", [P, BLOCKS * NB])
        neg_lane = sb("neg_lane", [P, ITEMS])
        rows_idx = sb("rows_idx", [P, ITEMS], i32)
        iblk = sb("iblk", [1, ITEMS], i32)
        carries = sb("carries", [1, ITEMS])
        carry = sb("carry", [1, 3 * ITEMS], bf16)
        car = carry[:, :].rearrange("p (k i) -> p k i", k=3)
        kv = sb("kv", [P, 2 * G * 2 * D])
        onehot = sb("onehot", [P, 2 * G * P])
        work = sb("work", [P, WORK])
        seg = sb("seg", [P, 2 * (IH * P + 1)])
        rows8 = sb("rows8", [1, 3 * H * G])
        end_run = sb("end_run", [1, 2 * H * G + 2])
        end_out = sb("end_out", [1, 2 * H * G])
        run_top = sb("run_top", [1, 4 * H])
        cols = sb("cols", [P, 4])
        rise = sb("rise", [P, H])
        idx_now = [sb(f"idx_now{r}", [P, G], i32) for r in range(2)]

        class Space:
            def __init__(self, tensor, size, at=0):
                self.tensor, self.size, self.at = tensor, size, at

            def take(self, n, rows=P):
                self.at += n
                assert self.at <= self.size
                return self.tensor[0:rows, self.at - n:self.at]

        s2 = Space(work, WORK)
        sq = s2.take(4 * P).rearrange("p (u e) -> p u e", u=4)
        spread = s2.take(2 * 4 * P).rearrange("p (r u e) -> p r u e", r=2, u=4)
        prod = s2.take(2 * 4 * D).rearrange("p (r u d) -> p r u d", r=2, u=4)
        wv = s2.take(WR * 4 * W).rearrange("p (r u w) -> p r u w", r=WR, u=4)
        score = s2.take(2 * IH * H * IL).rearrange("p (r c) -> p r c", r=2)
        fwd = s2.take(IH * P)
        bwd = s2.take(IH * P)
        diff = s2.take(IH * P)
        s1 = Space(kv, 2 * G * 2 * D)
        x_in = s1.take(CN)
        xT = s1.take(CN)
        scaled = s1.take(2 * NB * CN).rearrange("p (r b n) -> p r b n", r=2, b=NB)
        kvT = s1.take(2 * CN).rearrange("p (r n) -> p r n", r=2)
        stage = s1.take(2 * T * 2 * D).rearrange("p (r t f) -> p r t f", r=2, t=T)
        w1 = Space(work, WORK)
        ntype = w1.take(CN, 96).bitcast(i32)
        is_type = w1.take(CN // 2, 96).bitcast(bf16)
        comp_w = w1.take(3 * NB * P // 2, 96).bitcast(bf16).rearrange("p (j m) -> p j m", m=P)
        Bq, Bk, Bv = [w1.take(NB * D).rearrange("p (b d) -> p b d", b=NB) for _ in range(3)]
        pri = w1.take(T)
        comp = w1.take(4 * NB, 96)
        comp_r = w1.take(4 * NB, 96)
        comp_p = w1.take(3 * 2 * NB, 96).bitcast(bf16).rearrange("p (k j) -> p k j", k=3)
        comp_s = w1.take(2 * NB, 96).bitcast(bf16)
        h1 = Space(onehot, 2 * G * P)
        att = h1.take(T * D)
        msg = h1.take(T * D)
        tfl = h1.take(2 * TILES)
        tstart = h1.take(TILES)
        tgap = h1.take(TILES)
        tcmp = h1.take(TILES)
        tprod = h1.take(TILES)
        fc = h1.take(IPR * 6).rearrange("p (k c) -> p k c", k=6)
        ic = h1.take(IPR * 3).bitcast(i32).rearrange("p (k c) -> p k c", k=3)
        pad_rows = h1.take(3 * P, PADT).bitcast(i32)
        a0 = Space(agg, BLOCKS * W)
        s0i = a0.take(TPR * 3 * P).bitcast(i32)
        tdst = s0i[0:TROWS, 0:TPR * P].rearrange("p (c e) -> p c e", c=TPR)
        irows = s0i.rearrange("p (c k e) -> p c k e", c=IPR, k=3)
        irow = s0i.rearrange("p (c f) -> p c f", c=IPR)
        lanes = a0.take(IPR * P).rearrange("p (c e) -> p c e", c=IPR)
        krow = a0.take(3 * ITEMS, 1).rearrange("p (k i) -> p k i", k=3)
        etf = tfl[:, 0:IPR * P].rearrange("p (c e) -> p c e", c=IPR)
        srcf = h1.take(IPR * P).rearrange("p (c e) -> p c e", c=IPR)
        biasr = neg_lane[:, :].rearrange("p (c e) -> p c e", c=IPR)
        s3 = Space(kv, 2 * G * 2 * D)
        x3 = s3.take(CN)
        an = s3.take(CN)
        anb = s3.take(NB * CN).rearrange("p (b n) -> p b n", b=NB)
        anT = s3.take(2 * NB * P).rearrange("p (r b n) -> p r b n", r=2, b=NB)
        xT3 = s3.take(CN)
        y = s3.take(CN)
        yo = s3.take(CN)
        rden = s3.take(CB * H)
        stats = s3.take(CB * 6).rearrange("p (c k) -> p c k", c=CB)
        mv = s3.take(CB * 2).rearrange("p (c k) -> p c k", c=CB)
        rstd = s3.take(CB)
        eps = s3.take(1)

        PB = [pb(f"pb{i}") for i in range(8)]

        s_const = sem("s_const")
        s_wload = sem("s_wload")
        s_comp = sem("s_comp")
        s_rel = sem("s_rel")
        s_setup = sem("s_setup")
        s_trow = sem("s_trow")
        s_tdst = sem("s_tdst")
        s_tb = sem("s_tb")
        s_tbr = sem("s_tbr")
        s_irow = sem("s_irow")
        s_iblk = sem("s_iblk")
        s_ikey = sem("s_ikey")
        s_ibias = sem("s_ibias")
        s_rows = sem("s_rows")
        s_turned = sem("s_turned")
        s_untld = sem("s_untld")
        s_xin = sem("s_xin")
        s_nt = sem("s_nt")
        s_xt = sem("s_xt")
        s_xtc = sem("s_xtc")
        s_ot = sem("s_ot")
        s_cb = sem("s_cb")
        s_sc = sem("s_sc")
        s_pj = sem("s_pj")
        s_pjc = sem("s_pjc")
        s_hold = sem("s_hold")
        s_tk = sem("s_tk")
        s_ta = sem("s_ta")
        s_tv = sem("s_tv")
        s_tab = [sem(f"s_tab{r}") for r in range(2)]
        s_idx = [sem(f"s_idx{r}") for r in range(2)]
        s_seg = [sem(f"s_seg{r}") for r in range(2)]
        s_kv = [[sem(f"s_kv{r}_{b}") for b in range(NBATCH)] for r in range(2)]
        s_sq = sem("s_sq")
        s_hot = sem("s_hot")
        s_turn = sem("s_turn")
        s_spr = sem("s_spr")
        s_qe = sem("s_qe")
        s_prod = sem("s_prod")
        s_score = sem("s_score")
        s_t1 = sem("s_t1")
        s_t3 = sem("s_t3")
        s_t5 = sem("s_t5")
        s_t7 = sem("s_t7")
        s_t9 = sem("s_t9")
        s_r8 = sem("s_r8")
        s_mx = sem("s_mx")
        s_ex = sem("s_ex")
        s_rise = sem("s_rise")
        s_resc = sem("s_resc")
        s_wv = sem("s_wv")
        s_part = sem("s_part")
        s_add = sem("s_add")
        s_end = sem("s_end")
        s_x3 = sem("s_x3")
        s_nrm = sem("s_nrm")
        s_v3 = sem("s_v3")
        s_anb = sem("s_anb")
        s_xt3 = sem("s_xt3")
        s_xc3 = sem("s_xc3")
        s_tr3 = sem("s_tr3")
        s_cp3 = sem("s_cp3")
        s_mm3 = sem("s_mm3")
        s_o3 = sem("s_o3")
        s_res = sem("s_res")
        s_stat = sem("s_stat")
        s_aggr = sem("s_aggr")
        s_std = sem("s_std")
        s_fin = sem("s_fin")
        s_out = sem("s_out")

        block = ctx.enter_context(nc.Block())

        RING = [(CB + 1 - r) // 2 for r in range(2)]
        MX_SCAN, MX_CARRY, MX_TOP, MX_DIFF, MX = 2, 12, 17, 20, 20
        PJ = CB + 4
        V3 = V3_RSTD = 3
        POOL_FROM = 4
        SUMS = [[], [], [0, 1], [2], [3, 4], [5], [6], [7]]
        mark = {}

        def known(g):
            return isinstance(g, int)

        def after(engine, s, base, per, k):
            if known(base) and base * per + k <= 0:
                return
            engine.wait_ge(s, base * per + k)

        def hold(engine):
            engine.sem_inc(s_hold, 1)

        @block.vector
        def _(dve):
            n = [0]

            def did(ins, name=None):
                n[0] += 1
                ins.then_inc(s_setup, 1)
                if name:
                    mark[name] = n[0]
                dve.wait_ge(s_setup, n[0])

            v = nc.vector
            did(v.memset(pad_rows[:, 0:P], NP - 1))
            did(v.memset(pad_rows[:, P:3 * P], 0), "pad")
            did(v.memset(att, 0.0))
            did(v.memset(msg, 0.0), "rel_zero")
            did(v.memset(ones[:, :], 1.0))
            did(v.memset(ntype, -1))
            did(v.memset(comp, 0.0), "comp_zero")

            dve.wait_ge(s_comp, 16 * 12)
            did(v.tensor_copy(comp_p[:, 0, :], comp))
            did(v.tensor_tensor(comp_r, comp, comp_p[:, 0, :], ALU.subtract))
            did(v.tensor_copy(comp_p[:, 1, :], comp_r))
            did(v.tensor_tensor(comp_r, comp_r, comp_p[:, 1, :], ALU.subtract))
            did(v.tensor_copy(comp_p[:, 2, :], comp_r))
            for k in range(3):
                did(v.tensor_copy(comp_s[32 * k:32 * k + 32, :], comp_p[32 * k:32 * k + 32, k, :]))
            did(v.tensor_copy(comp_w, comp_s[:, 0:3 * NB].unsqueeze(2).broadcast_to([96, 3 * NB, P])),
                "comp")
            dve.wait_ge(s_rel, 16 * 3 * H)
            a3 = att.rearrange("p (t d) -> p t d", t=T)
            did(v.scalar_tensor_tensor(a3, a3, SCALE, pri.unsqueeze(2).broadcast_to([P, T, D]),
                                       ALU.mult, ALU.mult), "att")

            def stage1(ch):
                dve.wait_ge(s_nt, ch * 48 + 48)
                after(dve, s_pj, ch, PJ, 0)
                v.tensor_scalar(is_type, ntype, type_no[:, :], None, ALU.is_equal).then_inc(s_ot, 1)
                for kind in range(3):
                    for h in range(2):
                        for b in range(NB):
                            j = (kind * 2 + h) * NB + b
                            if j == 0:
                                dve.wait_ge(s_xtc, ch * 2 + 2)
                            if j == 2 * 2 * NB:
                                dve.wait_ge(s_pj, ch * PJ + CB)
                            dve.wait_ge(s_cb, ch * 24 + j + 1)
                            v.tensor_tensor(scaled[:, kind % 2, b, h * HALF:(h + 1) * HALF],
                                            xT[:, h * HALF:(h + 1) * HALF],
                                            PB[j % 2][:, 0:HALF], ALU.mult).then_inc(s_sc, 1)
                for blk in range(CB):
                    for u in range(2):
                        dve.wait_ge(s_tk, (ch * CB + blk) * 4 + 2 + u + 1)
                        if u == 0:
                            after(dve, s_tab[blk % 2], ch, 16 * RING[blk % 2], 16 * (blk // 2))
                        v.tensor_copy(stage[:, blk % 2, 4 * u:4 * u + 4, D:2 * D],
                                      PB[4 + 2 + u][:, :].rearrange("p (t d) -> p t d", t=4))\
                            .then_inc(s_tv, 1)

            dve.wait_ge(s_tdst, 16)
            did(v.tensor_copy(ic[0:TROWS, 0, :], tdst[:, :, 0]))
            did(v.tensor_copy(ic[0:TROWS, 1, :], tdst[:, :, P - 1]))
            did(v.tensor_scalar(ic[0:TROWS, 2, :], ic[0:TROWS, 0, :], P.bit_length() - 1, None,
                                ALU.logical_shift_right))
            did(v.tensor_copy(fc[0:TROWS, 0, :], ic[0:TROWS, 2, :]))
            did(v.tensor_scalar(ic[0:TROWS, 2, :], ic[0:TROWS, 1, :], P.bit_length() - 1, None,
                                ALU.logical_shift_right))
            did(v.tensor_copy(fc[0:TROWS, 1, :], ic[0:TROWS, 2, :]))
            did(v.scalar_tensor_tensor(fc[0:TROWS, 1, :], fc[0:TROWS, 1, :], 1.0, fc[0:TROWS, 0, :],
                                       ALU.add, ALU.subtract), "tiles")
            dve.wait_ge(s_const, 7)
            stage1(0)

            dve.wait_ge(s_tbr, 16)
            tb, tn = tfl[:, 0:TILES], tfl[:, TILES:2 * TILES]
            did(v.tensor_tensor_scan(tstart, tn, tn, 0.0, ALU.add, ALU.max))
            did(v.tensor_tensor(tstart, tstart, tn, ALU.subtract))
            did(v.tensor_tensor(tcmp, tb, tstart, ALU.subtract))
            did(v.tensor_copy(tgap[:, 0:1], tcmp[:, 0:1]))
            did(v.tensor_tensor(tgap[:, 1:TILES], tcmp[:, 1:TILES], tcmp[:, 0:TILES - 1], ALU.subtract))
            for k in range(IPR):
                did(v.tensor_scalar(tcmp, tstart, item_no[:, k:k + 1], None, ALU.is_le))
                did(v.tensor_reduce(fc[:, 0, k:k + 1], tcmp, AX.X, ALU.add))
                did(v.tensor_tensor(tprod, tcmp, tgap, ALU.mult))
                did(v.tensor_reduce(fc[:, 1, k:k + 1], tprod, AX.X, ALU.add))
            did(v.tensor_scalar(fc[:, 0, :], fc[:, 0, :], -1.0, None, ALU.add))
            did(v.tensor_copy(ic[:, 0, :], fc[:, 0, :]), "item_tile")
            did(v.tensor_tensor(fc[:, 1, :], fc[:, 1, :], item_no[:, :], ALU.add))
            did(v.tensor_scalar(fc[:, 2, :], fc[:, 1, :], float(BLOCKS - 1), None, ALU.min))
            did(v.tensor_copy(ic[:, 1, :], fc[:, 2, :]), "item_block")
            did(v.tensor_scalar(fc[:, 5, :], fc[:, 1, :], float(P), None, ALU.mult))
            stage1(1)

            dve.wait_ge(s_irow, 16 * IPR)
            did(v.tensor_copy(lanes, irows[:, :, 0, :]))
            did(v.tensor_copy(fc[:, 3, :], lanes[:, :, 0]))
            did(v.tensor_copy(fc[:, 4, :], lanes[:, :, P - 1]), "item_ends")
            did(v.tensor_tensor(biasr[:, :, 1:P], lanes[:, :, 1:P], lanes[:, :, 0:P - 1], ALU.not_equal))
            did(v.memset(biasr[:, :, 0:1], 1.0))
            did(v.tensor_scalar(biasr, biasr, -BIG, None, ALU.mult), "bias")
            for k in range(IPR):
                did(v.tensor_scalar(lanes[:, k, :], lanes[:, k, :], -1.0, fc[:, 5, k:k + 1],
                                    ALU.mult, ALU.add))
            did(v.tensor_copy(srcf, irows[:, :, 1, :]))
            did(v.tensor_copy(etf, irows[:, :, 2, :]))
            did(v.scalar_tensor_tensor(srcf, srcf, float(T), etf, ALU.mult, ALU.add), "rows")
            stage1(2)

            dve.wait_ge(s_ibias, 16)
            for a, (o, first_bank) in enumerate(((neg_lane, 4), (rows_idx, 6))):
                turned = o[:, :].rearrange("e (p c) -> e c p", c=IPR)
                for k in range(IPR):
                    if k % 4 == 0:
                        dve.wait_ge(s_turned, a * IPR + min(k + 4, IPR))
                    v.tensor_copy(turned[:, k, :],
                                  PB[first_bank + k // 4][:, (k % 4) * P:(k % 4 + 1) * P]).then_inc(s_untld, 1)
            dve.wait_ge(s_ikey, 48)
            last = ITEMS - 1
            it_, if_, il_ = krow[:, 0, :], krow[:, 1, :], krow[:, 2, :]
            did(v.memset(carries[:, 0:1], 0.0))
            did(v.tensor_tensor(carries[:, 1:], it_[:, 1:], it_[:, 0:last], ALU.subtract))
            did(v.tensor_scalar(carries[:, 1:], carries[:, 1:], 1.0, None, ALU.is_equal))
            did(v.tensor_tensor(it_[:, 1:], if_[:, 1:], il_[:, 0:last], ALU.is_equal))
            did(v.tensor_tensor(carries[:, 1:], carries[:, 1:], it_[:, 1:], ALU.mult))
            did(v.tensor_tensor(it_, if_, il_, ALU.is_equal))
            did(v.tensor_tensor(if_, it_, carries[:, :], ALU.mult))
            did(v.memset(il_[:, last:], 0.0))
            did(v.tensor_tensor(il_[:, 0:last], it_[:, 0:last], carries[:, 1:], ALU.mult))
            for k, a in enumerate((if_, carries[:, :], il_)):
                did(v.tensor_scalar(car[:, k, :], a, -1.0, BIG, ALU.add, ALU.mult))
            did(v.memset(end_run[:, :], 0.0))
            did(v.memset(run_top[:, :], 0.0))
            for r in range(2):
                did(v.memset(seg[:, (r + 1) * (IH * P + 1) - 1:(r + 1) * (IH * P + 1)], -BIG))
            dve.wait_ge(s_turned, 2 * IPR)
            did(v.memset(agg[:, :], 0.0), "stage0")
            with dve.Fori(3, CHUNKS) as ch:
                stage1(ch)

            def rows_of(par, b):
                o = (par * G + b * 4) * 2 * D
                return kv[:, o:o + 4 * 2 * D].rearrange("p (u f) -> p u f", u=4)

            def products(g, par, use, b):
                dve.wait_ge(s_kv[par][b], use * 64 + 64)
                dve.wait_ge(s_qe, g * NBATCH + b + 1)
                v.tensor_tensor(prod[:, b % 2, :, :], rows_of(par, b)[:, :, 0:D],
                                PB[2 + b % 2][:, :].rearrange("p (u d) -> p u d", u=4), ALU.mult)\
                    .then_inc(s_prod, 1)

            def scores(g, par, b):
                dve.wait_ge(s_prod, g * NBATCH + b + 1)
                o = b // (IL // 4) * H * IL
                sc = score[:, par, o:o + H * IL].rearrange("p (h l) -> p h l", h=H)
                l0 = b % (IL // 4) * 4
                v.tensor_reduce(sc[:, :, l0:l0 + 4].rearrange("p h l -> p l h"),
                                prod[:, b % 2, :, :].rearrange("p u (h k) -> p u h k", h=H),
                                AX.X, ALU.add).then_inc(s_score, 1)

            eT, topT = PB[6][:, 0:IH * P], PB[6][:, IH * P:2 * IH * P]
            L = IH * P
            HG = H * G
            r8 = rows8[:, :].rearrange("p (k h i) -> p k h i", k=3, h=H)
            ahead = end_run[:, 1:HG + 1]
            behind = end_run[:, HG + 1:2 * HG + 1]
            by_row = lambda a: a.rearrange("p (h i l) -> p i h l", h=H, i=IH)
            eout = end_out[:, :].rearrange("p (k i h l) -> p k i h l", k=2, i=IH, h=H)

            def maxima(g, par, use):
                k = [0]

                def step(ins):
                    k[0] += 1
                    ins.then_inc(s_mx, 1)
                    dve.wait_ge(s_mx, g * MX + k[0])

                sg = seg[:, par * (L + 1):(par + 1) * (L + 1)]
                run_in = run_top[:, (1 - par) * H:(2 - par) * H]
                run_out = run_top[:, par * H:(par + 1) * H]
                delta = run_top[:, 2 * H:3 * H]

                def scans():
                    dve.wait_ge(s_seg[par], (use + 1) * 16 * H)
                    dve.wait_ge(s_t1, g + 1)
                    step(v.tensor_tensor_scan(fwd, sg[:, 0:L], eT, 0.0, ALU.add, ALU.max))
                    step(v.tensor_tensor_scan(bwd[:, ::-1], sg[:, L:0:-1], eT[:, ::-1], 0.0,
                                              ALU.add, ALU.max))
                    assert k[0] == MX_SCAN

                def carried():
                    dve.wait_ge(s_t3, g + 1)
                    dve.wait_ge(s_r8, g * 3 + 3)
                    rl = PB[7][0:1, 0:HG].rearrange("p (h i) -> p h i", h=H)
                    step(v.tensor_tensor(delta, run_in, r8[:, 0, :, 0], ALU.add))
                    step(v.tensor_tensor(rl[:, :, 0], rl[:, :, 0], delta, ALU.max))
                    step(v.memset(r8[:, 0, :, 0:1], -BIG))
                    step(v.memset(r8[:, 2, :, G - 1:G], -BIG))
                    step(v.tensor_tensor_scan(ahead, rows8[:, 0:HG], PB[7][0:1, 0:HG], 0.0,
                                              ALU.add, ALU.max))
                    step(v.tensor_tensor_scan(behind[:, ::-1], rows8[:, 3 * HG - 1:2 * HG - 1:-1],
                                              PB[7][0:1, 2 * HG - 1:HG - 1:-1], 0.0, ALU.add, ALU.max))
                    into = rows8[:, HG:2 * HG]
                    step(v.tensor_tensor(eout[:, 0, :, :, :], by_row(end_run[:, 0:HG]), by_row(into), ALU.add))
                    step(v.tensor_tensor(eout[:, 0, 0, :, 0], run_in, r8[:, 1, :, 0], ALU.add))
                    step(v.tensor_tensor(eout[:, 1, :, :, :], by_row(end_run[:, HG + 2:2 * HG + 2]),
                                         by_row(rows8[:, HG + 1:2 * HG + 1]), ALU.add))
                    step(v.memset(eout[:, 1, IH - 1, :, IL - 1:IL], -BIG))
                    assert k[0] == MX_CARRY

                def tops():
                    dve.wait_ge(s_t5, g + 1)
                    step(v.tensor_copy(cols[:, :], PB[7][:, 0:4]))
                    e3 = eT.rearrange("p (i e) -> p i e", i=IH)
                    step(v.tensor_tensor(e3[:, :, 0], e3[:, :, 0], cols[:, 0:IH], ALU.max))
                    step(v.tensor_tensor(e3[:, :, P - 1], e3[:, :, P - 1], cols[:, IH:2 * IH], ALU.max))
                    step(v.tensor_tensor_scan(fwd, sg[:, 0:L], eT, 0.0, ALU.add, ALU.max))
                    step(v.tensor_tensor_scan(bwd[:, ::-1], sg[:, L:0:-1], fwd[:, ::-1], 0.0,
                                              ALU.add, ALU.max))
                    assert k[0] == MX_TOP

                def differences():
                    dve.wait_ge(s_t7, g + 1)
                    step(v.tensor_tensor(delta, run_in, topT[0:1, 0:H * IL:IL], ALU.subtract))
                    step(v.tensor_scalar(delta, delta, carries[0:1, bass.ds(g * G, 1)], None, ALU.mult))
                    v.tensor_copy(run_out, ahead[:, G - 1::G])
                    step(v.tensor_tensor(diff, score[:, par, :], topT, ALU.subtract))
                    assert k[0] == MX_DIFF == MX

                return scans, carried, tops, differences

            def weigh(g, par, b):
                dve.wait_ge(s_ex, g * NBATCH + b + 1)
                rows = rows_of(par, b)[:, :, D:2 * D]
                w = wv[:, b % WR, :, :]
                v.tensor_tensor(w[:, :, 0:D].rearrange("p u (h k) -> p u h k", h=H),
                                rows.rearrange("p u (h k) -> p u h k", h=H),
                                w[:, :, D:W].unsqueeze(3).broadcast_to([P, 4, H, DK]), ALU.mult)\
                    .then_inc(s_wv, 1)

            def blocks_of(g, i, count):
                return nc.values_load_multi_w_load_instructions(
                    iblk[0:1, bass.ds(g * G + i, count)], engines=(dve.engine,), min_val=0,
                    max_val=BLOCKS - 1, skip_runtime_bounds_check_because="clamped when written")[1]

            def rescale(g):
                (blk,) = blocks_of(g, 0, 1)
                a = agg[:, bass.ds(blk * W, W)]
                dve.wait_ge(s_rise, g + 1)
                after(dve, s_add, g, G, 0)
                v.tensor_tensor(a[:, 0:D].rearrange("p (h k) -> p h k", h=H),
                                a[:, 0:D].rearrange("p (h k) -> p h k", h=H),
                                rise[:, :].unsqueeze(2).broadcast_to([P, H, DK]), ALU.mult)\
                    .then_inc(s_resc, 1)
                v.tensor_tensor(a[:, D:W], a[:, D:W], rise[:, :], ALU.mult).then_inc(s_resc, 1)
                dve.wait_ge(s_resc, g * 2 + 2)

            def adding(g, b):
                blks = blocks_of(g, b * 4, 4)

                def add(u):
                    i = b * 4 + u
                    if u % 2 == 0:
                        dve.wait_ge(s_part, g * 2 * NBATCH + i // 2 + 1)
                    after(dve, s_add, g, G, i)
                    a = agg[:, bass.ds(blks[u] * W, W)]
                    v.tensor_tensor(a, a, PB[4 + i // 2 % 2][:, (u % 2) * 256:(u % 2) * 256 + W],
                                    ALU.add).then_inc(s_add, 1)

                return [lambda u=u: add(u) for u in range(4)]

            def merge(a, b):
                for k in range(max(len(a), len(b))):
                    for steps in (a, b):
                        if k < len(steps):
                            steps[k]()

            def group(g, par, use, prev):
                p, gp = 1 - par, g - 1
                scans, carried, tops, differences = maxima(gp, p, use if par else use - 1) if prev else [lambda: 0] * 4
                for s in range(NBATCH):
                    own = [lambda: products(g, par, use, s), lambda: scores(g, par, s)]
                    if s == 0:
                        merge([scans, carried], own)
                    elif s == 1:
                        merge([tops, differences], own)
                    elif prev:
                        if s == 2:
                            weigh(gp, p, 0)
                            rescale(gp)
                            weigh(gp, p, 1)
                        todo = SUMS[s]
                        extra = [lambda b=b: weigh(gp, p, b + 2) for b in todo if b + 2 < NBATCH]
                        steps = own + extra
                        if len(todo) == 2:
                            merge(adding(gp, todo[0]) + adding(gp, todo[1]), steps)
                        else:
                            merge(adding(gp, todo[0]), steps)
                    else:
                        merge([], own)

            group(0, 0, 0, False)
            group(1, 1, 0, True)
            with dve.Fori(1, GROUPS // 2) as it:
                group(it * 2, 0, it, True)
                group(it * 2 + 1, 1, it, True)
            g = GROUPS - 1
            for steps in maxima(g, 1, GROUPS // 2 - 1):
                steps()
            weigh(g, 1, 0)
            rescale(g)
            weigh(g, 1, 1)
            for b in range(NBATCH):
                merge(adding(g, b), [lambda: weigh(g, 1, b + 2)] if b + 2 < NBATCH else [])

            dve.wait_ge(s_add, GROUPS * G)
            v.memset(eps, EPS).then_inc(s_end, 1)
            def stage3(ch):
                k3 = [0]

                def step3(ins):
                    k3[0] += 1
                    ins.then_inc(s_v3, 1)
                    dve.wait_ge(s_v3, ch * V3 + k3[0])

                ag = agg[:, bass.ds(ch * (CB * W), CB * W)].rearrange("p (c w) -> p c w", c=CB)
                rd = rden.rearrange("p (c h) -> p c h", c=CB)
                step3(v.tensor_scalar(rd, ag[:, :, D:W], 1e-30, None, ALU.max))
                step3(v.reciprocal(rden, rden))
                after(dve, s_anb, ch, NB, 0)
                after(dve, s_tr3, ch, CB, 0)
                v.tensor_tensor(an.rearrange("p (c h k) -> p c h k", c=CB, h=H),
                                ag[:, :, 0:D].rearrange("p c (h k) -> p c h k", h=H),
                                rd.unsqueeze(3).broadcast_to([P, CB, H, DK]), ALU.mult).then_inc(s_nrm, 1)
                dve.wait_ge(s_nrm, ch + 1)
                for b in range(2):
                    cab = ca[:, bass.ds(ch * (CB * NB), CB * NB)]\
                        .rearrange("p (c b) -> p c b", b=NB)[:, :, b:b + 1]
                    v.tensor_tensor(anb[:, b, :].rearrange("p (c d) -> p c d", c=CB),
                                    an.rearrange("p (c d) -> p c d", c=CB),
                                    cab.broadcast_to([P, CB, D]), ALU.mult).then_inc(s_anb, 1)
                after(dve, s_fin, ch, CB, 0)
                for h, (c0, c1) in enumerate(((0, 4), (4, CB))):
                    dve.wait_ge(s_o3, ch * 2 + h + 1)
                    v.scalar_tensor_tensor(y[:, c0 * D:c1 * D], PB[4 + h][:, 0:(c1 - c0) * D], 0.0,
                                           x3[:, c0 * D:c1 * D], ALU.max, ALU.add).then_inc(s_res, 1)
                dve.wait_ge(s_res, ch * 2 + 2)
                for c in range(CB):
                    v.bn_stats(stats[:, c, :], y[:, c * D:(c + 1) * D]).then_inc(s_stat, 1)
                dve.wait_ge(s_stat, ch * CB + CB)
                hold(dve)
                for c in range(CB):
                    v.bn_aggr(mv[:, c, :], stats[:, c, :]).then_inc(s_aggr, 1)
                dve.wait_ge(s_std, ch + 1)
                step3(v.reciprocal(rstd, rstd))
                assert k3[0] == V3_RSTD == V3
                after(dve, s_out, ch, 16, 0)
                for c in range(POOL_FROM):
                    v.tensor_scalar(yo[:, c * D:(c + 1) * D], y[:, c * D:(c + 1) * D], mv[:, c, 0:1],
                                    rstd[:, c:c + 1], ALU.subtract, ALU.mult).then_inc(s_fin, 1)

            stage3(0)
            with dve.Fori(1, CHUNKS) as ch:
                stage3(ch)

        @block.sync
        def _(sp):
            for b, w in ((Bq, basis_q), (Bk, basis_k), (Bv, basis_v), (Ba, basis_a)):
                sp.dma_start(b[:, :, :], w.rearrange("b (i o) -> i b o", o=D)).then_inc(s_wload, 16)
            sp.dma_start(Wl[:, :], loop_w).then_inc(s_wload, 16)
            sp.dma_start(brow[:, :], bias.rearrange("(a d) -> a d", a=1)).then_inc(s_wload, 16)

            def tile_load(k, a):
                sp.dma_start(tile_rows[0:FULL, k * P:(k + 1) * P],
                             a[0:FULL * P].rearrange("(t e) -> t e", e=P)).then_inc(s_trow, 16)
                sp.dma_start(tile_rows[FULL:FULL + 1, k * P:k * P + REST],
                             a[FULL * P:].rearrange("(t e) -> t e", t=1)).then_inc(s_trow, 16)

            tile_load(0, dst)
            tile_load(1, src)
            tile_load(2, edge_type)
            sp.wait_ge(s_setup, mark["pad"])
            p3 = pad_rows.rearrange("p (k e) -> p k e", k=3)
            r3 = tile_rows.rearrange("t (k e) -> t k e", k=3)
            sp.dma_start(r3[FULL:FULL + 1, :, REST:P], p3[0:1, :, REST:P]).then_inc(s_trow, 16)
            sp.dma_start(r3[FULL + 1:TILES, :, :], p3[1:PADT, :, :]).then_inc(s_trow, 16)

            def chunk_in(ch):
                after(sp, s_xt, ch, CB, 0)
                hold(sp)
                full = CB if not (known(ch) and ch == CHUNKS - 1) else CB - 1
                xi = x_in.rearrange("p (c d) -> p c d", c=CB)
                sp.dma_start(xi[:, 0:full, :],
                             x[bass.ds(ch * CN, full * P), :].rearrange("(c p) d -> p c d", p=P))\
                    .then_inc(s_xin, 16)
                rest = N - (CHUNKS - 1) * CN - (CB - 1) * P
                if full < CB:
                    sp.dma_start(xi[0:rest, full, :], x[N - rest:N, :]).then_inc(s_xin, 16)
                after(sp, s_ot, ch, 1, 0)
                hold(sp)
                many = CN if full == CB else N - (CHUNKS - 1) * CN
                for k in range(3):
                    sp.dma_start(ntype[32 * k:32 * k + T, 0:many],
                                 node_type[bass.ds(ch * CN, many)].rearrange("(a n) -> a n", a=1)
                                 .broadcast_to([T, many])).then_inc(s_nt, 16)

            def chunk_out(ch):
                for blk in range(CB):
                    sp.wait_ge(s_ta, (ch * CB + blk) * 2 + 2)
                    sp.wait_ge(s_tv, (ch * CB + blk) * 2 + 2)
                    hold(sp)
                    sp.dma_start(table[bass.ds((ch * CB + blk) * P * T, P * T), :]
                                 .rearrange("(p t) f -> p t f", t=T),
                                 stage[:, blk % 2, :, :]).then_inc(s_tab[blk % 2], 16)

            sp.wait_ge(s_setup, mark["comp_zero"])
            chunk_in(0)
            sp.wait_ge(s_trow, 16 * 8)
            sp.dma_start(tdst, tile_rows.rearrange("(p c) f -> p c f", c=TPR)[:, :, 0:P])\
                .then_inc(s_tdst, 16)
            sp.wait_ge(s_setup, mark["tiles"])
            sp.dma_start(tile_blocks.rearrange("k (p c) -> p k c", c=TPR), fc[0:TROWS, 0:2, :])\
                .then_inc(s_tb, 16)
            sp.wait_ge(s_tb, 16)
            sp.dma_start(tfl, tile_blocks.rearrange("(a k) t -> a (k t)", a=1).broadcast_to([P, 2 * TILES]))\
                .then_inc(s_tbr, 16)
            chunk_in(1)
            chunk_out(0)
            sp.wait_ge(s_setup, mark["item_block"])
            sp.dma_start(item_block.rearrange("a (p c) -> (a p) c", c=IPR), ic[:, 1, :]).then_inc(s_iblk, 16)
            sp.wait_ge(s_iblk, 16)
            sp.dma_start(iblk[:, :], item_block).then_inc(s_iblk, 16)
            chunk_in(2)
            chunk_out(1)
            sp.wait_ge(s_setup, mark["item_ends"])
            kd = item_keys.rearrange("k (p c) -> p k c", c=IPR)
            sp.dma_start(kd[:, 0:1, :], fc[:, 0:1, :]).then_inc(s_ikey, 16)
            sp.dma_start(kd[:, 1:3, :], fc[:, 3:5, :]).then_inc(s_ikey, 16)
            sp.wait_ge(s_ikey, 32)
            sp.dma_start(krow, item_keys.rearrange("(a k) i -> a k i", a=1)).then_inc(s_ikey, 16)
            sp.wait_ge(s_setup, mark["bias"])
            sp.dma_start(item_bias.rearrange("(p c) e -> p c e", c=IPR), biasr).then_inc(s_ibias, 16)
            chunk_in(3)
            chunk_out(2)
            with sp.Fori(3, CHUNKS - 2) as ch:
                chunk_in(ch + 1)
                chunk_out(ch)
            chunk_in(CHUNKS - 1)
            chunk_out(CHUNKS - 2)
            chunk_out(CHUNKS - 1)

            sp.wait_ge(s_setup, mark["stage0"])

            def group(g, par):
                after(sp, s_score, g - 2, NBATCH, NBATCH)
                hold(sp)
                sp.dma_start(idx_now[par][:, :], rows_idx[:, bass.ds(g * G, G)]).then_inc(s_idx[par], 16)
                after(sp, s_mx, g - 2, MX, MX_TOP)
                hold(sp)
                seg3 = seg[:, par * (IH * P + 1):par * (IH * P + 1) + IH * P]\
                    .rearrange("p (i e) -> p i e", i=IH)
                rows = item_bias[bass.ds(g * G, G), :].rearrange("(i l) e -> l i e", l=IL)
                for h in range(H):
                    sp.dma_start(seg3[h * IL:(h + 1) * IL, :, :], rows).then_inc(s_seg[par], 16)

            group(0, 0)
            group(1, 1)
            with sp.Fori(1, GROUPS // 2) as it:
                group(it * 2, 0)
                group(it * 2 + 1, 1)

            sp.wait_ge(s_end, 1)
            whole = BLOCKS - 1
            rest = N - whole * P

            def load(ch):
                after(sp, s_res, ch, 2, 0)
                hold(sp)
                last = known(ch) and ch == CHUNKS - 1
                n = CB - 1 if last else CB
                xc = x3.rearrange("p (c d) -> p c d", c=CB)
                sp.dma_start(xc[:, 0:n, :],
                             x[bass.ds(ch * CN, n * P), :].rearrange("(c p) d -> p c d", p=P)).then_inc(s_x3, 16)
                if last:
                    sp.dma_start(xc[0:rest, n, :], x[whole * P:N, :]).then_inc(s_x3, 16)

            def store(ch):
                sp.wait_ge(s_fin, ch * CB + CB)
                hold(sp)
                last = known(ch) and ch == CHUNKS - 1
                n = CB - 1 if last else CB
                oc = yo.rearrange("p (c d) -> p c d", c=CB)
                sp.dma_start(out[bass.ds(ch * CN, n * P), :].rearrange("(c p) d -> p c d", p=P),
                             oc[:, 0:n, :]).then_inc(s_out, 16)
                if last:
                    sp.dma_start(out[whole * P:N, :], oc[0:rest, n, :]).then_inc(s_out, 16)

            load(0)
            load(1)
            store(0)
            with sp.Fori(1, CHUNKS - 2) as ch:
                load(ch + 1)
                store(ch)
            load(CHUNKS - 1)
            store(CHUNKS - 2)
            store(CHUNKS - 1)
            sp.wait_ge(s_out, 16 * (CHUNKS + 1))

        @block.gpsimd
        def _(pool):
            g_ = nc.gpsimd
            g_.memset(ident[:, :], 0.0).then_inc(s_const, 1)
            g_.iota(lane[:, :], [[1, P]], base=0, channel_multiplier=0,
                    allow_small_or_imprecise_dtypes=True).then_inc(s_const, 1)
            g_.iota(item_no[:, :], [[1, IPR]], base=0, channel_multiplier=IPR,
                    allow_small_or_imprecise_dtypes=True).then_inc(s_const, 1)
            for k in range(3):
                pool.wait_ge(s_const, 3 + k)
                g_.iota(type_no[32 * k:32 * k + 32, :], [[0, 1]], base=0, channel_multiplier=1,
                        allow_small_or_imprecise_dtypes=True).then_inc(s_const, 1)
            pool.wait_ge(s_const, 6)
            g_.affine_select(out=ident[:, :], in_=ident[:, :], compare_op=ALU.not_equal, fill=1.0,
                             base=0, pattern=[[-1, P]], channel_multiplier=1).then_inc(s_const, 1)

            pool.wait_ge(s_setup, mark["item_tile"])
            for k in range(IPR):
                pool.indirect_dma_start(
                    out=irow[:, k, :], out_offset=None, in_=tile_rows,
                    in_offset=bass.IndirectOffsetOnAxis(ap=ic[:, 0, k:k + 1], axis=0)).then_inc(s_irow, 16)

            for r in range(2):
                pool.wait_ge(s_tab[r], 16 * RING[r] * CHUNKS)

            def gather(g, par, use):
                after(pool, s_idx[par], use, 16, 16)
                for b in range(NBATCH):
                    after(pool, s_wv, g - 2, NBATCH, b + 1)
                    hold(pool)
                    for u in range(4):
                        i = b * 4 + u
                        o = (par * G + i) * 2 * D
                        pool.indirect_dma_start(
                            out=kv[:, o:o + 2 * D], out_offset=None, in_=table,
                            in_offset=bass.IndirectOffsetOnAxis(ap=idx_now[par][:, i:i + 1], axis=0))\
                            .then_inc(s_kv[par][b], 16)

            gather(0, 0, 0)
            gather(1, 1, 0)
            with pool.Fori(1, GROUPS // 2) as it:
                gather(it * 2, 0, it)
                gather(it * 2 + 1, 1, it)

            def coefficients(ch):
                pool.wait_ge(s_nrm, ch + 1)
                after(pool, s_tr3, ch, CB, 0)
                hold(pool)
                for b in range(2, NB):
                    cab = ca[:, bass.ds(ch * (CB * NB), CB * NB)].rearrange("p (c b) -> p c b", b=NB)[:, :, b:b + 1]
                    g_.tensor_tensor(anb[:, b, :].rearrange("p (c d) -> p c d", c=CB),
                                     an.rearrange("p (c d) -> p c d", c=CB),
                                     cab.broadcast_to([P, CB, D]), ALU.mult).then_inc(s_anb, 1)

            def normalise(ch):
                pool.wait_ge(s_v3, ch * V3 + V3_RSTD)
                after(pool, s_out, ch, 16, 0)
                hold(pool)
                for c in range(POOL_FROM, CB):
                    g_.tensor_scalar(yo[:, c * D:(c + 1) * D], y[:, c * D:(c + 1) * D], mv[:, c, 0:1],
                                     rstd[:, c:c + 1], ALU.subtract, ALU.mult).then_inc(s_fin, 1)

            coefficients(0)
            normalise(0)
            with pool.Fori(1, CHUNKS) as ch:
                coefficients(ch)
                normalise(ch)

        @block.scalar
        def _(act):
            a_ = nc.scalar
            act.wait_ge(s_setup, mark["comp_zero"])
            for k in range(3):
                for j, w in enumerate((comp_q, comp_k, comp_v, comp_a)):
                    act.dma_start(comp[32 * k:32 * k + T, j * NB:(j + 1) * NB], w).then_inc(s_comp, 16)
            for h in range(H):
                r = slice(h * DK, (h + 1) * DK)
                for m, w in ((att, rel_att), (msg, rel_msg)):
                    act.dma_start(m.rearrange("p (t d) -> p t d", t=T)[r, :, r],
                                  w[:, h, :, :].rearrange("t i j -> i t j")).then_inc(s_rel, 16)
                with nc.allow_non_contiguous_dma(reason="64 priorities"):
                    act.dma_start(pri[r, :], rel_pri[:, h:h + 1].rearrange("t a -> a t").broadcast_to([DK, T]))\
                        .then_inc(s_rel, 16)

            def stage1(ch):
                for u, (c0, c1) in enumerate(((0, 4), (4, CB))):
                    act.wait_ge(s_xt, ch * CB + c1)
                    if u == 0:
                        after(act, s_sc, ch, 24, 0)
                    a_.activation(xT[:, c0 * P:c1 * P], PB[2 + u][:, 0:(c1 - c0) * P], ACT.Copy)\
                        .then_inc(s_xtc, 1)
                for o in range(PJ):
                    act.wait_ge(s_pj, ch * PJ + o + 1)
                    bank = PB[2 + o % 2]
                    if o < CB:
                        hold(act)
                        a_.activation(q_all[:, bass.ds((ch * CB + o) * D, D)], bank[:, 0:D], ACT.Copy)
                        a_.activation(ca[:, bass.ds((ch * CB + o) * NB, NB)], bank[:, D:D + NB], ACT.Copy)\
                            .then_inc(s_pjc, 1)
                    else:
                        kind, h = (o - CB) // 2, (o - CB) % 2
                        if o == CB:
                            after(act, s_tk, ch, CB * 4, 0)
                        a_.activation(kvT[:, kind, h * HALF:(h + 1) * HALF], bank[:, 0:HALF], ACT.Copy)\
                            .then_inc(s_pjc, 1)
                for blk in range(CB):
                    for u in range(2):
                        act.wait_ge(s_tk, (ch * CB + blk) * 4 + u + 1)
                        if u == 0:
                            after(act, s_tab[blk % 2], ch, 16 * RING[blk % 2], 16 * (blk // 2))
                        a_.activation(stage[:, blk % 2, 4 * u:4 * u + 4, 0:D],
                                      PB[4 + u][:, :].rearrange("p (t d) -> p t d", t=4), ACT.Copy)\
                            .then_inc(s_ta, 1)

            for ch in range(3):
                stage1(ch)
            with act.Fori(3, CHUNKS) as ch:
                stage1(ch)

            act.wait_ge(s_tk, CHUNKS * CB * 4)
            act.wait_ge(s_setup, mark["stage0"])

            def one_hot(g, par, b):
                after(act, s_hot, g, NBATCH, b)
                hold(act)
                for u in range(4):
                    a_.activation(sq[:, u, :], lane[:, :], ACT.Square,
                                  bias=neg_lane[:, bass.ds(g * G + b * 4 + u, 1)]).then_inc(s_sq, 1)
                act.wait_ge(s_sq, g * G + b * 4 + 4)
                after(act, s_part, g - 2, 2 * NBATCH, 2 * b + 2)
                o = (par * G + b * 4) * P
                a_.activation(onehot[:, o:o + 4 * P], sq[:, :, :].rearrange("p u e -> p (u e)"), ACT.Relu,
                              bias=1.0, scale=-1.0).then_inc(s_hot, 1)

            def evacuate(g, b):
                act.wait_ge(s_turn, g * NBATCH + b + 1)
                after(act, s_qe, g, NBATCH, b - 1)
                a_.activation(spread[:, b % 2, :, :].rearrange("p u e -> p (u e)"), PB[b % 2][:, :], ACT.Copy)\
                    .then_inc(s_spr, 1)

            def carry_terms(g):
                after(act, s_mx, g - 1, MX, MX_CARRY)
                hold(act)
                for k in range(3):
                    a_.activation(rows8[:, k * H * G:(k + 1) * H * G].rearrange("p (h i) -> p h i", h=H),
                                  car[:, k, bass.ds(g * G, G)].unsqueeze(1).broadcast_to([1, H, G]),
                                  ACT.Copy).then_inc(s_r8, 1)

            def exponentials(g, b):
                if b == 0:
                    act.wait_ge(s_mx, g * MX + MX)
                after(act, s_part, g, 2 * NBATCH, 2 * (b - WR) + 2)
                o = b // (IL // 4) * H * IL
                l0 = b % (IL // 4) * 4
                d = diff[:, o:o + H * IL].rearrange("p (h l) -> p l h", h=H)[:, l0:l0 + 4, :]
                a_.activation(wv[:, b % WR, :, D:W], d, ACT.Exp).then_inc(s_ex, 1)

            def rise_exp(g):
                act.wait_ge(s_t9, g + 1)
                after(act, s_resc, g, 2, 0)
                a_.activation(rise[:, :], PB[7][:, 8:8 + H], ACT.Exp).then_inc(s_rise, 1)

            def group(g, par, prev, final=False):
                for s in range(NBATCH):
                    if prev and s == 0:
                        carry_terms(g - 1)
                    if prev and s == 2:
                        exponentials(g - 1, 0)
                        rise_exp(g - 1)
                        exponentials(g - 1, 1)
                    if prev:
                        for b in SUMS[s]:
                            if b + 2 < NBATCH:
                                exponentials(g - 1, b + 2)
                    if s + 3 < NBATCH:
                        one_hot(g, par, s + 3)
                    elif not final:
                        one_hot(g + 1, 1 - par, s + 3 - NBATCH)
                    if s + 2 < NBATCH:
                        evacuate(g, s + 2)
                    elif not final:
                        evacuate(g + 1, s + 2 - NBATCH)

            for b in range(3):
                one_hot(0, 0, b)
            for b in range(2):
                evacuate(0, b)
            group(0, 0, False)
            group(1, 1, True)
            with act.Fori(1, GROUPS // 2 - 1) as it:
                group(it * 2, 0, True)
                group(it * 2 + 1, 1, True)
            group(GROUPS - 2, 0, True)
            group(GROUPS - 1, 1, True, final=True)
            carry_terms(GROUPS - 1)
            exponentials(GROUPS - 1, 0)
            rise_exp(GROUPS - 1)
            for b in range(1, NBATCH):
                exponentials(GROUPS - 1, b)

            def stage3(ch):
                for u, (c0, c1) in enumerate(((0, 4), (4, CB))):
                    act.wait_ge(s_xt3, ch * CB + c1)
                    after(act, s_mm3, ch, CB, 0)
                    a_.activation(xT3[:, c0 * P:c1 * P], PB[2 + u][:, 0:(c1 - c0) * P], ACT.Copy)\
                        .then_inc(s_xc3, 1)
                for c in range(CB):
                    act.wait_ge(s_tr3, ch * CB + c + 1)
                    after(act, s_mm3, ch, CB, max(c - 1, 0))
                    a_.activation(anT[:, c % 2, :, :].rearrange("p b n -> p (b n)"), PB[c % 2][:, :], ACT.Copy)\
                        .then_inc(s_cp3, 1)
                act.wait_ge(s_aggr, ch * CB + CB)
                a_.activation(rstd, mv[:, :, 1], ACT.Sqrt, bias=eps[:, 0:1]).then_inc(s_std, 1)

            stage3(0)
            with act.Fori(1, CHUNKS) as ch:
                stage3(ch)

        @block.tensor
        def _(pe):
            t_ = nc.tensor

            def stage1(ch):
                last = known(ch) and ch == CHUNKS - 1
                pe.wait_ge(s_xin, (ch + (2 if last else 1)) * 16)
                after(pe, s_pjc, ch, PJ, 0)
                for c in range(CB):
                    t_.transpose(PB[2 + c // 4][:, c % 4 * P:(c % 4 + 1) * P], x_in[:, c * D:(c + 1) * D],
                                 ident[:, :]).then_inc(s_xt, 1)
                pe.wait_ge(s_ot, ch + 1)

                def coefficients(kind):
                    for h in range(2):
                        for b in range(NB):
                            j = (kind * 2 + h) * NB + b
                            after(pe, s_sc, ch, 24, j - 1)
                            t_.matmul(PB[j % 2][:, 0:HALF], comp_w[:, kind * NB + b, :],
                                      is_type[:, h * HALF:(h + 1) * HALF], start=True, stop=True)\
                                .then_inc(s_cb, 1)

                def place(o):
                    if o < 2:
                        pe.wait_ge(s_xtc, ch * 2 + 2)
                    else:
                        pe.wait_ge(s_pjc, ch * PJ + o - 1)
                    return PB[2 + o % 2]

                def project(kind, B):
                    for h in range(2):
                        pe.wait_ge(s_sc, ch * 24 + (kind * 2 + h + 1) * NB)
                        o = CB + (kind - 1) * 2 + h
                        bank = place(o)
                        for b in range(NB):
                            mm = t_.matmul(bank[:, 0:HALF], B[:, b, :],
                                           scaled[:, kind % 2, b, h * HALF:(h + 1) * HALF],
                                           start=(b == 0), stop=(b == NB - 1))
                        mm.then_inc(s_pj, 1)

                coefficients(0)
                coefficients(1)
                for o in range(CB):
                    pe.wait_ge(s_sc, ch * 24 + (2 if (o + 1) * P > HALF else 1) * NB)
                    bank = place(o)
                    for b in range(NB):
                        t_.matmul(bank[:, 0:D], scaled[:, 0, b, o * P:(o + 1) * P], Bq[:, b, :],
                                  start=(b == 0), stop=(b == NB - 1))
                    t_.matmul(bank[:, D:D + NB], is_type[:, o * P:(o + 1) * P], comp_s[:, 3 * NB:4 * NB],
                              start=True, stop=True).then_inc(s_pj, 1)
                coefficients(2)
                project(1, Bk)
                project(2, Bv)
                for blk in range(CB):
                    for j in range(4):
                        kind, h = j // 2, j % 2
                        if blk == 0 and h == 0:
                            pe.wait_ge(s_pjc, ch * PJ + CB + 2 * kind + 2)
                        after(pe, (s_ta, s_tv)[kind], ch, 2 * CB, 2 * blk + h - 1)
                        t_.matmul(PB[4 + j][:, :], kvT[:, kind, blk * P:(blk + 1) * P],
                                  (att, msg)[kind][:, h * 512:(h + 1) * 512], start=True, stop=True)\
                            .then_inc(s_tk, 1)

            pe.wait_ge(s_const, 7)
            pe.wait_ge(s_wload, 16 * 6)
            pe.wait_ge(s_setup, mark["att"])
            for ch in range(3):
                stage1(ch)
            pe.wait_ge(s_setup, mark["rows"])
            pe.wait_ge(s_ta, 3 * 2 * CB)
            pe.wait_ge(s_tv, 3 * 2 * CB)
            for a, (rows, bank) in enumerate(((lanes, 4), (srcf, 6))):
                for k in range(IPR):
                    t_.transpose(PB[bank + k // 4][:, k % 4 * P:(k % 4 + 1) * P], rows[:, k, :],
                                 ident[:, :]).then_inc(s_turned, 1)
            pe.wait_ge(s_untld, 2 * IPR)
            with pe.Fori(3, CHUNKS - 1) as ch:
                stage1(ch)
            stage1(CHUNKS - 1)

            pe.wait_ge(s_pjc, CHUNKS * PJ)
            pe.wait_ge(s_ta, CHUNKS * 2 * CB)
            pe.wait_ge(s_tv, CHUNKS * 2 * CB)
            pe.wait_ge(s_iblk, 32)
            L = IH * P
            HG = H * G

            def turn(g, par, b):
                pe.wait_ge(s_hot, g * NBATCH + b + 1)
                after(pe, s_spr, g, NBATCH, b - 1)
                for u in range(4):
                    o = (par * G + b * 4 + u) * P
                    mm = t_.transpose(PB[b % 2][:, u * P:(u + 1) * P], onehot[:, o:o + P], ident[:, :])
                mm.then_inc(s_turn, 1)

            def queries(g, b):
                blks = nc.values_load_multi_w_load_instructions(
                    iblk[0:1, bass.ds(g * G + b * 4, 4)], engines=(pe.engine,), min_val=0,
                    max_val=BLOCKS - 1, skip_runtime_bounds_check_because="clamped when written")[1]
                pe.wait_ge(s_spr, g * NBATCH + b + 1)
                after(pe, s_prod, g, NBATCH, b - 1)
                for u in range(4):
                    mm = t_.matmul(PB[2 + b % 2][:, u * D:(u + 1) * D], spread[:, b % 2, u, :],
                                   q_all[:, bass.ds(blks[u] * D, D)], start=True, stop=True)
                mm.then_inc(s_qe, 1)

            def turn_scores(g, par):
                pe.wait_ge(s_score, g * NBATCH + NBATCH)
                for i in range(IH):
                    mm = t_.transpose(PB[6][:, i * P:(i + 1) * P], score[:, par, i * P:(i + 1) * P], ident[:, :])
                mm.then_inc(s_t1, 1)

            def turn_ends(g):
                pe.wait_ge(s_mx, g * MX + MX_SCAN)
                after(pe, s_rise, g, 1, 0)
                for k, (scan, e) in enumerate(((fwd, P - 1), (bwd, 0))):
                    for i in range(IH):
                        dest = PB[7][0:1, k * HG:(k + 1) * HG].rearrange("p (h j) -> p h j", h=H)
                        mm = t_.transpose(dest[:, :, i * IL:(i + 1) * IL], scan[:, i * P + e:i * P + e + 1],
                                          ident[:, :])
                mm.then_inc(s_t3, 1)

            def turn_carried(g):
                pe.wait_ge(s_mx, g * MX + MX_CARRY)
                for k in range(2):
                    for i in range(IH):
                        o = (k * IH + i) * P
                        mm = t_.matmul(PB[7][:, k * IH + i:k * IH + i + 1], end_out[:, o:o + P],
                                       ones[0:1, 0:1], start=True, stop=True)
                mm.then_inc(s_t5, 1)

            def turn_tops(g):
                pe.wait_ge(s_mx, g * MX + MX_TOP)
                for i in range(IH):
                    mm = t_.transpose(PB[6][:, L + i * P:L + (i + 1) * P], bwd[:, i * P:(i + 1) * P],
                                      ident[:, :])
                mm.then_inc(s_t7, 1)

            def place_rise(g, par):
                pe.wait_ge(s_mx, g * MX + MX_DIFF)
                t_.matmul(PB[7][:, 8:8 + H], onehot[0:1, par * G * P:par * G * P + P],
                          run_top[:, 2 * H:3 * H], start=True, stop=True).then_inc(s_t9, 1)

            def sums(g, par, b):
                for h in range(2):
                    pe.wait_ge(s_wv, g * NBATCH + b + 1)
                    after(pe, s_add, g, G, 4 * b + 2 * h - 2)
                    for u in range(2):
                        i = b * 4 + h * 2 + u
                        bank = PB[4 + h]
                        o = (par * G + i) * P
                        mm = t_.matmul(bank[:, u * 256:u * 256 + W], onehot[:, o:o + P],
                                       wv[:, b % WR, h * 2 + u, :], start=True, stop=True)
                    mm.then_inc(s_part, 1)

            def group(g, par, prev, final=False):
                gp, p = g - 1, 1 - par
                for s in range(NBATCH):
                    if prev and s == 0:
                        turn_scores(gp, p)
                        turn_ends(gp)
                    if prev and s == 1:
                        turn_carried(gp)
                        turn_tops(gp)
                    if prev and s == 2:
                        place_rise(gp, p)
                    if s + 1 < NBATCH:
                        queries(g, s + 1)
                    elif not final:
                        queries(g + 1, 0)
                    if prev:
                        for b in SUMS[s]:
                            sums(gp, p, b)
                    if s + 2 < NBATCH:
                        turn(g, par, s + 2)
                    elif not final:
                        turn(g + 1, p, s + 2 - NBATCH)

            turn(0, 0, 0)
            turn(0, 0, 1)
            queries(0, 0)
            group(0, 0, False)
            group(1, 1, True)
            with pe.Fori(1, GROUPS // 2 - 1) as it:
                group(it * 2, 0, True)
                group(it * 2 + 1, 1, True)
            group(GROUPS - 2, 0, True)
            group(GROUPS - 1, 1, True, final=True)
            g = GROUPS - 1
            turn_scores(g, 1)
            turn_ends(g)
            turn_carried(g)
            turn_tops(g)
            place_rise(g, 1)
            for b in range(NBATCH):
                sums(g, 1, b)

            def stage3(ch):
                last = known(ch) and ch == CHUNKS - 1
                pe.wait_ge(s_x3, (ch + (2 if last else 1)) * 16)
                after(pe, s_xc3, ch, 2, 0)
                for c in range(CB):
                    t_.transpose(PB[2 + c // 4][:, c % 4 * P:(c % 4 + 1) * P], x3[:, c * D:(c + 1) * D],
                                 ident[:, :]).then_inc(s_xt3, 1)

                def turn3(c):
                    if c == 0:
                        pe.wait_ge(s_anb, ch * NB + NB)
                    after(pe, s_cp3, ch, CB, max(c - 1, 0))
                    for b in range(NB):
                        mm = t_.transpose(PB[c % 2][:, b * P:(b + 1) * P], anb[:, b, c * D:(c + 1) * D],
                                          ident[:, :])
                    mm.then_inc(s_tr3, 1)

                turn3(0)
                for c in range(CB):
                    if c + 1 < CB:
                        turn3(c + 1)
                    if c % 4 == 0:
                        pe.wait_ge(s_xc3, ch * 2 + c // 4 + 1)
                        after(pe, s_res, ch, 2, 0)
                    pe.wait_ge(s_cp3, ch * CB + c + 1)
                    o = PB[4 + c // 4][:, c % 4 * D:(c % 4 + 1) * D]
                    for b in range(NB):
                        mm = t_.matmul(o, anT[:, c % 2, b, :], Ba[:, b, :], start=(b == 0), stop=False)
                    mm.then_inc(s_mm3, 1)
                    t_.matmul(o, xT3[:, c * P:(c + 1) * P], Wl[:, :], start=False, stop=False)
                    mm = t_.matmul(o, ones[0:1, :], brow[:, :], start=False, stop=True)
                    if c in (3, CB - 1):
                        mm.then_inc(s_o3, 1)

            stage3(0)
            with pe.Fori(1, CHUNKS - 1) as ch:
                stage3(ch)
            stage3(CHUNKS - 1)



_INS = ["x", "src", "dst", "edge_type_8", "node_type_8",
        "L0_gnn_w_comp_k", "L0_gnn_w_basis_k", "L0_gnn_w_comp_q", "L0_gnn_w_basis_q",
        "L0_gnn_w_comp_v", "L0_gnn_w_basis_v", "L0_gnn_w_comp_a", "L0_gnn_w_basis_a",
        "L0_gnn_relation_pri", "L0_gnn_relation_att", "L0_gnn_relation_msg",
        "L0_gnn_loop_weight", "L0_gnn_bias"]


def kernel(**inputs):
    import numpy as _np
    import concourse.bacc as _bacc
    from concourse import mybir as _mybir
    from concourse.bass_utils import run_bass_kernel_spmd as _run

    nc = _bacc.Bacc("TRN2", target_bir_lowering=False, num_devices=1)
    arrays, args = {}, []
    for name in _INS:
        a = _np.ascontiguousarray(inputs[name])
        arrays[f"in_{name}_dram"] = a
        args.append(nc.dram_tensor(f"in_{name}_dram", a.shape, _mybir.dt.from_np(a.dtype), kind="ExternalInput").ap())
    n, d = arrays["in_x_dram"].shape
    args.append(nc.dram_tensor("out_0_dram", (n, d), _mybir.dt.float32, kind="ExternalOutput").ap())
    graph_transformer_layer(nc, *args)
    r = _run(nc, [arrays], core_ids=[0])
    return r.results[0]["out_0_dram"]
```

```python
import concourse.bass as bass
from concourse import mybir
from contextlib import ExitStack


def graph_transformer_layer(
    nc: bass.Bass,
    x: bass.AP,
    src: bass.AP,
    dst: bass.AP,
    edge_type: bass.AP,
    node_type: bass.AP,
    comp_k: bass.AP,
    basis_k: bass.AP,
    comp_q: bass.AP,
    basis_q: bass.AP,
    comp_v: bass.AP,
    basis_v: bass.AP,
    comp_a: bass.AP,
    basis_a: bass.AP,
    rel_pri: bass.AP,
    rel_att: bass.AP,
    rel_msg: bass.AP,
    loop_w: bass.AP,
    bias: bass.AP,
    out: bass.AP,
):
    f32, i32, bf16 = mybir.dt.float32, mybir.dt.int32, mybir.dt.bfloat16
    ALU, ACT, AX = mybir.AluOpType, mybir.ActivationFunctionType, mybir.AxisListType

    P = 128
    N, D = x.shape
    E = src.shape[0]
    T, H, DK, _ = rel_att.shape
    NB = comp_k.shape[1]
    SCALE = float(D / H) ** -0.5
    BIG = 1e30
    EPS = 1e-5

    BLOCKS = -(-N // P)
    NP = BLOCKS * P
    CB = 7
    CHUNKS = BLOCKS // CB
    CN = CB * P
    HALF = CN // 2
    assert CHUNKS * CB == BLOCKS and CN % 2 == 0 and HALF <= 512

    G = 32
    NBATCH = G // 4
    IL = 16
    IH = G // IL
    TROWS = 112
    TPR = 7
    TILES = TROWS * TPR
    FULL = E // P
    REST = E - FULL * P
    PADT = TILES - FULL
    assert -(-E // P) <= TILES and TILES + BLOCKS - 1 <= P * TPR
    GROUPS = -(-(TILES + BLOCKS - 1) // G)
    IPR = 7
    ITEMS = P * IPR
    assert GROUPS * G <= ITEMS and GROUPS % 2 == 0
    W = D + H
    WR = 4
    WORK = 4 * P + 2 * 4 * P + 2 * 4 * D + WR * 4 * W + 2 * IH * P + 3 * IH * P

    table = nc.dram_tensor("table", [NP * T, 2 * D], f32, kind="Internal").ap()
    tile_rows = nc.dram_tensor("tile_rows", [TILES, 3 * P], i32, kind="Internal").ap()
    tile_blocks = nc.dram_tensor("tile_blocks", [2, TILES], f32, kind="Internal").ap()
    item_bias = nc.dram_tensor("item_bias", [ITEMS, P], f32, kind="Internal").ap()
    item_keys = nc.dram_tensor("item_keys", [3, ITEMS], f32, kind="Internal").ap()
    item_block = nc.dram_tensor("item_block", [1, ITEMS], i32, kind="Internal").ap()

    ctx = ExitStack()
    with ctx:
        def sb(name, shape, dt=f32):
            return ctx.enter_context(nc.sbuf_tensor(name, shape, dt))

        def pb(name):
            return ctx.enter_context(nc.psum_tensor(name, [P, 512], f32))

        def sem(name):
            return ctx.enter_context(nc.semaphore(name))

        ident = sb("ident", [P, P])
        ones = sb("ones", [1, P])
        lane = sb("lane", [P, P])
        item_no = sb("item_no", [P, IPR])
        type_no = sb("type_no", [96, 1])
        Ba = sb("Ba", [P, NB, D])
        Wl = sb("Wl", [P, D])
        bias_ones = sb("bias_ones", [96, D // 2 + P // 2])
        bias3 = bias_ones[:, 0:D // 2].bitcast(bf16)
        ones3 = bias_ones[:, D // 2:D // 2 + P // 2].bitcast(bf16)
        q_all = sb("q_all", [P, BLOCKS * D])
        agg = sb("agg", [P, BLOCKS * W])
        ca = sb("ca", [P, BLOCKS * NB])
        neg_lane = sb("neg_lane", [P, ITEMS])
        rows_idx = sb("rows_idx", [P, ITEMS], i32)
        iblk = sb("iblk", [1, ITEMS], i32)
        carries = sb("carries", [1, ITEMS])
        carry = sb("carry", [1, 3 * ITEMS], bf16)
        car = carry[:, :].rearrange("p (k i) -> p k i", k=3)
        kv = sb("kv", [P, 2 * G * 2 * D])
        onehot = sb("onehot", [P, 2 * G * P])
        work = sb("work", [P, WORK])
        seg = sb("seg", [P, 2 * (IH * P + 1)])
        rows8 = sb("rows8", [1, 3 * H * G])
        end_run = sb("end_run", [1, 2 * H * G + 2])
        end_out = sb("end_out", [1, 2 * H * G])
        run_top = sb("run_top", [1, 4 * H])
        cols = sb("cols", [P, 4])
        rise = sb("rise", [P, H])
        idx_now = [sb(f"idx_now{r}", [P, G], i32) for r in range(2)]

        class Space:
            def __init__(self, tensor, size, at=0):
                self.tensor, self.size, self.at = tensor, size, at

            def take(self, n, rows=P):
                self.at += n
                assert self.at <= self.size
                return self.tensor[0:rows, self.at - n:self.at]

        s2 = Space(work, WORK)
        sq = s2.take(4 * P).rearrange("p (u e) -> p u e", u=4)
        spread = s2.take(2 * 4 * P).rearrange("p (r u e) -> p r u e", r=2, u=4)
        prod = s2.take(2 * 4 * D).rearrange("p (r u d) -> p r u d", r=2, u=4)
        wv = s2.take(WR * 4 * W).rearrange("p (r u w) -> p r u w", r=WR, u=4)
        score = s2.take(2 * IH * H * IL).rearrange("p (r c) -> p r c", r=2)
        fwd = s2.take(IH * P)
        bwd = s2.take(IH * P)
        diff = s2.take(IH * P)
        s1 = Space(kv, 2 * G * 2 * D)
        x_in = s1.take(CN)
        xT = s1.take(CN)
        scaled = s1.take(2 * NB * CN).rearrange("p (r b n) -> p r b n", r=2, b=NB)
        kvT = s1.take(2 * CN).rearrange("p (r n) -> p r n", r=2)
        stage = s1.take(2 * T * 2 * D).rearrange("p (r t f) -> p r t f", r=2, t=T)
        w1 = Space(work, WORK)
        ntype = w1.take(CN, 96).bitcast(i32)
        is_type = w1.take(CN // 2, 96).bitcast(bf16)
        comp_w = w1.take(2 * NB * P // 2, 96).bitcast(bf16).rearrange("p (j m) -> p j m", m=P)
        Bk, Bv = [w1.take(NB * D).rearrange("p (b d) -> p b d", b=NB) for _ in range(2)]
        pri = w1.take(T)
        comp = w1.take(4 * NB, 96)
        comp_r = w1.take(4 * NB, 96)
        comp_p = w1.take(3 * 2 * NB, 96).bitcast(bf16).rearrange("p (k j) -> p k j", k=3)
        comp_s = w1.take(2 * NB, 96).bitcast(bf16)
        bias_in = w1.take(D, 96)
        bias_p = w1.take(3 * D // 2, 96).bitcast(bf16).rearrange("p (k d) -> p k d", k=3)
        h1 = Space(onehot, 2 * G * P)
        att = h1.take(T * D)
        msg = h1.take(T * D)
        tfl = h1.take(2 * TILES)
        tstart = h1.take(TILES)
        tgap = h1.take(TILES)
        tcmp = h1.take(TILES)
        pairs = [h1.take(2 * TILES)]
        fc = h1.take(IPR * 6).rearrange("p (k c) -> p k c", k=6)
        ic = h1.take(IPR * 3).bitcast(i32).rearrange("p (k c) -> p k c", k=3)
        pad_rows = h1.take(3 * P, PADT).bitcast(i32)
        coef_q = h1.take(BLOCKS * NB)
        a0 = Space(agg, BLOCKS * W)
        rows3 = a0.take(TPR * 3 * P)
        pairs.append(rows3[:, 0:2 * TILES])
        s0i = rows3.bitcast(i32)
        tdst = s0i[0:TROWS, 0:TPR * P].rearrange("p (c e) -> p c e", c=TPR)
        irows = s0i.rearrange("p (c k e) -> p c k e", c=IPR, k=3)
        irow = s0i.rearrange("p (c f) -> p c f", c=IPR)
        lanes = a0.take(IPR * P).rearrange("p (c e) -> p c e", c=IPR)
        krow = a0.take(3 * ITEMS, 1).rearrange("p (k i) -> p k i", k=3)
        etf = tfl[:, 0:IPR * P].rearrange("p (c e) -> p c e", c=IPR)
        srcf = pairs[0][:, 0:IPR * P].rearrange("p (c e) -> p c e", c=IPR)
        biasr = neg_lane[:, :].rearrange("p (c e) -> p c e", c=IPR)
        hq = Space(onehot, 2 * G * P - BLOCKS * NB, at=G * P)
        Bq = hq.take(NB * D)
        x_q = hq.take(CN)
        xTq = hq.take(CN)
        s3 = Space(kv, 2 * G * 2 * D)
        x3 = [s3.take(CN) for _ in range(2)]
        xT3 = [s3.take(CN) for _ in range(2)]
        y = [s3.take(CN) for _ in range(2)]
        yo = s3.take(CN)
        anT = s3.take(2 * NB * P).rearrange("p (r b n) -> p r b n", r=2, b=NB)
        rden = s3.take(CB * H).rearrange("p (c h) -> p c h", c=CB)
        factor = [s3.take(NB * CB * H).rearrange("p (b c h) -> p b c h", b=NB, c=CB) for _ in range(2)]
        stats = s3.take(CB * 6).rearrange("p (c k) -> p c k", c=CB)
        mv = s3.take(CB * 2).rearrange("p (c k) -> p c k", c=CB)
        rstd = s3.take(CB)
        eps = s3.take(1)
        h3 = Space(onehot, 2 * G * P)
        anb = [h3.take(NB * CN).rearrange("p (b n) -> p b n", b=NB) for _ in range(2)]

        PB = [pb(f"pb{i}") for i in range(8)]

        s_const = sem("s_const")
        s_bases_loaded = sem("s_bases_loaded")
        s_last_weights_loaded = sem("s_last_weights_loaded")
        s_comp_loaded = sem("s_comp_loaded")
        s_relations_loaded = sem("s_relations_loaded")
        s_setup = sem("s_setup")
        s_tile_rows = sem("s_tile_rows")
        s_tile_dst = sem("s_tile_dst")
        s_tile_blocks_out = sem("s_tile_blocks_out")
        s_tile_blocks_in = sem("s_tile_blocks_in")
        s_scan = sem("s_scan")
        s_chain = sem("s_chain")
        s_pair_made = sem("s_pair_made")
        s_column = sem("s_column")
        s_item_rows = sem("s_item_rows")
        s_item_blocks = sem("s_item_blocks")
        s_item_keys = sem("s_item_keys")
        s_item_starts = sem("s_item_starts")
        s_lanes_rows = sem("s_lanes_rows")
        s_stage0 = sem("s_stage0")
        s_items_turned = sem("s_items_turned")
        s_items_copied = sem("s_items_copied")
        s_x_loaded = sem("s_x_loaded")
        s_node_types_loaded = sem("s_node_types_loaded")
        s_x_turned = sem("s_x_turned")
        s_xT_copied = sem("s_xT_copied")
        s_types = sem("s_types")
        s_coef_spread = sem("s_coef_spread")
        s_scaled = sem("s_scaled")
        s_projected = sem("s_projected")
        s_projection_copied = sem("s_projection_copied")
        s_hold = sem("s_hold")
        s_table_product = sem("s_table_product")
        s_table_keys = sem("s_table_keys")
        s_table_values = sem("s_table_values")
        s_table_stored = [sem(f"s_table_stored{r}") for r in range(2)]
        s_q_bases = sem("s_q_bases")
        s_x_again = sem("s_x_again")
        s_x_again_turned = sem("s_x_again_turned")
        s_x_again_copied = sem("s_x_again_copied")
        s_q_product = sem("s_q_product")
        s_q_first = sem("s_q_first")
        s_q_terms = sem("s_q_terms")
        s_indices = [sem(f"s_indices{r}") for r in range(2)]
        s_segments = [sem(f"s_segments{r}") for r in range(2)]
        s_gathered = [[sem(f"s_gathered{r}_{b}") for b in range(NBATCH)] for r in range(2)]
        s_squares = sem("s_squares")
        s_one_hot = sem("s_one_hot")
        s_one_hot_turned = sem("s_one_hot_turned")
        s_spread_copied = sem("s_spread_copied")
        s_edge_queries = sem("s_edge_queries")
        s_products = sem("s_products")
        s_scores = sem("s_scores")
        s_scores_turned = sem("s_scores_turned")
        s_ends_turned = sem("s_ends_turned")
        s_carried_turned = sem("s_carried_turned")
        s_tops_turned = sem("s_tops_turned")
        s_rise_placed = sem("s_rise_placed")
        s_carry_terms = sem("s_carry_terms")
        s_maxima = sem("s_maxima")
        s_weights = sem("s_weights")
        s_rise = sem("s_rise")
        s_rescaled = sem("s_rescaled")
        s_weighted = sem("s_weighted")
        s_item_sums = sem("s_item_sums")
        s_added = sem("s_added")
        s_x3_loaded = [sem(f"s_x3_loaded{r}") for r in range(2)]
        s_factors = sem("s_factors")
        s_products_dve = sem("s_products_dve")
        s_products_pool = sem("s_products_pool")
        s_x3_turned = sem("s_x3_turned")
        s_xT3_copied = sem("s_xT3_copied")
        s_products_turned = sem("s_products_turned")
        s_products_copied = sem("s_products_copied")
        s_block_multiplied = sem("s_block_multiplied")
        s_layer_out = sem("s_layer_out")
        s_residual = sem("s_residual")
        s_stats = sem("s_stats")
        s_mean_var = sem("s_mean_var")
        s_deviation = sem("s_deviation")
        s_inverse_deviation = sem("s_inverse_deviation")
        s_normalised = sem("s_normalised")
        s_stored = sem("s_stored")

        block = ctx.enter_context(nc.Block())

        RING = [(CB + 1 - r) // 2 for r in range(2)]
        AHEAD = [0, 3, 3, 3, 3, 2, 2]
        CO = 2 * 2 * NB
        assert len(AHEAD) == CB and sum(AHEAD) == CO
        MX_SCAN, MX_CARRY, MX_TOP, MX_DIFF, MX = 2, 12, 17, 18, 20
        PJ = 5
        V3 = 3
        XAT = 3
        SUMS = [[12, 13], [14, 15]] + [[2 * k, 2 * k + 1] for k in range(6)]
        ADDS = [[11, 12], [13, 14, 15], [0]] + [[2 * k - 1, 2 * k] for k in range(1, 6)]
        SBANKS = [4, 5]
        LAST_SBANKS = [4, 5, 0, 1]
        WEIGHS = [[], [], [0, 1], [2], [3], [4], [5, 6], [7]]
        STAGE0 = 5
        QBANK = [4, 5, 6, 7, 0, 1, 3]
        QGROUPS = [(0, 2), (2, 4), (4, CB)]
        mark = {}

        def known(g):
            return isinstance(g, int)

        def after(engine, s, base, per, k):
            if known(base) and base * per + k <= 0:
                return
            engine.wait_ge(s, base * per + k)

        def hold(engine):
            engine.sem_inc(s_hold, 1)

        @block.vector
        def _(dve):
            n = [0]

            def did(ins, name=None):
                n[0] += 1
                ins.then_inc(s_setup, 1)
                if name:
                    mark[name] = n[0]
                dve.wait_ge(s_setup, n[0])

            v = nc.vector
            did(v.memset(comp, 0.0))
            did(v.memset(ntype, -1), "comp_zero")
            did(v.memset(pad_rows[:, 0:P], NP - 1))
            did(v.memset(pad_rows[:, P:3 * P], 0))
            did(v.memset(bias_in, 0.0), "pad")
            did(v.memset(att, 0.0))
            did(v.memset(msg, 0.0), "rel_zero")

            dve.wait_ge(s_comp_loaded, 16 * 12)
            did(v.tensor_copy(comp_p[:, 0, :], comp))
            did(v.tensor_tensor(comp_r, comp, comp_p[:, 0, :], ALU.subtract))
            did(v.tensor_copy(comp_p[:, 1, :], comp_r))
            did(v.tensor_tensor(comp_r, comp_r, comp_p[:, 1, :], ALU.subtract))
            did(v.tensor_copy(comp_p[:, 2, :], comp_r))
            for k in range(3):
                did(v.tensor_copy(comp_s[32 * k:32 * k + 32, :], comp_p[32 * k:32 * k + 32, k, :]))
            did(v.tensor_copy(comp_w, comp_s[:, 0:2 * NB].unsqueeze(2).broadcast_to([96, 2 * NB, P])),
                "comp")

            def types(ch):
                dve.wait_ge(s_node_types_loaded, ch * 48 + 48)
                after(dve, s_projected, ch - 1, PJ, 1)
                v.tensor_scalar(is_type, ntype, type_no[:, :], None, ALU.is_equal).then_inc(s_types, 1)

            def scale_x(ch, j):
                kind, h, b = j // (2 * NB), j // NB % 2, j % NB
                if j == 0:
                    dve.wait_ge(s_xT_copied, ch * 2 + 2)
                    after(dve, s_projected, ch, PJ, 0)
                dve.wait_ge(s_coef_spread, ch * CO + j + 1)
                v.tensor_tensor(scaled[:, kind, b, h * HALF:(h + 1) * HALF],
                                xT[:, h * HALF:(h + 1) * HALF],
                                PB[j % 2][:, 0:HALF], ALU.mult).then_inc(s_scaled, 1)

            def copy_values(ch, blk, u):
                dve.wait_ge(s_table_product, (ch * CB + blk) * 4 + 2 + u + 1)
                if u == 0:
                    after(dve, s_table_stored[blk % 2], ch, 16 * RING[blk % 2], 16 * (blk // 2))
                v.tensor_copy(stage[:, blk % 2, 4 * u:4 * u + 4, D:2 * D],
                              PB[4 + 2 + u][:, :].rearrange("p (t d) -> p t d", t=4)).then_inc(s_table_values, 1)

            def table(ch, final=False, columns=False):
                j = 0
                for blk in range(CB):
                    n_ahead = 0 if final else AHEAD[blk]
                    for u in range(2):
                        if u < n_ahead:
                            scale_x(ch + 1, j)
                            j += 1
                        copy_values(ch, blk, u)
                    if n_ahead == 3:
                        scale_x(ch + 1, j)
                        j += 1
                    if blk == 0 and not final:
                        types(ch + 1)
                    if columns:
                        item_column(blk)

            def item_column(k):
                dve.wait_ge(s_pair_made, k + 1)
                v.tensor_reduce(fc[:, 0:2, k], pairs[k % 2].rearrange("p (a t) -> p a t", a=2), AX.X,
                                ALU.add).then_inc(s_column, 1)

            dve.wait_ge(s_const, 8)
            types(0)
            for j in range(CO):
                scale_x(0, j)
            dve.wait_ge(s_relations_loaded, 16 * 3 * H)
            a3 = att.rearrange("p (t d) -> p t d", t=T)
            did(v.scalar_tensor_tensor(a3, a3, SCALE, pri.unsqueeze(2).broadcast_to([P, T, D]),
                                       ALU.mult, ALU.mult), "att")
            dve.wait_ge(s_tile_dst, 16)
            did(v.tensor_copy(ic[0:TROWS, 0, :], tdst[:, :, 0]))
            did(v.tensor_copy(ic[0:TROWS, 1, :], tdst[:, :, P - 1]))
            did(v.tensor_scalar(ic[0:TROWS, 2, :], ic[0:TROWS, 0, :], P.bit_length() - 1, None,
                                ALU.logical_shift_right))
            did(v.tensor_copy(fc[0:TROWS, 0, :], ic[0:TROWS, 2, :]))
            did(v.tensor_scalar(ic[0:TROWS, 2, :], ic[0:TROWS, 1, :], P.bit_length() - 1, None,
                                ALU.logical_shift_right))
            did(v.tensor_copy(fc[0:TROWS, 1, :], ic[0:TROWS, 2, :]))
            did(v.scalar_tensor_tensor(fc[0:TROWS, 1, :], fc[0:TROWS, 1, :], 1.0, fc[0:TROWS, 0, :],
                                       ALU.add, ALU.subtract), "tiles")
            dve.wait_ge(s_tile_blocks_in, 16)
            tn = tfl[:, TILES:2 * TILES]
            v.tensor_tensor_scan(tcmp, tn, tn, 0.0, ALU.add, ALU.max).then_inc(s_scan, 1)
            table(0, columns=True)
            dve.wait_ge(s_column, IPR)
            did(v.tensor_scalar(fc[:, 0, :], fc[:, 0, :], -1.0, None, ALU.add))
            did(v.tensor_copy(ic[:, 0, :], fc[:, 0, :]), "item_tile")
            did(v.tensor_tensor(fc[:, 1, :], fc[:, 1, :], item_no[:, :], ALU.add))
            did(v.tensor_scalar(fc[:, 2, :], fc[:, 1, :], float(BLOCKS - 1), None, ALU.min))
            did(v.tensor_copy(ic[:, 1, :], fc[:, 2, :]))
            did(v.tensor_scalar(fc[:, 5, :], fc[:, 1, :], float(P), None, ALU.mult), "item_block")
            dve.wait_ge(s_last_weights_loaded, 16 * 5)
            did(v.memset(ones3, 1.0))
            did(v.tensor_copy(bias_p[:, 0, :], bias_in))
            did(v.tensor_tensor(bias_in, bias_in, bias_p[:, 0, :], ALU.subtract))
            did(v.tensor_copy(bias_p[:, 1, :], bias_in))
            did(v.tensor_tensor(bias_in, bias_in, bias_p[:, 1, :], ALU.subtract))
            did(v.tensor_copy(bias_p[:, 2, :], bias_in))
            for k in range(3):
                did(v.tensor_copy(bias3[32 * k:32 * k + 32, :], bias_p[32 * k:32 * k + 32, k, :]), "bias")
            table(1)
            dve.wait_ge(s_item_starts, 16)
            for a, (o, first_bank) in enumerate(((neg_lane, 4), (rows_idx, 6))):
                turned = o[:, :].rearrange("e (p c) -> e c p", c=IPR)
                for k in range(IPR):
                    if k % 4 == 0:
                        dve.wait_ge(s_items_turned, a * IPR + min(k + 4, IPR))
                    v.tensor_copy(turned[:, k, :],
                                  PB[first_bank + k // 4][:, (k % 4) * P:(k % 4 + 1) * P]).then_inc(s_items_copied, 1)
            table(2)
            with dve.Fori(3, CHUNKS - 1) as ch:
                table(ch)
            table(CHUNKS - 1, final=True)

            def combine(ch):
                for c0, c1 in QGROUPS:
                    for b in range(1, NB):
                        for c in range(c0, c1):
                            if b == 1:
                                dve.wait_ge(s_q_first, ch * CB + c + 1)
                            else:
                                dve.wait_ge(s_q_terms, (ch * CB + c0) * (NB - 1) + (b - 2) * (c1 - c0) + c - c0 + 1)
                            o = q_all[:, bass.ds((ch * CB + c) * D, D)]
                            v.scalar_tensor_tensor(o, PB[QBANK[c]][:, b * D:(b + 1) * D],
                                                   coef_q[:, bass.ds((ch * CB + c) * NB + b, 1)], o,
                                                   ALU.mult, ALU.add).then_inc(s_q_terms, 1)

            combine(0)
            with dve.Fori(1, CHUNKS) as ch:
                combine(ch)

            def rows_of(par, b):
                o = (par * G + b * 4) * 2 * D
                return kv[:, o:o + 4 * 2 * D].rearrange("p (u f) -> p u f", u=4)

            def products(g, par, use, b):
                dve.wait_ge(s_gathered[par][b], use * 64 + 64)
                dve.wait_ge(s_edge_queries, g * NBATCH + b + 1)
                v.tensor_tensor(prod[:, b % 2, :, :], rows_of(par, b)[:, :, 0:D],
                                PB[2 + b % 2][:, :].rearrange("p (u d) -> p u d", u=4), ALU.mult)\
                    .then_inc(s_products, 1)

            def scores(g, par, b):
                dve.wait_ge(s_products, g * NBATCH + b + 1)
                o = b // (IL // 4) * H * IL
                sc = score[:, par, o:o + H * IL].rearrange("p (h l) -> p h l", h=H)
                l0 = b % (IL // 4) * 4
                v.tensor_reduce(sc[:, :, l0:l0 + 4].rearrange("p h l -> p l h"),
                                prod[:, b % 2, :, :].rearrange("p u (h k) -> p u h k", h=H),
                                AX.X, ALU.add).then_inc(s_scores, 1)

            eT, topT = PB[6][:, 0:IH * P], PB[6][:, IH * P:2 * IH * P]
            L = IH * P
            HG = H * G
            r8 = rows8[:, :].rearrange("p (k h i) -> p k h i", k=3, h=H)
            ahead = end_run[:, 1:HG + 1]
            behind = end_run[:, HG + 1:2 * HG + 1]
            by_row = lambda a: a.rearrange("p (h i l) -> p i h l", h=H, i=IH)
            eout = end_out[:, :].rearrange("p (k i h l) -> p k i h l", k=2, i=IH, h=H)

            def maxima(g, par, use):
                k = [0]

                def step(ins):
                    k[0] += 1
                    ins.then_inc(s_maxima, 1)

                def ready():
                    dve.wait_ge(s_maxima, g * MX + k[0])

                sg = seg[:, par * (L + 1):(par + 1) * (L + 1)]
                run_in = run_top[:, (1 - par) * H:(2 - par) * H]
                run_out = run_top[:, par * H:(par + 1) * H]
                delta = run_top[:, 2 * H:3 * H]

                def scans():
                    dve.wait_ge(s_segments[par], (use + 1) * 16 * H)
                    dve.wait_ge(s_scores_turned, g + 1)
                    step(v.tensor_tensor_scan(fwd, sg[:, 0:L], eT, 0.0, ALU.add, ALU.max))
                    step(v.tensor_tensor_scan(bwd[:, ::-1], sg[:, L:0:-1], eT[:, ::-1], 0.0,
                                              ALU.add, ALU.max))
                    assert k[0] == MX_SCAN

                def carried():
                    dve.wait_ge(s_carry_terms, g * 3 + 3)
                    step(v.tensor_tensor(delta, run_in, r8[:, 0, :, 0], ALU.add))
                    ready()
                    step(v.memset(r8[:, 0, :, 0:1], -BIG))
                    step(v.memset(r8[:, 2, :, G - 1:G], -BIG))
                    dve.wait_ge(s_ends_turned, g + 1)
                    rl = PB[7][0:1, 0:HG].rearrange("p (h i) -> p h i", h=H)
                    step(v.tensor_tensor(rl[:, :, 0], rl[:, :, 0], delta, ALU.max))
                    ready()
                    step(v.tensor_tensor_scan(ahead, rows8[:, 0:HG], PB[7][0:1, 0:HG], 0.0,
                                              ALU.add, ALU.max))
                    step(v.tensor_tensor_scan(behind[:, ::-1], rows8[:, 3 * HG - 1:2 * HG - 1:-1],
                                              PB[7][0:1, 2 * HG - 1:HG - 1:-1], 0.0, ALU.add, ALU.max))
                    ready()
                    into = rows8[:, HG:2 * HG]
                    step(v.tensor_tensor(eout[:, 0, :, :, :], by_row(end_run[:, 0:HG]), by_row(into), ALU.add))
                    step(v.tensor_tensor(eout[:, 1, :, :, :], by_row(end_run[:, HG + 2:2 * HG + 2]),
                                         by_row(rows8[:, HG + 1:2 * HG + 1]), ALU.add))
                    ready()
                    step(v.tensor_tensor(eout[:, 0, 0, :, 0], run_in, r8[:, 1, :, 0], ALU.add))
                    step(v.memset(eout[:, 1, IH - 1, :, IL - 1:IL], -BIG))
                    assert k[0] == MX_CARRY

                def tops():
                    dve.wait_ge(s_carried_turned, g + 1)
                    step(v.tensor_copy(cols[:, :], PB[7][:, 0:4]))
                    ready()
                    e3 = eT.rearrange("p (i e) -> p i e", i=IH)
                    step(v.tensor_tensor(e3[:, :, 0], e3[:, :, 0], cols[:, 0:IH], ALU.max))
                    step(v.tensor_tensor(e3[:, :, P - 1], e3[:, :, P - 1], cols[:, IH:2 * IH], ALU.max))
                    ready()
                    step(v.tensor_tensor_scan(fwd, sg[:, 0:L], eT, 0.0, ALU.add, ALU.max))
                    ready()
                    step(v.tensor_tensor_scan(bwd[:, ::-1], sg[:, L:0:-1], fwd[:, ::-1], 0.0,
                                              ALU.add, ALU.max))
                    assert k[0] == MX_TOP

                def differences():
                    dve.wait_ge(s_tops_turned, g + 1)
                    step(v.tensor_tensor(diff, score[:, par, :], topT, ALU.subtract))
                    assert k[0] == MX_DIFF
                    step(v.tensor_tensor(delta, run_in, topT[0:1, 0:H * IL:IL], ALU.subtract))
                    ready()
                    v.tensor_copy(run_out, ahead[:, G - 1::G])
                    step(v.tensor_scalar(delta, delta, carries[0:1, bass.ds(g * G, 1)], None, ALU.mult))
                    assert k[0] == MX

                return scans, carried, tops, differences

            def weigh(g, par, b):
                dve.wait_ge(s_weights, g * NBATCH + b + 1)
                rows = rows_of(par, b)[:, :, D:2 * D]
                w = wv[:, b % WR, :, :]
                v.tensor_tensor(w[:, :, 0:D].rearrange("p u (h k) -> p u h k", h=H),
                                rows.rearrange("p u (h k) -> p u h k", h=H),
                                w[:, :, D:W].unsqueeze(3).broadcast_to([P, 4, H, DK]), ALU.mult)\
                    .then_inc(s_weighted, 1)

            def blocks_of(g, i, count):
                return nc.values_load_multi_w_load_instructions(
                    iblk[0:1, bass.ds(g * G + i, count)], engines=(dve.engine,), min_val=0,
                    max_val=BLOCKS - 1, skip_runtime_bounds_check_because="clamped when written")[1]

            def rescale(g):
                (blk,) = blocks_of(g, 0, 1)
                a = agg[:, bass.ds(blk * W, W)]
                dve.wait_ge(s_rise, g + 1)
                after(dve, s_added, g, G, 0)
                v.tensor_tensor(a[:, 0:D].rearrange("p (h k) -> p h k", h=H),
                                a[:, 0:D].rearrange("p (h k) -> p h k", h=H),
                                rise[:, :].unsqueeze(2).broadcast_to([P, H, DK]), ALU.mult)\
                    .then_inc(s_rescaled, 1)
                v.tensor_tensor(a[:, D:W], a[:, D:W], rise[:, :], ALU.mult).then_inc(s_rescaled, 1)
                dve.wait_ge(s_rescaled, g * 2 + 2)

            def adding(g, halves, banks=SBANKS):
                if not halves:
                    return []
                first = halves[0] * 2
                blks = blocks_of(g, first, len(halves) * 2)

                def add(i):
                    if i % 2 == 0:
                        dve.wait_ge(s_item_sums, g * 2 * NBATCH + i // 2 + 1)
                    after(dve, s_added, g, G, i)
                    a = agg[:, bass.ds(blks[i - first] * W, W)]
                    v.tensor_tensor(a, a, PB[banks[i // 2 % len(banks)]][:, (i % 2) * 256:(i % 2) * 256 + W],
                                    ALU.add).then_inc(s_added, 1)

                return [lambda i=i: add(i) for i in range(first, first + len(halves) * 2)]

            def merge(a, b):
                for k in range(max(len(a), len(b))):
                    for steps in (a, b):
                        if k < len(steps):
                            steps[k]()

            def group(g, par, use, prev):
                p, gp = 1 - par, g - 1
                scans, carried, tops, differences = maxima(gp, p, use if par else use - 1) if prev else [lambda: 0] * 4
                for s in range(NBATCH):
                    mine, my_scores = lambda: products(g, par, use, s), lambda: scores(g, par, s)
                    if not prev:
                        mine()
                        my_scores()
                    elif s == 0:
                        late = adding(g - 2, ADDS[0]) if prev == 2 else [lambda: 0] * 4
                        late[0]()
                        mine()
                        late[1]()
                        scans()
                        late[2]()
                        my_scores()
                        late[3]()
                        carried()
                    elif s == 1:
                        mine()
                        late = adding(g - 2, ADDS[1]) if prev == 2 else [lambda: 0] * 6
                        late[0]()
                        late[1]()
                        tops()
                        late[2]()
                        my_scores()
                        late[3]()
                        differences()
                        late[4]()
                        late[5]()
                    else:
                        extra = [lambda b=b: weigh(gp, p, b) for b in WEIGHS[s]]
                        adds = adding(gp, ADDS[s])
                        if s == 2:
                            mine()
                            extra[0]()
                            rescale(gp)
                            extra[1]()
                            merge(adds, [my_scores])
                        else:
                            merge(adds, [mine] + extra + [my_scores])

            dve.wait_ge(s_stage0, STAGE0)
            group(0, 0, 0, 0)
            group(1, 1, 0, 1)
            with dve.Fori(1, GROUPS // 2) as it:
                group(it * 2, 0, it, 2)
                group(it * 2 + 1, 1, it, 2)
            g = GROUPS - 1
            late = adding(g - 1, ADDS[0] + ADDS[1])
            for k, steps in enumerate(maxima(g, 1, GROUPS // 2 - 1)):
                late[2 * k]()
                late[2 * k + 1]()
                steps()
            late[8]()
            late[9]()
            weigh(g, 1, 0)
            rescale(g)
            weigh(g, 1, 1)
            for b in range(NBATCH):
                merge(adding(g, range(2 * b, 2 * b + 2), LAST_SBANKS), [lambda: weigh(g, 1, b + 2)] if b + 2 < NBATCH else [])

            dve.wait_ge(s_added, GROUPS * G)
            v.memset(eps, EPS)

            def chained(ins, s, base, k):
                ins.then_inc(s, 1)
                dve.wait_ge(s, base + k)

            def products3(ch, par):
                ag = agg[:, bass.ds(ch * (CB * W), CB * W)].rearrange("p (c w) -> p c w", c=CB)
                chained(v.tensor_scalar(rden, ag[:, :, D:W], 1e-30, None, ALU.max), s_factors, ch * V3, 1)
                chained(v.reciprocal(rden, rden), s_factors, ch * V3, 2)
                after(dve, s_products_pool, ch - 1, 2, 0)
                cab = ca[:, bass.ds(ch * (CB * NB), CB * NB)].rearrange("p (c b) -> p b c", b=NB)
                chained(v.tensor_tensor(factor[par], rden.unsqueeze(1).broadcast_to([P, NB, CB, H]),
                                        cab.unsqueeze(3).broadcast_to([P, NB, CB, H]), ALU.mult),
                        s_factors, ch * V3, V3)
                after(dve, s_products_turned, ch - 1, CB, 0)
                for b in range(2):
                    v.tensor_tensor(anb[par][:, b, :].rearrange("p (c h k) -> p c h k", c=CB, h=H),
                                    ag[:, :, 0:D].rearrange("p c (h k) -> p c h k", h=H),
                                    factor[par][:, b].unsqueeze(3).broadcast_to([P, CB, H, DK]),
                                    ALU.mult).then_inc(s_products_dve, 1)

            def residual(ch, par):
                after(dve, s_normalised, ch - 1, CB, 0)
                for h, (c0, c1) in enumerate(((0, 4), (4, CB))):
                    dve.wait_ge(s_layer_out, ch * 2 + h + 1)
                    v.scalar_tensor_tensor(y[par][:, c0 * D:c1 * D], PB[4 + 2 * par + h][:, 0:(c1 - c0) * D],
                                           0.0, x3[par][:, c0 * D:c1 * D], ALU.max, ALU.add)\
                        .then_inc(s_residual, 1)
                    dve.wait_ge(s_residual, ch * 2 + h + 1)
                    for c in range(c0, c1):
                        v.bn_stats(stats[:, c, :], y[par][:, c * D:(c + 1) * D]).then_inc(s_stats, 1)
                dve.wait_ge(s_stats, ch * CB + CB)
                after(dve, s_normalised, ch, CB, 0)
                hold(dve)
                for c in range(CB):
                    v.bn_aggr(mv[:, c, :], stats[:, c, :]).then_inc(s_mean_var, 1)

            def normalise(ch, par):
                dve.wait_ge(s_deviation, ch + 1)
                v.reciprocal(rstd, rstd).then_inc(s_inverse_deviation, 1)
                dve.wait_ge(s_inverse_deviation, ch + 1)
                after(dve, s_stored, ch, 16, 0)
                for c in range(CB):
                    v.tensor_scalar(yo[:, c * D:(c + 1) * D], y[par][:, c * D:(c + 1) * D],
                                    mv[:, c, 0:1], rstd[:, c:c + 1], ALU.subtract, ALU.mult)\
                        .then_inc(s_normalised, 1)

            def stage3(ch, par, first=False, final=False):
                if not final:
                    products3(ch + 1, 1 - par)
                if not first:
                    normalise(ch - 1, 1 - par)
                residual(ch, par)

            products3(0, 0)
            stage3(0, 0, first=True)
            stage3(1, 1)
            with dve.Fori(1, CHUNKS // 2) as it:
                stage3(it * 2, 0)
                stage3(it * 2 + 1, 1)
            stage3(CHUNKS - 1, 0, final=True)
            normalise(CHUNKS - 1, 0)

        @block.sync
        def _(sp):
            def chunk_in(ch):
                after(sp, s_x_turned, ch, CB, 0)
                hold(sp)
                last = known(ch) and ch == CHUNKS - 1
                rest = N - (CHUNKS - 1) * CN - (CB - 1) * P if last else P
                xi = x_in.rearrange("p (c d) -> p c d", c=CB)
                sp.dma_start(xi[:, 0:CB - 1, :],
                             x[bass.ds(ch * CN, (CB - 1) * P), :].rearrange("(c p) d -> p c d", p=P))\
                    .then_inc(s_x_loaded, 16)
                sp.dma_start(xi[0:rest, CB - 1, :], x[bass.ds(ch * CN + (CB - 1) * P, rest), :])\
                    .then_inc(s_x_loaded, 16)
                if known(ch) and ch == 0:
                    sp.wait_ge(s_setup, mark["comp_zero"])
                after(sp, s_types, ch, 1, 0)
                hold(sp)
                many = N - (CHUNKS - 1) * CN if last else CN
                for k in range(3):
                    sp.dma_start(ntype[32 * k:32 * k + T, 0:many],
                                 node_type[bass.ds(ch * CN, many)].rearrange("(a n) -> a n", a=1)
                                 .broadcast_to([T, many])).then_inc(s_node_types_loaded, 16)

            def chunk_out(ch):
                for blk in range(CB):
                    sp.wait_ge(s_table_keys, (ch * CB + blk) * 2 + 2)
                    sp.wait_ge(s_table_values, (ch * CB + blk) * 2 + 2)
                    hold(sp)
                    sp.dma_start(table[bass.ds((ch * CB + blk) * P * T, P * T), :]
                                 .rearrange("(p t) f -> p t f", t=T),
                                 stage[:, blk % 2, :, :]).then_inc(s_table_stored[blk % 2], 16)

            chunk_in(0)
            for b, w in ((Bk, basis_k), (Bv, basis_v)):
                sp.dma_start(b[:, :, :], w.rearrange("b (i o) -> i b o", o=D)).then_inc(s_bases_loaded, 16)
            chunk_in(1)
            chunk_out(0)
            with sp.Fori(1, CHUNKS - 2) as ch:
                chunk_in(ch + 1)
                chunk_out(ch)
            chunk_in(CHUNKS - 1)
            chunk_out(CHUNKS - 2)
            sp.wait_ge(s_stage0, STAGE0)
            sp.dma_start(Bq.rearrange("p (b d) -> p b d", b=NB), basis_q.rearrange("b (i o) -> i b o", o=D))\
                .then_inc(s_q_bases, 16)

            def x_again(ch):
                after(sp, s_x_again_turned, ch, CB, 0)
                hold(sp)
                rest = N - (CHUNKS - 1) * CN - (CB - 1) * P if known(ch) and ch == CHUNKS - 1 else P
                xi = x_q.rearrange("p (c d) -> p c d", c=CB)
                sp.dma_start(xi[:, 0:CB - 1, :],
                             x[bass.ds(ch * CN, (CB - 1) * P), :].rearrange("(c p) d -> p c d", p=P))\
                    .then_inc(s_x_again, 16)
                sp.dma_start(xi[0:rest, CB - 1, :], x[bass.ds(ch * CN + (CB - 1) * P, rest), :])\
                    .then_inc(s_x_again, 16)

            x_again(0)

            sp.wait_ge(s_items_copied, 2 * IPR)

            def group(g, par):
                after(sp, s_scores, g - 2, NBATCH, NBATCH)
                hold(sp)
                sp.dma_start(idx_now[par][:, :], rows_idx[:, bass.ds(g * G, G)]).then_inc(s_indices[par], 16)
                after(sp, s_maxima, g - 2, MX, MX_TOP)
                hold(sp)
                seg3 = seg[:, par * (IH * P + 1):par * (IH * P + 1) + IH * P]\
                    .rearrange("p (i e) -> p i e", i=IH)
                rows = item_bias[bass.ds(g * G, G), :].rearrange("(i l) e -> l i e", l=IL)
                for h in range(H):
                    sp.dma_start(seg3[h * IL:(h + 1) * IL, :, :], rows).then_inc(s_segments[par], 16)

            group(0, 0)
            group(1, 1)
            chunk_out(CHUNKS - 1)
            with sp.Fori(1, CHUNKS - 1) as ch:
                x_again(ch)
            x_again(CHUNKS - 1)

            with sp.Fori(1, GROUPS // 2) as it:
                group(it * 2, 0)
                group(it * 2 + 1, 1)

            sp.wait_ge(s_weighted, (GROUPS - 1) * NBATCH)
            whole = BLOCKS - 1
            rest = N - whole * P

            def load(ch, par):
                after(sp, s_residual, ch - 1, 2, 0)
                hold(sp)
                last = known(ch) and ch == CHUNKS - 1
                n = CB - 1 if last else CB
                xc = x3[par].rearrange("p (c d) -> p c d", c=CB)
                sp.dma_start(xc[:, 0:n, :],
                             x[bass.ds(ch * CN, n * P), :].rearrange("(c p) d -> p c d", p=P))\
                    .then_inc(s_x3_loaded[par], 16)
                if last:
                    sp.dma_start(xc[0:rest, n, :], x[whole * P:N, :]).then_inc(s_x3_loaded[par], 16)

            def store(ch):
                sp.wait_ge(s_normalised, ch * CB + CB)
                hold(sp)
                last = known(ch) and ch == CHUNKS - 1
                n = CB - 1 if last else CB
                oc = yo.rearrange("p (c d) -> p c d", c=CB)
                sp.dma_start(out[bass.ds(ch * CN, n * P), :].rearrange("(c p) d -> p c d", p=P),
                             oc[:, 0:n, :]).then_inc(s_stored, 16)
                if last:
                    sp.dma_start(out[whole * P:N, :], oc[0:rest, n, :]).then_inc(s_stored, 16)

            assert CHUNKS % 2 == 1
            load(0, 0)
            load(1, 1)
            with sp.Fori(0, CHUNKS // 2 - 1) as it:
                load(it * 2 + 2, 0)
                store(it * 2)
                load(it * 2 + 3, 1)
                store(it * 2 + 1)
            load(CHUNKS - 1, 0)
            for ch in range(CHUNKS - 3, CHUNKS):
                store(ch)
            sp.wait_ge(s_stored, 16 * (CHUNKS + 1))

        @block.gpsimd
        def _(pool):
            g_ = nc.gpsimd
            g_.memset(ident[:, :], 0.0).then_inc(s_const, 1)
            g_.memset(ones[:, :], 1.0).then_inc(s_const, 1)
            g_.iota(lane[:, :], [[1, P]], base=0, channel_multiplier=0,
                    allow_small_or_imprecise_dtypes=True).then_inc(s_const, 1)
            g_.iota(item_no[:, :], [[1, IPR]], base=0, channel_multiplier=IPR,
                    allow_small_or_imprecise_dtypes=True).then_inc(s_const, 1)
            for k in range(3):
                pool.wait_ge(s_const, 4 + k)
                g_.iota(type_no[32 * k:32 * k + 32, :], [[0, 1]], base=0, channel_multiplier=1,
                        allow_small_or_imprecise_dtypes=True).then_inc(s_const, 1)
            pool.wait_ge(s_const, 7)
            g_.affine_select(out=ident[:, :], in_=ident[:, :], compare_op=ALU.not_equal, fill=1.0,
                             base=0, pattern=[[-1, P]], channel_multiplier=1).then_inc(s_const, 1)

            def tile_load(k, a):
                pool.dma_start(tile_rows[0:FULL, k * P:(k + 1) * P],
                               a[0:FULL * P].rearrange("(t e) -> t e", e=P)).then_inc(s_tile_rows, 16)
                pool.dma_start(tile_rows[FULL:FULL + 1, k * P:k * P + REST],
                               a[FULL * P:].rearrange("(t e) -> t e", t=1)).then_inc(s_tile_rows, 16)

            tile_load(0, dst)
            tile_load(1, src)
            tile_load(2, edge_type)
            pool.wait_ge(s_setup, mark["pad"])
            p3 = pad_rows.rearrange("p (k e) -> p k e", k=3)
            r3 = tile_rows.rearrange("t (k e) -> t k e", k=3)
            pool.dma_start(r3[FULL:FULL + 1, :, REST:P], p3[0:1, :, REST:P]).then_inc(s_tile_rows, 16)
            pool.dma_start(r3[FULL + 1:TILES, :, :], p3[1:PADT, :, :]).then_inc(s_tile_rows, 16)
            n = [0]

            def did(ins):
                n[0] += 1
                ins.then_inc(s_chain, 1)
                pool.wait_ge(s_chain, n[0])

            pool.wait_ge(s_tile_rows, 16 * 8)
            pool.dma_start(tdst, tile_rows.rearrange("(p c) f -> p c f", c=TPR)[:, :, 0:P])\
                .then_inc(s_tile_dst, 16)
            pool.dma_start(Ba[:, :, :], basis_a.rearrange("b (i o) -> i b o", o=D)).then_inc(s_last_weights_loaded, 16)
            pool.dma_start(Wl[:, :], loop_w).then_inc(s_last_weights_loaded, 16)
            for k in range(3):
                pool.dma_start(bias_in[32 * k:32 * k + 1, :], bias.rearrange("(a d) -> a d", a=1))\
                    .then_inc(s_last_weights_loaded, 16)
            pool.wait_ge(s_setup, mark["tiles"])
            pool.dma_start(tile_blocks.rearrange("k (p c) -> p k c", c=TPR), fc[0:TROWS, 0:2, :])\
                .then_inc(s_tile_blocks_out, 16)
            pool.wait_ge(s_tile_blocks_out, 16)
            pool.dma_start(tfl, tile_blocks.rearrange("(a k) t -> a (k t)", a=1).broadcast_to([P, 2 * TILES]))\
                .then_inc(s_tile_blocks_in, 16)
            pool.wait_ge(s_scan, 1)
            tb, tn = tfl[:, 0:TILES], tfl[:, TILES:2 * TILES]
            did(g_.tensor_tensor(tstart, tcmp, tn, ALU.subtract))
            did(g_.tensor_tensor(tcmp, tb, tstart, ALU.subtract))
            did(g_.tensor_copy(tgap[:, 0:1], tcmp[:, 0:1]))
            did(g_.tensor_tensor(tgap[:, 1:TILES], tcmp[:, 1:TILES], tcmp[:, 0:TILES - 1], ALU.subtract))
            for k in range(IPR):
                pair = pairs[k % 2]
                if k >= 2:
                    pool.wait_ge(s_column, k - 1)
                did(g_.tensor_scalar(pair[:, 0:TILES], tstart, item_no[:, k:k + 1], None, ALU.is_le))
                g_.tensor_tensor(pair[:, TILES:2 * TILES], pair[:, 0:TILES], tgap, ALU.mult)\
                    .then_inc(s_pair_made, 1)
            pool.wait_ge(s_setup, mark["item_tile"])
            for k in range(IPR):
                pool.indirect_dma_start(
                    out=irow[:, k, :], out_offset=None, in_=tile_rows,
                    in_offset=bass.IndirectOffsetOnAxis(ap=ic[:, 0, k:k + 1], axis=0)).then_inc(s_item_rows, 16)
            pool.wait_ge(s_setup, mark["item_block"])
            pool.dma_start(item_block.rearrange("a (p c) -> (a p) c", c=IPR), ic[:, 1, :]).then_inc(s_item_blocks, 16)
            pool.wait_ge(s_item_blocks, 16)
            pool.dma_start(iblk[:, :], item_block).then_inc(s_item_blocks, 16)
            pool.wait_ge(s_item_rows, 16 * IPR)
            did(g_.tensor_copy(lanes, irows[:, :, 0, :]))
            did(g_.tensor_copy(fc[:, 3, :], lanes[:, :, 0]))
            did(g_.tensor_copy(fc[:, 4, :], lanes[:, :, P - 1]))
            kd = item_keys.rearrange("k (p c) -> p k c", c=IPR)
            pool.dma_start(kd[:, 0:1, :], fc[:, 0:1, :]).then_inc(s_item_keys, 16)
            pool.dma_start(kd[:, 1:3, :], fc[:, 3:5, :]).then_inc(s_item_keys, 16)
            did(g_.tensor_tensor(biasr[:, :, 1:P], lanes[:, :, 1:P], lanes[:, :, 0:P - 1], ALU.subtract))
            did(g_.memset(biasr[:, :, 0:1], 1.0))
            did(g_.tensor_scalar(biasr, biasr, 0.0, -BIG, ALU.is_gt, ALU.mult))
            pool.dma_start(item_bias.rearrange("(p c) e -> p c e", c=IPR), biasr).then_inc(s_item_starts, 16)
            for k in range(IPR):
                did(g_.tensor_scalar(lanes[:, k, :], lanes[:, k, :], -1.0, fc[:, 5, k:k + 1],
                                     ALU.mult, ALU.add))
            did(g_.tensor_copy(srcf, irows[:, :, 1, :]))
            did(g_.tensor_copy(etf, irows[:, :, 2, :]))
            did(g_.tensor_scalar(srcf, srcf, float(T), None, ALU.mult))
            g_.tensor_tensor(srcf, srcf, etf, ALU.add).then_inc(s_lanes_rows, 1)
            pool.wait_ge(s_item_keys, 32)
            pool.dma_start(krow, item_keys.rearrange("(a k) i -> a k i", a=1)).then_inc(s_item_keys, 16)
            pool.wait_ge(s_item_keys, 48)
            last = ITEMS - 1
            it_, if_, il_ = krow[:, 0, :], krow[:, 1, :], krow[:, 2, :]
            did(g_.memset(carries[:, 0:1], 0.0))
            did(g_.tensor_tensor(carries[:, 1:], it_[:, 1:], it_[:, 0:last], ALU.subtract))
            did(g_.tensor_scalar(carries[:, 1:], carries[:, 1:], 1.0, None, ALU.is_equal))
            did(g_.tensor_tensor(it_[:, 1:], if_[:, 1:], il_[:, 0:last], ALU.subtract))
            did(g_.tensor_scalar(it_[:, 1:], it_[:, 1:], 0.0, None, ALU.is_equal))
            did(g_.tensor_tensor(carries[:, 1:], carries[:, 1:], it_[:, 1:], ALU.mult))
            did(g_.tensor_tensor(it_, if_, il_, ALU.subtract))
            did(g_.tensor_scalar(it_, it_, 0.0, None, ALU.is_equal))
            did(g_.tensor_tensor(if_, it_, carries[:, :], ALU.mult))
            did(g_.memset(il_[:, last:], 0.0))
            did(g_.tensor_tensor(il_[:, 0:last], it_[:, 0:last], carries[:, 1:], ALU.mult))
            for k, a in enumerate((if_, carries[:, :], il_)):
                did(g_.tensor_scalar(car[:, k, :], a, -1.0, BIG, ALU.add, ALU.mult))
            g_.memset(end_run[:, :], 0.0).then_inc(s_stage0, 1)
            g_.memset(run_top[:, :], 0.0).then_inc(s_stage0, 1)
            for r in range(2):
                g_.memset(seg[:, (r + 1) * (IH * P + 1) - 1:(r + 1) * (IH * P + 1)], -BIG)\
                    .then_inc(s_stage0, 1)
            pool.wait_ge(s_items_turned, 2 * IPR)
            g_.memset(agg[:, :], 0.0).then_inc(s_stage0, 1)

            for r in range(2):
                pool.wait_ge(s_table_stored[r], 16 * RING[r] * CHUNKS)

            def gather(g, par, use):
                after(pool, s_indices[par], use, 16, 16)
                for b in range(NBATCH):
                    after(pool, s_weighted, g - 2, NBATCH, b + 1)
                    hold(pool)
                    for u in range(4):
                        i = b * 4 + u
                        o = (par * G + i) * 2 * D
                        pool.indirect_dma_start(
                            out=kv[:, o:o + 2 * D], out_offset=None, in_=table,
                            in_offset=bass.IndirectOffsetOnAxis(ap=idx_now[par][:, i:i + 1], axis=0))\
                            .then_inc(s_gathered[par][b], 16)

            gather(0, 0, 0)
            gather(1, 1, 0)
            with pool.Fori(1, GROUPS // 2) as it:
                gather(it * 2, 0, it)
                gather(it * 2 + 1, 1, it)

            def products3(ch, par):
                pool.wait_ge(s_factors, ch * V3 + V3)
                after(pool, s_products_turned, ch - 1, CB, 0)
                hold(pool)
                ag = agg[:, bass.ds(ch * (CB * W), CB * W)].rearrange("p (c w) -> p c w", c=CB)
                for b in range(2, NB):
                    g_.tensor_tensor(anb[par][:, b, :].rearrange("p (c h k) -> p c h k", c=CB, h=H),
                                     ag[:, :, 0:D].rearrange("p c (h k) -> p c h k", h=H),
                                     factor[par][:, b].unsqueeze(3).broadcast_to([P, CB, H, DK]),
                                     ALU.mult).then_inc(s_products_pool, 1)

            products3(0, 0)
            products3(1, 1)
            with pool.Fori(1, CHUNKS // 2) as it:
                products3(it * 2, 0)
                products3(it * 2 + 1, 1)
            products3(CHUNKS - 1, 0)

        @block.scalar
        def _(act):
            a_ = nc.scalar
            act.wait_ge(s_setup, 1)
            for k in range(3):
                for j, w in enumerate((comp_k, comp_v, comp_a, comp_q)):
                    act.dma_start(comp[32 * k:32 * k + T, j * NB:(j + 1) * NB], w).then_inc(s_comp_loaded, 16)
            def copy_x(ch):
                for u, (c0, c1) in enumerate(((0, 4), (4, CB))):
                    act.wait_ge(s_x_turned, ch * CB + c1)
                    if u == 0:
                        after(act, s_scaled, ch, CO, 0)
                    a_.activation(xT[:, c0 * P:c1 * P], PB[2 + u][:, 0:(c1 - c0) * P], ACT.Copy)\
                        .then_inc(s_xT_copied, 1)

            def stage1(ch, final=False):
                act.wait_ge(s_projected, ch * PJ + 1)
                hold(act)
                both = PB[2][:, 0:CB * 2 * NB].rearrange("p (c k b) -> p c k b", c=CB, k=2)
                for k, o in enumerate((ca, coef_q)):
                    cp = a_.activation(o[:, bass.ds(ch * (CB * NB), CB * NB)].rearrange("p (c b) -> p c b", b=NB),
                                       both[:, :, k, :], ACT.Copy)
                cp.then_inc(s_projection_copied, 1)
                for o in range(4):
                    kind, h = o // 2, o % 2
                    act.wait_ge(s_projected, ch * PJ + o + 2)
                    if o == 0:
                        after(act, s_table_product, ch, CB * 4, 0)
                    a_.activation(kvT[:, kind, h * HALF:(h + 1) * HALF], PB[2 + (o + 1) % 2][:, 0:HALF],
                                  ACT.Copy).then_inc(s_projection_copied, 1)
                for blk in range(CB):
                    for u in range(2):
                        act.wait_ge(s_table_product, (ch * CB + blk) * 4 + u + 1)
                        if u == 0:
                            after(act, s_table_stored[blk % 2], ch, 16 * RING[blk % 2], 16 * (blk // 2))
                        a_.activation(stage[:, blk % 2, 4 * u:4 * u + 4, 0:D],
                                      PB[4 + u][:, :].rearrange("p (t d) -> p t d", t=4), ACT.Copy)\
                            .then_inc(s_table_keys, 1)
                    if blk == 0 and not final:
                        copy_x(ch + 1)

            copy_x(0)
            act.wait_ge(s_setup, mark["rel_zero"])
            for h in range(H):
                r = slice(h * DK, (h + 1) * DK)
                for m, w in ((att, rel_att), (msg, rel_msg)):
                    act.dma_start(m.rearrange("p (t d) -> p t d", t=T)[r, :, r],
                                  w[:, h, :, :].rearrange("t i j -> i t j")).then_inc(s_relations_loaded, 16)
                with nc.allow_non_contiguous_dma(reason="64 priorities"):
                    act.dma_start(pri[r, :], rel_pri[:, h:h + 1].rearrange("t a -> a t").broadcast_to([DK, T]))\
                        .then_inc(s_relations_loaded, 16)
            stage1(0)
            with act.Fori(1, CHUNKS - 1) as ch:
                stage1(ch)
            stage1(CHUNKS - 1, final=True)

            def copy_again(ch, u):
                c0, c1 = 4 * u, min(4 * u + 4, CB)
                act.wait_ge(s_x_again_turned, ch * CB + c1)
                after(act, s_q_product, ch - 1, CB, c1)
                a_.activation(xTq[:, c0 * P:c1 * P], PB[2][:, 0:(c1 - c0) * P], ACT.Copy)\
                    .then_inc(s_x_again_copied, 1)

            def query_first(ch, final=False):
                for c in range(CB):
                    act.wait_ge(s_q_product, ch * CB + c + 1)
                    hold(act)
                    a_.activation(q_all[:, bass.ds((ch * CB + c) * D, D)], PB[QBANK[c]][:, 0:D], ACT.Copy,
                                  scale=coef_q[:, bass.ds((ch * CB + c) * NB, 1)]).then_inc(s_q_first, 1)
                    if not final and c in (3, CB - 1):
                        copy_again(ch + 1, c // 4)

            def first_hot(b):
                after(act, s_one_hot, b, 1, 0)
                hold(act)
                for u in range(4):
                    a_.activation(sq[:, u, :], lane[:, :], ACT.Square,
                                  bias=neg_lane[:, bass.ds(b * 4 + u, 1)]).then_inc(s_squares, 1)
                act.wait_ge(s_squares, b * 4 + 4)
                hold(act)
                a_.activation(onehot[:, bass.ds(b * (4 * P), 4 * P)], sq[:, :, :].rearrange("p u e -> p (u e)"),
                              ACT.Relu, bias=1.0, scale=-1.0).then_inc(s_one_hot, 1)

            assert CHUNKS <= NBATCH
            act.wait_ge(s_table_product, CHUNKS * CB * 4)
            act.wait_ge(s_items_copied, 2 * IPR)
            act.wait_ge(s_stage0, STAGE0)
            act.wait_ge(s_projection_copied, CHUNKS * PJ)
            copy_again(0, 0)
            copy_again(0, 1)
            query_first(0)
            first_hot(0)
            with act.Fori(1, CHUNKS - 1) as ch:
                query_first(ch)
                first_hot(ch)
            query_first(CHUNKS - 1, final=True)
            for b in range(CHUNKS - 1, NBATCH):
                first_hot(b)

            def one_hot(g, par, b):
                after(act, s_one_hot, g, NBATCH, b)
                hold(act)
                for u in range(4):
                    a_.activation(sq[:, u, :], lane[:, :], ACT.Square,
                                  bias=neg_lane[:, bass.ds(g * G + b * 4 + u, 1)]).then_inc(s_squares, 1)
                act.wait_ge(s_squares, g * G + b * 4 + 4)
                after(act, s_item_sums, g - 2, 2 * NBATCH, 2 * b + 2)
                o = (par * G + b * 4) * P
                a_.activation(onehot[:, o:o + 4 * P], sq[:, :, :].rearrange("p u e -> p (u e)"), ACT.Relu,
                              bias=1.0, scale=-1.0).then_inc(s_one_hot, 1)

            def evacuate(g, b):
                act.wait_ge(s_one_hot_turned, g * NBATCH + b + 1)
                after(act, s_edge_queries, g, NBATCH, b - 1)
                a_.activation(spread[:, b % 2, :, :].rearrange("p u e -> p (u e)"), PB[b % 2][:, :], ACT.Copy)\
                    .then_inc(s_spread_copied, 1)

            def carry_terms(g):
                after(act, s_maxima, g - 1, MX, MX_CARRY)
                hold(act)
                for k in range(3):
                    a_.activation(rows8[:, k * H * G:(k + 1) * H * G].rearrange("p (h i) -> p h i", h=H),
                                  car[:, k, bass.ds(g * G, G)].unsqueeze(1).broadcast_to([1, H, G]),
                                  ACT.Copy).then_inc(s_carry_terms, 1)

            def exponentials(g, b):
                if b == 0:
                    act.wait_ge(s_maxima, g * MX + MX_DIFF)
                after(act, s_item_sums, g, 2 * NBATCH, 2 * (b - WR) + 2)
                o = b // (IL // 4) * H * IL
                l0 = b % (IL // 4) * 4
                d = diff[:, o:o + H * IL].rearrange("p (h l) -> p l h", h=H)[:, l0:l0 + 4, :]
                a_.activation(wv[:, b % WR, :, D:W], d, ACT.Exp).then_inc(s_weights, 1)

            def rise_exp(g):
                act.wait_ge(s_rise_placed, g + 1)
                after(act, s_rescaled, g, 2, 0)
                a_.activation(rise[:, :], PB[7][:, 8:8 + H], ACT.Exp).then_inc(s_rise, 1)

            def group(g, par, prev, final=False):
                for s in range(NBATCH):
                    if prev and s == 0:
                        carry_terms(g - 1)
                    if prev and s == 2:
                        exponentials(g - 1, 0)
                        exponentials(g - 1, 1)
                        rise_exp(g - 1)
                    elif prev:
                        for b in WEIGHS[s]:
                            exponentials(g - 1, b)
                    if s + 2 < NBATCH:
                        evacuate(g, s + 2)
                    elif not final:
                        evacuate(g + 1, s + 2 - NBATCH)
                    if s + 3 < NBATCH:
                        if not (known(g) and g == 0):
                            one_hot(g, par, s + 3)
                    elif not final:
                        one_hot(g + 1, 1 - par, s + 3 - NBATCH)

            act.wait_ge(s_q_terms, BLOCKS * (NB - 1))
            for b in range(2):
                evacuate(0, b)
            group(0, 0, False)
            group(1, 1, True)
            with act.Fori(1, GROUPS // 2 - 1) as it:
                group(it * 2, 0, True)
                group(it * 2 + 1, 1, True)
            group(GROUPS - 2, 0, True)
            group(GROUPS - 1, 1, True, final=True)
            carry_terms(GROUPS - 1)
            def copy_x3(ch, par):
                for u, (c0, c1) in enumerate(((0, 4), (4, CB))):
                    act.wait_ge(s_x3_turned, ch * CB + c1)
                    after(act, s_layer_out, ch - 1, 2, 0)
                    a_.activation(xT3[par][:, c0 * P:c1 * P], PB[2 + u][:, 0:(c1 - c0) * P], ACT.Copy)\
                        .then_inc(s_xT3_copied, 1)

            exponentials(GROUPS - 1, 0)
            exponentials(GROUPS - 1, 1)
            rise_exp(GROUPS - 1)
            copy_x3(0, 0)
            for b in range(2, NBATCH):
                exponentials(GROUPS - 1, b)

            def copy_products(ch, par, c):
                act.wait_ge(s_products_turned, ch * CB + c + 1)
                after(act, s_block_multiplied, ch, CB, c - 1)
                k = (par * CB + c) % 2
                a_.activation(anT[:, k, :, :].rearrange("p b n -> p (b n)"), PB[k][:, :], ACT.Copy)\
                    .then_inc(s_products_copied, 1)

            def deviation(ch):
                act.wait_ge(s_mean_var, ch * CB + CB)
                a_.activation(rstd, mv[:, :, 1], ACT.Sqrt, bias=eps[:, 0:1]).then_inc(s_deviation, 1)

            def stage3(ch, par, first=False, final=False):
                for c in range(1, CB):
                    copy_products(ch, par, c)
                    if c == 3 and not first:
                        deviation(ch - 1)
                    if c == XAT + 1 and not final:
                        copy_x3(ch + 1, 1 - par)
                if not final:
                    copy_products(ch + 1, 1 - par, 0)

            copy_products(0, 0, 0)
            stage3(0, 0, first=True)
            stage3(1, 1)
            with act.Fori(1, CHUNKS // 2) as it:
                stage3(it * 2, 0)
                stage3(it * 2 + 1, 1)
            stage3(CHUNKS - 1, 0, final=True)
            deviation(CHUNKS - 1)

        @block.tensor
        def _(pe):
            t_ = nc.tensor

            def turn_x(ch):
                pe.wait_ge(s_x_loaded, (ch + 1) * 32)
                after(pe, s_projection_copied, ch, PJ, 0)
                for c in range(CB):
                    t_.transpose(PB[2 + c // 4][:, c % 4 * P:(c % 4 + 1) * P], x_in[:, c * D:(c + 1) * D],
                                 ident[:, :]).then_inc(s_x_turned, 1)

            def coefficient(ch, j):
                kind, h, b = j // (2 * NB), j // NB % 2, j % NB
                if j == 0:
                    pe.wait_ge(s_types, ch + 1)
                after(pe, s_scaled, ch, CO, j - 1)
                t_.matmul(PB[j % 2][:, 0:HALF], comp_w[:, kind * NB + b, :],
                          is_type[:, h * HALF:(h + 1) * HALF], start=True, stop=True).then_inc(s_coef_spread, 1)

            def place(ch, o):
                if o < 2:
                    pe.wait_ge(s_xT_copied, ch * 2 + 2)
                else:
                    pe.wait_ge(s_projection_copied, ch * PJ + o - 1)
                return PB[2 + o % 2]

            def projections(ch):
                pe.wait_ge(s_scaled, ch * CO + CO)
                bank = place(ch, 0)
                for c in range(CB):
                    mm = t_.matmul(bank[:, c * 2 * NB:(c + 1) * 2 * NB], is_type[:, c * P:(c + 1) * P],
                                   comp_s[:, 2 * NB:4 * NB], start=True, stop=True)
                mm.then_inc(s_projected, 1)
                for kind, B in enumerate((Bk, Bv)):
                    for h in range(2):
                        bank = place(ch, 1 + kind * 2 + h)
                        for b in range(NB):
                            mm = t_.matmul(bank[:, 0:HALF], B[:, b, :],
                                           scaled[:, kind, b, h * HALF:(h + 1) * HALF],
                                           start=(b == 0), stop=(b == NB - 1))
                        mm.then_inc(s_projected, 1)

            def table(ch, final=False):
                n = 0
                for blk in range(CB):
                    for j in range(4):
                        kind, h = j // 2, j % 2
                        if blk == 0 and h == 0:
                            pe.wait_ge(s_projection_copied, ch * PJ + 2 * kind + 3)
                        after(pe, (s_table_keys, s_table_values)[kind], ch, 2 * CB, 2 * blk + h - 1)
                        t_.matmul(PB[4 + j][:, :], kvT[:, kind, blk * P:(blk + 1) * P],
                                  (att, msg)[kind][:, h * 512:(h + 1) * 512], start=True, stop=True)\
                            .then_inc(s_table_product, 1)
                        if not final and 1 <= j <= AHEAD[blk]:
                            coefficient(ch + 1, n)
                            n += 1
                    if blk == 0 and not final:
                        turn_x(ch + 1)

            pe.wait_ge(s_const, 8)
            turn_x(0)
            pe.wait_ge(s_setup, mark["comp"])
            for j in range(CO):
                coefficient(0, j)
            pe.wait_ge(s_bases_loaded, 16 * 2)
            projections(0)
            pe.wait_ge(s_setup, mark["att"])
            table(0)
            projections(1)
            table(1)
            pe.wait_ge(s_lanes_rows, 1)
            pe.wait_ge(s_table_keys, 2 * 2 * CB)
            pe.wait_ge(s_table_values, 2 * 2 * CB)
            for a, (rows, bank) in enumerate(((lanes, 4), (srcf, 6))):
                for k in range(IPR):
                    t_.transpose(PB[bank + k // 4][:, k % 4 * P:(k % 4 + 1) * P], rows[:, k, :],
                                 ident[:, :]).then_inc(s_items_turned, 1)
            projections(2)
            pe.wait_ge(s_items_copied, 2 * IPR)
            table(2)
            with pe.Fori(3, CHUNKS - 1) as ch:
                projections(ch)
                table(ch)
            projections(CHUNKS - 1)
            table(CHUNKS - 1, final=True)

            def turn_again(ch, u):
                pe.wait_ge(s_x_again, (ch + 1) * 32)
                after(pe, s_x_again_copied, ch, 2, u)
                for c in range(4 * u, min(4 * u + 4, CB)):
                    t_.transpose(PB[2][:, c % 4 * P:(c % 4 + 1) * P], x_q[:, c * D:(c + 1) * D],
                                 ident[:, :]).then_inc(s_x_again_turned, 1)

            def query_products(ch, final=False):
                for c in range(CB):
                    if c % 4 == 0:
                        pe.wait_ge(s_x_again_copied, ch * 2 + c // 4 + 1)
                    done = min(c1 for _, c1 in QGROUPS if c1 > c)
                    after(pe, s_q_terms, ch - 1, CB * (NB - 1), done * (NB - 1))
                    t_.matmul(PB[QBANK[c]][:, :], xTq[:, c * P:(c + 1) * P], Bq, start=True, stop=True)\
                        .then_inc(s_q_product, 1)
                    if not final and c in (3, CB - 1):
                        turn_again(ch + 1, c // 4)

            pe.wait_ge(s_projection_copied, CHUNKS * PJ)
            pe.wait_ge(s_table_keys, CHUNKS * 2 * CB)
            pe.wait_ge(s_table_values, CHUNKS * 2 * CB)
            pe.wait_ge(s_q_bases, 16)
            turn_again(0, 0)
            turn_again(0, 1)
            query_products(0)
            with pe.Fori(1, CHUNKS - 1) as ch:
                query_products(ch)
            query_products(CHUNKS - 1, final=True)

            pe.wait_ge(s_q_terms, BLOCKS * (NB - 1))
            pe.wait_ge(s_item_blocks, 32)
            L = IH * P
            HG = H * G

            def turn(g, par, b):
                pe.wait_ge(s_one_hot, g * NBATCH + b + 1)
                after(pe, s_spread_copied, g, NBATCH, b - 1)
                for u in range(4):
                    o = (par * G + b * 4 + u) * P
                    mm = t_.transpose(PB[b % 2][:, u * P:(u + 1) * P], onehot[:, o:o + P], ident[:, :])
                mm.then_inc(s_one_hot_turned, 1)

            def queries(g, b):
                blks = nc.values_load_multi_w_load_instructions(
                    iblk[0:1, bass.ds(g * G + b * 4, 4)], engines=(pe.engine,), min_val=0,
                    max_val=BLOCKS - 1, skip_runtime_bounds_check_because="clamped when written")[1]
                pe.wait_ge(s_spread_copied, g * NBATCH + b + 1)
                after(pe, s_products, g, NBATCH, b - 1)
                for u in range(4):
                    mm = t_.matmul(PB[2 + b % 2][:, u * D:(u + 1) * D], spread[:, b % 2, u, :],
                                   q_all[:, bass.ds(blks[u] * D, D)], start=True, stop=True)
                mm.then_inc(s_edge_queries, 1)

            def turn_scores(g, par):
                pe.wait_ge(s_scores, g * NBATCH + NBATCH)
                for i in range(IH):
                    mm = t_.transpose(PB[6][:, i * P:(i + 1) * P], score[:, par, i * P:(i + 1) * P], ident[:, :])
                mm.then_inc(s_scores_turned, 1)

            def turn_ends(g):
                pe.wait_ge(s_maxima, g * MX + MX_SCAN)
                after(pe, s_rise, g, 1, 0)
                for k, (scan, e) in enumerate(((fwd, P - 1), (bwd, 0))):
                    for i in range(IH):
                        dest = PB[7][0:1, k * HG:(k + 1) * HG].rearrange("p (h j) -> p h j", h=H)
                        mm = t_.transpose(dest[:, :, i * IL:(i + 1) * IL], scan[:, i * P + e:i * P + e + 1],
                                          ident[:, :])
                mm.then_inc(s_ends_turned, 1)

            def turn_carried(g):
                pe.wait_ge(s_maxima, g * MX + MX_CARRY)
                for k in range(2):
                    for i in range(IH):
                        o = (k * IH + i) * P
                        mm = t_.matmul(PB[7][:, k * IH + i:k * IH + i + 1], end_out[:, o:o + P],
                                       ones[0:1, 0:1], start=True, stop=True)
                mm.then_inc(s_carried_turned, 1)

            def turn_tops(g):
                pe.wait_ge(s_maxima, g * MX + MX_TOP)
                for i in range(IH):
                    mm = t_.transpose(PB[6][:, L + i * P:L + (i + 1) * P], bwd[:, i * P:(i + 1) * P],
                                      ident[:, :])
                mm.then_inc(s_tops_turned, 1)

            def place_rise(g, par):
                pe.wait_ge(s_maxima, g * MX + MX)
                t_.matmul(PB[7][:, 8:8 + H], onehot[0:1, par * G * P:par * G * P + P],
                          run_top[:, 2 * H:3 * H], start=True, stop=True).then_inc(s_rise_placed, 1)

            def sums(g, par, k, banks=SBANKS):
                b, h = k // 2, k % 2
                pe.wait_ge(s_weighted, g * NBATCH + b + 1)
                after(pe, s_added, g, G, 2 * (k - len(banks)) + 2)
                for u in range(2):
                    o = (par * G + 2 * k + u) * P
                    mm = t_.matmul(PB[banks[k % len(banks)]][:, u * 256:u * 256 + W], onehot[:, o:o + P],
                                   wv[:, b % WR, h * 2 + u, :], start=True, stop=True)
                mm.then_inc(s_item_sums, 1)

            def group(g, par, prev, final=False):
                gp, p = g - 1, 1 - par
                for s in range(NBATCH):
                    if prev and s == 2:
                        place_rise(gp, p)
                    if s + 2 < NBATCH:
                        turn(g, par, s + 2)
                    elif not final:
                        turn(g + 1, p, s + 2 - NBATCH)
                    if prev and s == 0:
                        turn_scores(gp, p)
                    if prev and s == 1:
                        turn_carried(gp)
                    if s < 2:
                        halves = SUMS[s] if prev == 2 else []
                        whose = (g - 2, par)
                    else:
                        halves = SUMS[s] if prev else []
                        whose = (gp, p)
                    for k in halves[0:1]:
                        sums(*whose, k)
                    if s + 1 < NBATCH:
                        queries(g, s + 1)
                    elif not final:
                        queries(g + 1, 0)
                    if prev and s == 0:
                        turn_ends(gp)
                    if prev and s == 1:
                        turn_tops(gp)
                    for k in halves[1:]:
                        sums(*whose, k)

            turn(0, 0, 0)
            turn(0, 0, 1)
            queries(0, 0)
            def turn_x3(ch, par, use):
                last = known(ch) and ch == CHUNKS - 1
                pe.wait_ge(s_x3_loaded[par], (use + (2 if last else 1)) * 16)
                after(pe, s_xT3_copied, ch, 2, 0)
                for c in range(CB):
                    t_.transpose(PB[2 + c // 4][:, c % 4 * P:(c % 4 + 1) * P],
                                 x3[par][:, c * D:(c + 1) * D], ident[:, :]).then_inc(s_x3_turned, 1)

            group(0, 0, 0)
            group(1, 1, 1)
            with pe.Fori(1, GROUPS // 2 - 1) as it:
                group(it * 2, 0, 2)
                group(it * 2 + 1, 1, 2)
            group(GROUPS - 2, 0, 2)
            group(GROUPS - 1, 1, 2, final=True)
            g = GROUPS - 1
            turn_scores(g, 1)
            sums(g - 1, 0, 12)
            turn_ends(g)
            sums(g - 1, 0, 13)
            turn_carried(g)
            sums(g - 1, 0, 14)
            turn_tops(g)
            sums(g - 1, 0, 15)
            place_rise(g, 1)
            pe.wait_ge(s_products, GROUPS * NBATCH)
            turn_x3(0, 0, 0)
            for k in range(2 * NBATCH):
                sums(g, 1, k, LAST_SBANKS)

            def turn_products(ch, par, c):
                if c == 0:
                    pe.wait_ge(s_products_dve, ch * 2 + 2)
                    pe.wait_ge(s_products_pool, ch * 2 + 2)
                after(pe, s_products_copied, ch, CB, c - 1)
                for b in range(NB):
                    mm = t_.transpose(PB[(par * CB + c) % 2][:, b * P:(b + 1) * P],
                                      anb[par][:, b, c * D:(c + 1) * D], ident[:, :])
                mm.then_inc(s_products_turned, 1)

            def stage3(ch, par, use_next=None):
                for c in range(CB):
                    if c + 1 < CB:
                        turn_products(ch, par, c + 1)
                    elif use_next is not None:
                        turn_products(ch + 1, 1 - par, 0)
                    if c % 4 == 0:
                        pe.wait_ge(s_xT3_copied, ch * 2 + c // 4 + 1)
                        after(pe, s_residual, ch - 1, 2, 0)
                    pe.wait_ge(s_products_copied, ch * CB + c + 1)
                    o = PB[4 + 2 * par + c // 4][:, c % 4 * D:(c % 4 + 1) * D]
                    for b in range(NB):
                        mm = t_.matmul(o, anT[:, (par * CB + c) % 2, b, :], Ba[:, b, :],
                                       start=(b == 0), stop=False)
                    mm.then_inc(s_block_multiplied, 1)
                    t_.matmul(o, xT3[par][:, c * P:(c + 1) * P], Wl[:, :], start=False, stop=False)
                    mm = t_.matmul(o, ones3, bias3, start=False, stop=True)
                    if c in (3, CB - 1):
                        mm.then_inc(s_layer_out, 1)
                    if c == XAT and use_next is not None:
                        turn_x3(ch + 1, 1 - par, use_next)

            turn_products(0, 0, 0)
            pe.wait_ge(s_last_weights_loaded, 16 * 5)
            pe.wait_ge(s_setup, mark["bias"])
            stage3(0, 0, 0)
            stage3(1, 1, 1)
            with pe.Fori(1, CHUNKS // 2 - 1) as it:
                stage3(it * 2, 0, it)
                stage3(it * 2 + 1, 1, it + 1)
            stage3(CHUNKS - 3, 0, CHUNKS // 2 - 1)
            stage3(CHUNKS - 2, 1, CHUNKS // 2)
            stage3(CHUNKS - 1, 0)



_INS = ["x", "src", "dst", "edge_type_8", "node_type_8",
        "L0_gnn_w_comp_k", "L0_gnn_w_basis_k", "L0_gnn_w_comp_q", "L0_gnn_w_basis_q",
        "L0_gnn_w_comp_v", "L0_gnn_w_basis_v", "L0_gnn_w_comp_a", "L0_gnn_w_basis_a",
        "L0_gnn_relation_pri", "L0_gnn_relation_att", "L0_gnn_relation_msg",
        "L0_gnn_loop_weight", "L0_gnn_bias"]


def kernel(**inputs):
    import numpy as _np
    import concourse.bacc as _bacc
    from concourse import mybir as _mybir
    from concourse.bass_utils import run_bass_kernel_spmd as _run

    nc = _bacc.Bacc("TRN2", target_bir_lowering=False, num_devices=1)
    arrays, args = {}, []
    for name in _INS:
        a = _np.ascontiguousarray(inputs[name])
        arrays[f"in_{name}_dram"] = a
        args.append(nc.dram_tensor(f"in_{name}_dram", a.shape, _mybir.dt.from_np(a.dtype), kind="ExternalInput").ap())
    n, d = arrays["in_x_dram"].shape
    args.append(nc.dram_tensor("out_0_dram", (n, d), _mybir.dt.float32, kind="ExternalOutput").ap())
    graph_transformer_layer(nc, *args)
    r = _run(nc, [arrays], core_ids=[0])
    return r.results[0]["out_0_dram"]
```
